# Optimizing a Trainium2 kernel written in Bass

```python
import numpy as np
import jax
import jax.numpy as jnp

def _softmax(x, axis=-1):
    return jax.nn.softmax(x, axis=axis)

def _gelu(x):
    return jax.nn.gelu(x, approximate=True)

def _silu(x):
    return jax.nn.silu(x)

def _sigmoid(x):
    return jax.nn.sigmoid(x)

def _layernorm(x, axis=-1, eps=1e-05):
    m = jnp.mean(x, axis=axis, keepdims=True)
    v = jnp.var(x, axis=axis, keepdims=True)
    return (x - m) / jnp.sqrt(v + eps)

def _scatter_add(tgt, idx, src, axis=0):
    return tgt.at[idx].add(src)

def _segment_sum(src, seg, n):
    return jax.ops.segment_sum(src, seg, n)
kernel_name = 'mk_prb_d4_jaxref_r8_9ea1ce'

def setup_inputs(seed: int=0):
    np.random.seed(seed)
    _w = jnp.asarray

    def _L0_attn_setup():
        import jax, jax.numpy as jnp
        import numpy as np
        DIM = 128
        HEADS = 16
        DIM_HEAD = 64
        INNER = HEADS * DIM_HEAD
        EPS = 1e-10

        def safe_softmax(s):
            m = jnp.max(s, axis=-1, keepdims=True)
            e = jnp.exp(s - m)
            return e / (jnp.sum(e, axis=-1, keepdims=True) + EPS)
        key = jax.random.key(seed)
        ks = jax.random.split(key, 6)
        B, N = (4, 256)
        x = jax.random.normal(ks[0], (B, N, DIM), dtype=jnp.float32)
        s_in = 1.0 / np.sqrt(DIM)
        s_inner = 1.0 / np.sqrt(INNER)
        Wq = jax.random.uniform(ks[1], (INNER, DIM), jnp.float32, -s_in, s_in)
        Wk = jax.random.uniform(ks[2], (INNER, DIM), jnp.float32, -s_in, s_in)
        Wv = jax.random.uniform(ks[3], (INNER, DIM), jnp.float32, -s_in, s_in)
        Wo = jax.random.uniform(ks[4], (DIM, INNER), jnp.float32, -s_inner, s_inner)
        bo = jax.random.uniform(ks[5], (DIM,), jnp.float32, -s_inner, s_inner)
        return {'x': x, 'Wq': Wq, 'Wk': Wk, 'Wv': Wv, 'Wo': Wo, 'bo': bo}
    _L0_attn_in = _L0_attn_setup()

    def _L0_ffn_setup():
        import jax, jax.numpy as jnp
        import numpy as np
        B, S, H, D, E = (4, 128, 128, 512, 8)
        key = jax.random.key(seed)
        ks = jax.random.split(key, 12)

        def init(k, shape, fan_in):
            return jax.random.normal(k, shape, jnp.float32) / np.float32(np.sqrt(fan_in))
        return {'x': jax.random.normal(ks[0], (B, S, H), jnp.float32), 'Wq': init(ks[1], (H, H), H), 'bq': jnp.zeros((H,), jnp.float32), 'Wk': init(ks[2], (H, H), H), 'bk': jnp.zeros((H,), jnp.float32), 'Wv': init(ks[3], (H, H), H), 'bv': jnp.zeros((H,), jnp.float32), 'Wo': init(ks[4], (H, H), H), 'bo': jnp.zeros((H,), jnp.float32), 'Wg': init(ks[5], (H, E), H), 'bg': jnp.zeros((E,), jnp.float32), 'W1': init(ks[6], (E, H, D), H), 'b1': jnp.zeros((E, D), jnp.float32), 'W2': init(ks[7], (E, D, H), D), 'b2': jnp.zeros((E, H), jnp.float32)}
    _L0_ffn_in = _L0_ffn_setup()

    def _L1_attn_setup():
        import jax, jax.numpy as jnp
        import numpy as np
        import math
        N_HEADS = 16

        def _rope_tables(seq_len, head_dim):
            pos = jnp.arange(seq_len, dtype=jnp.float32)
            freqs = jnp.exp(jnp.arange(0, head_dim, 2, dtype=jnp.float32) * (-math.log(10000.0) / head_dim))
            angles = pos[:, None] * freqs[None, :]
            cos_emb = jnp.zeros((seq_len, head_dim), jnp.float32).at[:, 0::2].set(jnp.cos(angles))
            sin_emb = jnp.zeros((seq_len, head_dim), jnp.float32).at[:, 1::2].set(jnp.sin(angles))
            return (cos_emb, sin_emb)
        key = jax.random.key(seed)
        ks = jax.random.split(key, 5)
        B, S, D = (2, 256, 128)
        scale = 1.0 / math.sqrt(D)
        return {'x': jax.random.normal(ks[0], (B, S, D), jnp.float32), 'Wq': jax.random.normal(ks[1], (D, D), jnp.float32) * scale, 'Wk': jax.random.normal(ks[2], (D, D), jnp.float32) * scale, 'Wv': jax.random.normal(ks[3], (D, D), jnp.float32) * scale, 'Wo': jax.random.normal(ks[4], (D, D), jnp.float32) * scale}
    _L1_attn_in = _L1_attn_setup()

    def _L1_ffn_setup():
        import jax, jax.numpy as jnp
        import numpy as np
        B, S, H = (2, 256, 128)
        F = 512
        E = 8
        TOP_K = 2
        SHARED_SCALE = 0.1
        EPS = 1e-09

        def _moe_forward(x3, Wg, W1, b1, W2, b2, Ws1, bs1, Ws2, bs2):
            b, s, h = x3.shape
            x = x3.reshape(-1, h)
            T = x.shape[0]
            logits = x @ Wg
            probs = jax.nn.softmax(logits, axis=-1)
            vals, idx = jax.lax.top_k(probs, TOP_K)
            weights = vals / (jnp.sum(vals, axis=-1, keepdims=True) + EPS)
            cw = jnp.zeros((T, E), dtype=x.dtype).at[jnp.arange(T)[:, None], idx].set(weights)
            hpre = jnp.einsum('th,ehf->tef', x, W1) + b1
            act = jax.nn.silu(hpre)
            y = jnp.einsum('tef,efh->teh', act, W2) + b2
            out = jnp.einsum('te,teh->th', cw, y)
            shared = jax.nn.silu(x @ Ws1 + bs1) @ Ws2 + bs2
            out = out + SHARED_SCALE * shared
            return out.reshape(b, s, h)
        key = jax.random.key(seed)
        ks = jax.random.split(key, 10)
        sc = 0.02
        return {'hidden_states': jax.random.normal(ks[0], (B, S, H), dtype=jnp.float32), 'Wg': jax.random.normal(ks[1], (H, E), dtype=jnp.float32) * sc, 'W1': jax.random.normal(ks[2], (E, H, F), dtype=jnp.float32) * sc, 'b1': jnp.zeros((E, F), dtype=jnp.float32), 'W2': jax.random.normal(ks[3], (E, F, H), dtype=jnp.float32) * sc, 'b2': jnp.zeros((E, H), dtype=jnp.float32), 'Ws1': jax.random.normal(ks[4], (H, F), dtype=jnp.float32) * sc, 'bs1': jnp.zeros((F,), dtype=jnp.float32), 'Ws2': jax.random.normal(ks[5], (F, H), dtype=jnp.float32) * sc, 'bs2': jnp.zeros((H,), dtype=jnp.float32)}
    _L1_ffn_in = _L1_ffn_setup()

    def _L2_attn_setup():
        import jax, jax.numpy as jnp
        import numpy as np
        DIM = 128
        HEADS = 16
        DIM_HEAD = 64
        INNER = HEADS * DIM_HEAD
        EPS = 1e-06

        def elu_feature_map(t):
            return jnp.where(t > 0, t + 1.0, jnp.exp(t))
        key = jax.random.key(seed)
        k1, k2, k3, k4 = jax.random.split(key, 4)
        B, N = (4, 1024)
        x = jax.random.normal(k1, (B, N, DIM), dtype=jnp.float32)
        s_in = 1.0 / np.sqrt(DIM)
        s_out = 1.0 / np.sqrt(INNER)
        Wqkv = jax.random.uniform(k2, (DIM, 3 * INNER), dtype=jnp.float32, minval=-s_in, maxval=s_in)
        Wout = jax.random.uniform(k3, (INNER, DIM), dtype=jnp.float32, minval=-s_out, maxval=s_out)
        bout = jax.random.uniform(k4, (DIM,), dtype=jnp.float32, minval=-s_out, maxval=s_out)
        return {'x': x, 'Wqkv': Wqkv, 'Wout': Wout, 'bout': bout}
    _L2_attn_in = _L2_attn_setup()

    def _L2_ffn_setup():
        import jax, jax.numpy as jnp
        import numpy as np
        E = 8
        K = 2
        D = 128
        H = 512
        CAP_FACTOR = 1.0
        key = jax.random.key(seed)
        ks = jax.random.split(key, 5)
        x = jax.random.normal(ks[0], (4, 256, D), jnp.float32)
        gate_w = jax.random.normal(ks[1], (E, D), jnp.float32) * 0.02
        fc1_w = jax.random.normal(ks[2], (E, H, D), jnp.float32) * 0.02
        fc1_b = jnp.zeros((E, 1, H), jnp.float32)
        fc2_w = jax.random.normal(ks[3], (E, H, D), jnp.float32) * 0.02
        fc2_b = jnp.zeros((E, 1, D), jnp.float32)
        return {'x': x, 'gate_w': gate_w, 'fc1_w': fc1_w, 'fc1_b': fc1_b, 'fc2_w': fc2_w, 'fc2_b': fc2_b}
    _L2_ffn_in = _L2_ffn_setup()

    def _L3_attn_setup():
        import jax, jax.numpy as jnp
        import numpy as np
        D_MODEL = 128
        N_HEADS = 16
        KEY_DIM = D_MODEL // 2
        VAL_DIM = D_MODEL
        HEAD_QK = KEY_DIM // N_HEADS
        HEAD_V = VAL_DIM // N_HEADS
        PROJ_LR = 32
        GATE_LR = 64
        EPS = 1e-05
        key = jax.random.key(seed)
        ks = jax.random.split(key, 16)
        s = 0.02
        B, T = (4, 128)
        return {'x': jax.random.normal(ks[0], (B, T, D_MODEL), jnp.float32), 'mu_x': jax.random.normal(ks[1], (D_MODEL,), jnp.float32) * s, 'W_x1': jax.random.normal(ks[2], (D_MODEL, 5 * PROJ_LR), jnp.float32) * s, 'W_x2': jax.random.normal(ks[3], (D_MODEL, 5, PROJ_LR), jnp.float32) * s, 'x_bias': jax.random.normal(ks[4], (5, D_MODEL), jnp.float32) * s, 'W_r': jax.random.normal(ks[5], (D_MODEL, KEY_DIM), jnp.float32) * s, 'W_w1': jax.random.normal(ks[6], (D_MODEL, GATE_LR), jnp.float32) * s, 'W_w2': jax.random.normal(ks[7], (GATE_LR, KEY_DIM), jnp.float32) * s, 'b_w2': jax.random.normal(ks[8], (KEY_DIM,), jnp.float32) * s, 'W_k': jax.random.normal(ks[9], (D_MODEL, KEY_DIM), jnp.float32) * s, 'W_v': jax.random.normal(ks[10], (D_MODEL, VAL_DIM), jnp.float32) * s, 'W_g': jax.random.normal(ks[11], (D_MODEL, VAL_DIM), jnp.float32) * s, 'u': jax.random.normal(ks[12], (N_HEADS, HEAD_QK), jnp.float32) * s, 'gn_w': jnp.ones((VAL_DIM,), jnp.float32), 'gn_b': jnp.zeros((VAL_DIM,), jnp.float32), 'W_o': jax.random.normal(ks[13], (VAL_DIM, D_MODEL), jnp.float32) * s}
    _L3_attn_in = _L3_attn_setup()

    def _L3_ffn_setup():
        import jax, jax.numpy as jnp
        import numpy as np
        B, S, H, I, E, K = (2, 64, 128, 64, 64, 8)
        key = jax.random.key(seed)
        ks = jax.random.split(key, 8)
        return {'hidden_states': jax.random.normal(ks[0], (B, S, H), dtype=jnp.float32), 'router_w': jax.random.normal(ks[1], (H, E), dtype=jnp.float32) * 0.02, 'shared_gate_w': jax.random.normal(ks[2], (H, I), dtype=jnp.float32) * 0.02, 'shared_up_w': jax.random.normal(ks[3], (H, I), dtype=jnp.float32) * 0.02, 'shared_down_w': jax.random.normal(ks[4], (I, H), dtype=jnp.float32) * 0.02, 'expert_gate_k': jax.random.normal(ks[5], (E, H, I), dtype=jnp.float32) * 0.02, 'expert_up_k': jax.random.normal(ks[6], (E, H, I), dtype=jnp.float32) * 0.02, 'expert_down_k': jax.random.normal(ks[7], (E, I, H), dtype=jnp.float32) * 0.02}
    _L3_ffn_in = _L3_ffn_setup()
    _d = {'L0_attn_x': _L0_attn_in['x'], 'L0_attn_Wq': _L0_attn_in['Wq'], 'L0_attn_Wk': _L0_attn_in['Wk'], 'L0_attn_Wv': _L0_attn_in['Wv'], 'L0_attn_Wo': _L0_attn_in['Wo'], 'L0_attn_bo': _L0_attn_in['bo'], 'L0_ffn_Wq': _L0_ffn_in['Wq'], 'L0_ffn_bq': _L0_ffn_in['bq'], 'L0_ffn_Wk': _L0_ffn_in['Wk'], 'L0_ffn_bk': _L0_ffn_in['bk'], 'L0_ffn_Wv': _L0_ffn_in['Wv'], 'L0_ffn_bv': _L0_ffn_in['bv'], 'L0_ffn_Wo': _L0_ffn_in['Wo'], 'L0_ffn_bo': _L0_ffn_in['bo'], 'L0_ffn_Wg': _L0_ffn_in['Wg'], 'L0_ffn_bg': _L0_ffn_in['bg'], 'L0_ffn_W1': _L0_ffn_in['W1'], 'L0_ffn_b1': _L0_ffn_in['b1'], 'L0_ffn_W2': _L0_ffn_in['W2'], 'L0_ffn_b2': _L0_ffn_in['b2'], 'L1_attn_Wq': _L1_attn_in['Wq'], 'L1_attn_Wk': _L1_attn_in['Wk'], 'L1_attn_Wv': _L1_attn_in['Wv'], 'L1_attn_Wo': _L1_attn_in['Wo'], 'L1_ffn_Wg': _L1_ffn_in['Wg'], 'L1_ffn_W1': _L1_ffn_in['W1'], 'L1_ffn_b1': _L1_ffn_in['b1'], 'L1_ffn_W2': _L1_ffn_in['W2'], 'L1_ffn_b2': _L1_ffn_in['b2'], 'L1_ffn_Ws1': _L1_ffn_in['Ws1'], 'L1_ffn_bs1': _L1_ffn_in['bs1'], 'L1_ffn_Ws2': _L1_ffn_in['Ws2'], 'L1_ffn_bs2': _L1_ffn_in['bs2'], 'L2_attn_Wqkv': _L2_attn_in['Wqkv'], 'L2_attn_Wout': _L2_attn_in['Wout'], 'L2_attn_bout': _L2_attn_in['bout'], 'L2_ffn_gate_w': _L2_ffn_in['gate_w'], 'L2_ffn_fc1_w': _L2_ffn_in['fc1_w'], 'L2_ffn_fc1_b': _L2_ffn_in['fc1_b'], 'L2_ffn_fc2_w': _L2_ffn_in['fc2_w'], 'L2_ffn_fc2_b': _L2_ffn_in['fc2_b'], 'L3_attn_mu_x': _L3_attn_in['mu_x'], 'L3_attn_W_x1': _L3_attn_in['W_x1'], 'L3_attn_W_x2': _L3_attn_in['W_x2'], 'L3_attn_x_bias': _L3_attn_in['x_bias'], 'L3_attn_W_r': _L3_attn_in['W_r'], 'L3_attn_W_w1': _L3_attn_in['W_w1'], 'L3_attn_W_w2': _L3_attn_in['W_w2'], 'L3_attn_b_w2': _L3_attn_in['b_w2'], 'L3_attn_W_k': _L3_attn_in['W_k'], 'L3_attn_W_v': _L3_attn_in['W_v'], 'L3_attn_W_g': _L3_attn_in['W_g'], 'L3_attn_u': _L3_attn_in['u'], 'L3_attn_gn_w': _L3_attn_in['gn_w'], 'L3_attn_gn_b': _L3_attn_in['gn_b'], 'L3_attn_W_o': _L3_attn_in['W_o'], 'L3_ffn_router_w': _L3_ffn_in['router_w'], 'L3_ffn_shared_gate_w': _L3_ffn_in['shared_gate_w'], 'L3_ffn_shared_up_w': _L3_ffn_in['shared_up_w'], 'L3_ffn_shared_down_w': _L3_ffn_in['shared_down_w'], 'L3_ffn_expert_gate_k': _L3_ffn_in['expert_gate_k'], 'L3_ffn_expert_up_k': _L3_ffn_in['expert_up_k'], 'L3_ffn_expert_down_k': _L3_ffn_in['expert_down_k']}
    _x0 = _d['L0_attn_x']
    _d['L0_attn_x'] = jax.random.normal(jax.random.fold_in(jax.random.key(seed), 1), (4, 1024, 128), dtype=_x0.dtype)
    del _x0
    return _d

def reference(L0_attn_x, L0_attn_Wq, L0_attn_Wk, L0_attn_Wv, L0_attn_Wo, L0_attn_bo, L0_ffn_Wq, L0_ffn_bq, L0_ffn_Wk, L0_ffn_bk, L0_ffn_Wv, L0_ffn_bv, L0_ffn_Wo, L0_ffn_bo, L0_ffn_Wg, L0_ffn_bg, L0_ffn_W1, L0_ffn_b1, L0_ffn_W2, L0_ffn_b2, L1_attn_Wq, L1_attn_Wk, L1_attn_Wv, L1_attn_Wo, L1_ffn_Wg, L1_ffn_W1, L1_ffn_b1, L1_ffn_W2, L1_ffn_b2, L1_ffn_Ws1, L1_ffn_bs1, L1_ffn_Ws2, L1_ffn_bs2, L2_attn_Wqkv, L2_attn_Wout, L2_attn_bout, L2_ffn_gate_w, L2_ffn_fc1_w, L2_ffn_fc1_b, L2_ffn_fc2_w, L2_ffn_fc2_b, L3_attn_mu_x, L3_attn_W_x1, L3_attn_W_x2, L3_attn_x_bias, L3_attn_W_r, L3_attn_W_w1, L3_attn_W_w2, L3_attn_b_w2, L3_attn_W_k, L3_attn_W_v, L3_attn_W_g, L3_attn_u, L3_attn_gn_w, L3_attn_gn_b, L3_attn_W_o, L3_ffn_router_w, L3_ffn_shared_gate_w, L3_ffn_shared_up_w, L3_ffn_shared_down_w, L3_ffn_expert_gate_k, L3_ffn_expert_up_k, L3_ffn_expert_down_k):

    def _L0_attn_ref(x, Wq, Wk, Wv, Wo, bo):
        import jax, jax.numpy as jnp
        import numpy as np
        DIM = 128
        HEADS = 16
        DIM_HEAD = 64
        INNER = HEADS * DIM_HEAD
        EPS = 1e-10

        def safe_softmax(s):
            m = jnp.max(s, axis=-1, keepdims=True)
            e = jnp.exp(s - m)
            return e / (jnp.sum(e, axis=-1, keepdims=True) + EPS)
        B, N, _ = x.shape
        scale = DIM_HEAD ** (-0.5)

        def split_heads(t):
            return t.reshape(B, N, HEADS, DIM_HEAD).transpose(0, 2, 1, 3)
        q = split_heads(x @ Wq.T)
        k = split_heads(x @ Wk.T)
        v = split_heads(x @ Wv.T)
        sim = jnp.einsum('bhid,bhjd->bhij', q, k) * scale
        attn = safe_softmax(sim)
        out = jnp.einsum('bhij,bhjd->bhid', attn, v)
        out = out.transpose(0, 2, 1, 3).reshape(B, N, INNER)
        return out @ Wo.T + bo

    def _L0_ffn_ref(x, Wq, bq, Wk, bk, Wv, bv, Wo, bo, Wg, bg, W1, b1, W2, b2):
        import jax, jax.numpy as jnp
        import numpy as np
        B, S, H, D, E = (4, 128, 128, 512, 8)
        q = x @ Wq + bq
        k = x @ Wk + bk
        v = x @ Wv + bv
        scale = jnp.asarray(1.0 / np.sqrt(H), x.dtype)
        scores = jnp.einsum('bqh,bkh->bqk', q, k) * scale
        attn = jax.nn.softmax(scores, axis=-1)
        a = jnp.einsum('bqk,bkh->bqh', attn, v) @ Wo + bo
        x = x + a
        gates = jax.nn.softmax(x @ Wg + bg, axis=-1)
        hmid = jax.nn.relu(jnp.einsum('bsh,ehd->bsed', x, W1) + b1)
        eout = jnp.einsum('bsed,edh->bseh', hmid, W2) + b2
        y = jnp.einsum('bse,bseh->bsh', gates, eout)
        return x + y

    def _L1_attn_ref(x, Wq, Wk, Wv, Wo):
        import jax, jax.numpy as jnp
        import numpy as np
        import math
        N_HEADS = 16

        def _rope_tables(seq_len, head_dim):
            pos = jnp.arange(seq_len, dtype=jnp.float32)
            freqs = jnp.exp(jnp.arange(0, head_dim, 2, dtype=jnp.float32) * (-math.log(10000.0) / head_dim))
            angles = pos[:, None] * freqs[None, :]
            cos_emb = jnp.zeros((seq_len, head_dim), jnp.float32).at[:, 0::2].set(jnp.cos(angles))
            sin_emb = jnp.zeros((seq_len, head_dim), jnp.float32).at[:, 1::2].set(jnp.sin(angles))
            return (cos_emb, sin_emb)
        B, S, D = x.shape
        H = N_HEADS
        hd = D // H
        q = (x @ Wq.T).reshape(B, S, H, hd)
        k = (x @ Wk.T).reshape(B, S, H, hd)
        v = (x @ Wv.T).reshape(B, S, H, hd)
        cos_emb, sin_emb = _rope_tables(S, hd)
        cos = cos_emb[None, :, None, :]
        sin = sin_emb[None, :, None, :]
        q = q * cos - jnp.roll(q, 1, axis=-1) * sin
        k = k * cos - jnp.roll(k, 1, axis=-1) * sin
        q = q.transpose(0, 2, 1, 3)
        k = k.transpose(0, 2, 1, 3)
        v = v.transpose(0, 2, 1, 3)
        scores = jnp.einsum('bhqd,bhkd->bhqk', q, k) / math.sqrt(hd)
        attn = jax.nn.softmax(scores, axis=-1)
        ctx = jnp.einsum('bhqk,bhkd->bhqd', attn, v)
        ctx = ctx.transpose(0, 2, 1, 3).reshape(B, S, D)
        return ctx @ Wo.T

    def _L1_ffn_ref(hidden_states, Wg, W1, b1, W2, b2, Ws1, bs1, Ws2, bs2):
        import jax, jax.numpy as jnp
        import numpy as np
        B, S, H = (2, 256, 128)
        F = 512
        E = 8
        TOP_K = 2
        SHARED_SCALE = 0.1
        EPS = 1e-09

        def _moe_forward(x3, Wg, W1, b1, W2, b2, Ws1, bs1, Ws2, bs2):
            b, s, h = x3.shape
            x = x3.reshape(-1, h)
            T = x.shape[0]
            logits = x @ Wg
            probs = jax.nn.softmax(logits, axis=-1)
            vals, idx = jax.lax.top_k(probs, TOP_K)
            weights = vals / (jnp.sum(vals, axis=-1, keepdims=True) + EPS)
            cw = jnp.zeros((T, E), dtype=x.dtype).at[jnp.arange(T)[:, None], idx].set(weights)
            hpre = jnp.einsum('th,ehf->tef', x, W1) + b1
            act = jax.nn.silu(hpre)
            y = jnp.einsum('tef,efh->teh', act, W2) + b2
            out = jnp.einsum('te,teh->th', cw, y)
            shared = jax.nn.silu(x @ Ws1 + bs1) @ Ws2 + bs2
            out = out + SHARED_SCALE * shared
            return out.reshape(b, s, h)
        return _moe_forward(hidden_states, Wg, W1, b1, W2, b2, Ws1, bs1, Ws2, bs2)

    def _L2_attn_ref(x, Wqkv, Wout, bout):
        import jax, jax.numpy as jnp
        import numpy as np
        DIM = 128
        HEADS = 16
        DIM_HEAD = 64
        INNER = HEADS * DIM_HEAD
        EPS = 1e-06

        def elu_feature_map(t):
            return jnp.where(t > 0, t + 1.0, jnp.exp(t))
        B, N, D = x.shape
        qkv = x @ Wqkv
        q, k, v = jnp.split(qkv, 3, axis=-1)
        resh = lambda t: t.reshape(B, N, HEADS, DIM_HEAD).transpose(0, 2, 1, 3)
        q, k, v = (resh(q), resh(k), resh(v))
        q = elu_feature_map(q)
        k = elu_feature_map(k)
        kv = jnp.einsum('bhnd,bhnf->bhdf', k, v)
        k_sum = k.sum(axis=-2)
        qkv_out = jnp.einsum('bhnd,bhdf->bhnf', q, kv)
        q_k_sum = jnp.einsum('bhnd,bhd->bhn', q, k_sum)
        out = qkv_out / (q_k_sum[..., None] + EPS)
        out = out.transpose(0, 2, 1, 3).reshape(B, N, INNER)
        return out @ Wout + bout

    def _L2_ffn_ref(x, gate_w, fc1_w, fc1_b, fc2_w, fc2_b):
        import jax, jax.numpy as jnp
        import numpy as np
        E = 8
        K = 2
        D = 128
        H = 512
        CAP_FACTOR = 1.0
        B, S, Dm = x.shape
        xf = x.reshape(-1, Dm)
        N = xf.shape[0]
        cap = int(K * CAP_FACTOR * ((N + E - 1) // E))
        logits = xf @ gate_w.T
        scores = jax.nn.softmax(logits, axis=-1)
        topv, topi = jax.lax.top_k(scores, K)
        gates = topv / jnp.sum(topv, axis=-1, keepdims=True)
        offset = jnp.zeros((E,), jnp.int32)
        locs = []
        for j in range(K):
            mask = jax.nn.one_hot(topi[:, j], E, dtype=jnp.int32)
            loc_in = jnp.cumsum(mask, axis=0) - 1 + offset[None, :]
            locs.append(jnp.take_along_axis(loc_in, topi[:, j:j + 1], axis=1)[:, 0])
            offset = offset + mask.sum(axis=0)
        loc = jnp.stack(locs, axis=1)
        valid = loc < cap
        flat_idx = jnp.where(valid, topi * cap + loc, 0)
        w = valid.astype(xf.dtype)
        disp = jnp.zeros((E * cap, Dm), xf.dtype)
        disp = disp.at[flat_idx.reshape(-1)].add((xf[:, None, :] * w[:, :, None]).reshape(-1, Dm))
        de = disp.reshape(E, cap, Dm)
        h = jax.nn.relu(jnp.einsum('ecd,ehd->ech', de, fc1_w) + fc1_b)
        eo = jnp.einsum('ech,ehd->ecd', h, fc2_w) + fc2_b
        gathered = eo.reshape(E * cap, Dm)[flat_idx]
        out = jnp.sum(gathered * (gates * w)[:, :, None], axis=1)
        return out.reshape(B, S, Dm)

    def _L3_attn_ref(x, mu_x, W_x1, W_x2, x_bias, W_r, W_w1, W_w2, b_w2, W_k, W_v, W_g, u, gn_w, gn_b, W_o):
        import jax, jax.numpy as jnp
        import numpy as np
        D_MODEL = 128
        N_HEADS = 16
        KEY_DIM = D_MODEL // 2
        VAL_DIM = D_MODEL
        HEAD_QK = KEY_DIM // N_HEADS
        HEAD_V = VAL_DIM // N_HEADS
        PROJ_LR = 32
        GATE_LR = 64
        EPS = 1e-05
        B, T, D = x.shape
        shifted = jnp.pad(x, ((0, 0), (1, 0), (0, 0)))[:, :T]
        delta = shifted - x
        low = jnp.tanh((x + delta * mu_x) @ W_x1).reshape(B, T, 5, PROJ_LR)
        mus = jnp.einsum('blnr,dnr->blnd', low, W_x2) + x_bias
        xr, xw, xk, xv, xg = [x + delta * mus[:, :, i] for i in range(5)]
        r = (xr @ W_r).reshape(B, T, N_HEADS, HEAD_QK)
        w = (jnp.tanh(xw @ W_w1) @ W_w2 + b_w2).reshape(B, T, N_HEADS, HEAD_QK)
        k = (xk @ W_k).reshape(B, T, N_HEADS, HEAD_QK)
        v = (xv @ W_v).reshape(B, T, N_HEADS, HEAD_V)
        g = xg @ W_g
        w = -jnp.exp(w)

        def step(S, inp):
            r_t, k_t, v_t, w_t = inp
            o_t = jnp.einsum('bhk,bhkv->bhv', r_t, S) + jnp.einsum('bhk,hk,bhk,bhv->bhv', r_t, u, k_t, v_t)
            S = jnp.exp(w_t)[..., None] * S + k_t[..., :, None] * v_t[..., None, :]
            return (S, o_t)
        S0 = jnp.zeros((B, N_HEADS, HEAD_QK, HEAD_V), x.dtype)
        xs = tuple((jnp.moveaxis(t, 1, 0) for t in (r, k, v, w)))
        _, o = jax.lax.scan(step, S0, xs)
        o = jnp.moveaxis(o, 0, 1)
        mean = o.mean(-1, keepdims=True)
        var = o.var(-1, keepdims=True)
        o = ((o - mean) * jax.lax.rsqrt(var + EPS)).reshape(B, T, VAL_DIM)
        o = (o * gn_w + gn_b) * (g * jax.nn.sigmoid(g))
        return o @ W_o

    def _L3_ffn_ref(hidden_states, router_w, shared_gate_w, shared_up_w, shared_down_w, expert_gate_k, expert_up_k, expert_down_k):
        import jax, jax.numpy as jnp
        import numpy as np
        B, S, H, I, E, K = (2, 64, 128, 64, 64, 8)
        logits = jnp.einsum('bsh,he->bse', hidden_states.astype(jnp.float32), router_w)
        affinity = jax.nn.sigmoid(logits)
        top_scores, top_idx = jax.lax.top_k(affinity, K)
        top_w = top_scores / (jnp.sum(top_scores, axis=-1, keepdims=True) + 1e-09)
        one_hot = jax.nn.one_hot(top_idx, E, dtype=top_w.dtype)
        router_mask = jnp.einsum('bske,bsk->bse', one_hot, top_w).astype(hidden_states.dtype)
        shared = jnp.einsum('bsi,ih->bsh', jax.nn.silu(hidden_states @ shared_gate_w) * (hidden_states @ shared_up_w), shared_down_w)
        gate_out = jnp.einsum('bsh,ehi->bsei', hidden_states, expert_gate_k)
        up_out = jnp.einsum('bsh,ehi->bsei', hidden_states, expert_up_k)
        expert_act = jax.nn.silu(gate_out) * up_out
        routed = jnp.einsum('bsei,eih->bsh', expert_act * router_mask[..., None], expert_down_k)
        return shared + routed
    x = L0_attn_x
    xn = _layernorm(x, axis=-1)
    x = x + _L0_attn_ref(xn, L0_attn_Wq, L0_attn_Wk, L0_attn_Wv, L0_attn_Wo, L0_attn_bo) + _L0_ffn_ref(xn, L0_ffn_Wq, L0_ffn_bq, L0_ffn_Wk, L0_ffn_bk, L0_ffn_Wv, L0_ffn_bv, L0_ffn_Wo, L0_ffn_bo, L0_ffn_Wg, L0_ffn_bg, L0_ffn_W1, L0_ffn_b1, L0_ffn_W2, L0_ffn_b2)
    xn = _layernorm(x, axis=-1)
    x = x + _L1_attn_ref(xn, L1_attn_Wq, L1_attn_Wk, L1_attn_Wv, L1_attn_Wo) + _L1_ffn_ref(xn, L1_ffn_Wg, L1_ffn_W1, L1_ffn_b1, L1_ffn_W2, L1_ffn_b2, L1_ffn_Ws1, L1_ffn_bs1, L1_ffn_Ws2, L1_ffn_bs2)
    xn = _layernorm(x, axis=-1)
    x = x + _L2_attn_ref(xn, L2_attn_Wqkv, L2_attn_Wout, L2_attn_bout) + _L2_ffn_ref(xn, L2_ffn_gate_w, L2_ffn_fc1_w, L2_ffn_fc1_b, L2_ffn_fc2_w, L2_ffn_fc2_b)
    xn = _layernorm(x, axis=-1)
    x = x + _L3_attn_ref(xn, L3_attn_mu_x, L3_attn_W_x1, L3_attn_W_x2, L3_attn_x_bias, L3_attn_W_r, L3_attn_W_w1, L3_attn_W_w2, L3_attn_b_w2, L3_attn_W_k, L3_attn_W_v, L3_attn_W_g, L3_attn_u, L3_attn_gn_w, L3_attn_gn_b, L3_attn_W_o) + _L3_ffn_ref(xn, L3_ffn_router_w, L3_ffn_shared_gate_w, L3_ffn_shared_up_w, L3_ffn_shared_down_w, L3_ffn_expert_gate_k, L3_ffn_expert_up_k, L3_ffn_expert_down_k)
    return x

_drawn_inputs = setup_inputs


def setup_inputs(seed=0):
    import zlib

    import numpy as np

    out = dict(_drawn_inputs(seed))
    spreads = {'L0_ffn_bq': (0.0, 2.0),
     'L0_ffn_bk': (0.0, 2.0),
     'L0_ffn_bv': (0.0, 0.543),
     'L0_ffn_bo': (0.0, 0.53),
     'L0_ffn_bg': (0.0, 2.0),
     'L0_ffn_b1': (0.0, 1.777),
     'L0_ffn_b2': (0.0, 1.261),
     'L1_ffn_b1': (0.0, 0.8),
     'L1_ffn_b2': (0.0, 0.786),
     'L1_ffn_bs1': (0.0, 2.0),
     'L1_ffn_bs2': (0.0, 2.0),
     'L2_ffn_fc1_b': (0.0, 2.0),
     'L2_ffn_fc2_b': (0.0, 0.8),
     'L3_attn_gn_w': (1.0, 0.6),
     'L3_attn_gn_b': (0.0, 0.8)}
    factors = {'L0_attn_Wq': 8.0,
     'L0_attn_Wk': 8.0,
     'L0_attn_Wv': 6.286,
     'L0_attn_Wo': 6.333,
     'L0_attn_bo': 21.677,
     'L1_attn_Wq': 3.24,
     'L1_attn_Wk': 3.158,
     'L1_ffn_W1': 3.02,
     'L1_ffn_W2': 2.764,
     'L1_ffn_Ws1': 8.0,
     'L1_ffn_Ws2': 8.0,
     'L2_attn_bout': 29.524,
     'L2_ffn_fc1_w': 11.495,
     'L3_attn_mu_x': 8.0,
     'L3_attn_W_x1': 8.0,
     'L3_attn_W_x2': 8.0,
     'L3_attn_x_bias': 8.0,
     'L3_attn_W_r': 4.506,
     'L3_attn_W_w1': 8.0,
     'L3_attn_W_w2': 8.0,
     'L3_attn_b_w2': 52.709,
     'L3_attn_W_k': 4.505,
     'L3_attn_W_v': 4.512,
     'L3_attn_W_g': 4.477,
     'L3_attn_u': 29.096,
     'L3_attn_W_o': 4.475,
     'L3_ffn_router_w': 8.0,
     'L3_ffn_shared_gate_w': 8.0,
     'L3_ffn_shared_up_w': 8.0,
     'L3_ffn_shared_down_w': 8.0,
     'L3_ffn_expert_gate_k': 8.0,
     'L3_ffn_expert_up_k': 8.0,
     'L3_ffn_expert_down_k': 8.0,
     'L0_ffn_Wq': 4.063,
     'L0_ffn_Wk': 3.521,
     'L0_ffn_Wv': 3.303,
     'L0_ffn_Wo': 2.685,
     'L2_attn_Wqkv': 8.0,
     'L2_attn_Wout': 8.0,
     'L2_ffn_gate_w': 2.764}
    for name, (base, spread) in spreads.items():
        noise = np.random.default_rng([zlib.crc32(name.encode()), seed]).standard_normal(out[name].shape)
        drawn = base * np.exp(spread * noise) if base else spread * noise
        out[name] = jnp.asarray(drawn.astype(out[name].dtype))
    for name, factor in factors.items():
        out[name] = (out[name] * factor).astype(out[name].dtype)
    return out
```

```python
from contextlib import ExitStack

import numpy as np
import concourse.bass as bass
from concourse import mybir

F32 = mybir.dt.float32
F16 = mybir.dt.float16
BF16 = mybir.dt.bfloat16
ALU = mybir.AluOpType
ACT = mybir.ActivationFunctionType
AX = mybir.AxisListType

P = 128
B, N = 4, 1024
T = B * N
BANK = 512
CH = T // BANK
NT = T // P


class Place:

    def __init__(self, nc, ctx, stage):
        self.nc, self.ctx, self.stage, self.sems = nc, ctx, stage, []

    def sb(self, name, shape, dt=F32):
        return self.ctx.enter_context(self.nc.sbuf_tensor(f"{self.stage}_{name}", shape, dt))

    def ps(self, name, shape, dt=F32):
        return self.ctx.enter_context(self.nc.psum_tensor(f"{self.stage}_{name}", shape, dt))

    def sem(self, name):
        self.sems.append(self.ctx.enter_context(self.nc.semaphore(f"{self.stage}_{name}")))
        return self.sems[-1]

    def close(self):
        with self.nc.Block() as block:
            @block.sync
            def _(eng):
                for s in self.sems:
                    eng.sem_clear(s)


class Steps:

    def __init__(self, sem, names):
        self.sem, self.names, self.place = sem, names, {n: i + 1 for i, n in enumerate(names)}
        assert len(self.place) == len(names)

    def wait(self, eng, name, rnd):
        if isinstance(rnd, int) and rnd < 0:
            return
        eng.wait_ge(self.sem, rnd * len(self.names) + self.place[name])


def layer_norm(nc, stage, res_t, xn_t, avg_d, bias_d):
    with ExitStack() as ctx:
        pl = Place(nc, ctx, stage)
        avg = pl.sb("avg", [P, P])
        bias = pl.sb("bias", [P, 1])
        cen = pl.sb("cen", [P, 2, BANK])
        sq = pl.sb("sq", [P, 2, BANK])
        std = pl.sb("std", [P, 2, BANK])
        mean = pl.ps("mean", [P, 2, BANK])
        var = pl.ps("var", [P, 2, BANK])
        const_in = pl.sem("const_in")
        mean_full = pl.sem("mean_full")
        centred = pl.sem("centred")
        squared = pl.sem("squared")
        var_full = pl.sem("var_full")
        eps_added = pl.sem("eps_added")
        rooted = pl.sem("rooted")
        inverted = pl.sem("inverted")
        done = pl.sem("done")

        with nc.Block() as block:
            @block.sync
            def _(eng):
                eng.dma_start(avg[:, :], avg_d).then_inc(const_in, 16)
                if bias_d is not None:
                    eng.dma_start(bias[:, :], bias_d).then_inc(const_in, 16)
                eng.wait_ge(const_in, 32 if bias_d is not None else 16)

            @block.tensor
            def _(eng):
                eng.wait_ge(const_in, 32 if bias_d is not None else 16)
                for c in range(CH + 1):
                    if c < CH:
                        if c >= 2:
                            eng.wait_ge(centred, c - 1)
                        eng.matmul(mean[:, c % 2, :], avg[:, :], res_t[:, c * BANK:(c + 1) * BANK],
                                   start=True, stop=True).then_inc(mean_full, 1)
                    if c >= 1:
                        eng.wait_ge(squared, c)
                        if c >= 3:
                            eng.wait_ge(eps_added, c - 2)
                        eng.matmul(var[:, (c - 1) % 2, :], avg[:, :], sq[:, (c - 1) % 2, :],
                                   start=True, stop=True).then_inc(var_full, 1)

            @block.scalar
            def _(eng):
                for c in range(CH + 1):
                    if c < CH:
                        eng.wait_ge(centred, c + 1)
                        if c >= 2:
                            eng.wait_ge(var_full, c - 1)
                        eng.activation(sq[:, c % 2, :], cen[:, c % 2, :], ACT.Square).then_inc(squared, 1)
                    if c >= 1:
                        eng.wait_ge(eps_added, c)
                        eng.activation(std[:, (c - 1) % 2, :], std[:, (c - 1) % 2, :], ACT.Sqrt).then_inc(rooted, 1)

            @block.vector
            def _(eng):
                if bias_d is not None:
                    eng.wait_ge(const_in, 32)
                for c in range(CH + 2):
                    if c < CH:
                        eng.wait_ge(mean_full, c + 1)
                        if c >= 2:
                            eng.wait_ge(done, c - 1)
                        at = slice(c * BANK, (c + 1) * BANK)
                        eng.tensor_tensor(cen[:, c % 2, :], res_t[:, at], mean[:, c % 2, :], ALU.subtract).then_inc(centred, 1)
                    if 1 <= c <= CH:
                        k = c - 1
                        eng.wait_ge(var_full, k + 1)
                        if k >= 2:
                            eng.wait_ge(done, k - 1)
                        eng.tensor_scalar(std[:, k % 2, :], var[:, k % 2, :], 1e-5, None, ALU.add).then_inc(eps_added, 1)
                        eng.wait_ge(rooted, k + 1)
                        eng.reciprocal(std[:, k % 2, :], std[:, k % 2, :]).then_inc(inverted, 1)
                        at = slice(k * BANK, (k + 1) * BANK)
                        if bias_d is not None:
                            eng.wait_ge(centred, k + 1)
                            eng.tensor_scalar(res_t[:, at], res_t[:, at], bias[:, 0:1], None, ALU.add)
                        eng.wait_ge(inverted, k + 1)
                        eng.tensor_tensor(xn_t[:, at], cen[:, k % 2, :], std[:, k % 2, :], ALU.mult).then_inc(done, 1)

        pl.close()


def head_attention(nc, stage, res_t, xn_t, w_qkv, w_out, ident_d, rows_d, rope_d,
                   groups, heads, scale, eps):
    rows = P // heads
    pairs = heads // 2
    units = B * groups
    kts = N // P
    events = N // BANK * kts
    LAG = 2
    RING = 4
    maxima = [(qt, kh, hp) for qt in range(kts) for kh in range(2) for hp in range(pairs)]
    PREP = 4 + len(maxima)
    PHASE = PREP + 2

    def schedule(first, last):
        jobs = []
        if not last:
            jobs += [(LAG, ("v",)), (LAG + 1, ("q",)), (LAG + 2, ("k",))]
            at = LAG + 3
            jobs += [(at + m * (events - 1 - at) // len(maxima), ("max", m)) for m in range(len(maxima))]
            jobs += [(events - 1, ("shift",))]
        if not first:
            jobs.append((LAG + 1, ("out", 1)))
        jobs.append((kts + LAG + 1, ("out", 0)))
        jobs.sort(key=lambda j: j[0])
        order, pos = [], 0
        for e in range(events + (LAG if last else 0)):
            if e < events:
                order.append(("scores", e, 0, 0))
            if e >= LAG:
                order.append(("values", e - LAG, 0, 0))
            elif not first:
                order.append(("values", events + e - LAG, 1, 0))
            for at, job in jobs:
                if at == e:
                    order.append((job[0], job[1] if len(job) > 1 else 0, 0, pos))
                    pos += 1
        if last:
            order.append(("out", 1, -1, pos))
        return order

    PREPARE = [("v", 0, 0, 0), ("q", 0, 0, 1), ("k", 0, 0, 2)] \
        + [("max", m, 0, 3 + m) for m in range(len(maxima))] + [("shift", 0, 0, PREP - 1)]

    def run(eng, body):
        body(-1, 1, 0, PREPARE)
        body(0, 0, PREP, schedule(True, False))
        with eng.Fori(0, (units - 2) // 2) as i:
            body(2 * i + 1, 1, (2 * i + 1) * PHASE + PREP - 1, schedule(False, False))
            body(2 * i + 2, 0, (2 * i + 2) * PHASE + PREP - 1, schedule(False, False))
        body(units - 1, 1, (units - 1) * PHASE + PREP - 1, schedule(False, True))

    with ExitStack() as ctx:
        pl = Place(nc, ctx, stage)
        xb = pl.sb("xb", [P, 2, N])
        wqkv = pl.sb("wqkv", [P, 2, 3, P])
        wo = pl.sb("wo", [P, 2, P])
        ident = pl.sb("ident", [P, P])
        rowmask = pl.sb("rowmask", [P, kts])
        rope = pl.sb("rope", [P, 2, N]) if rope_d is not None else None
        whole = [pl.sb(f"whole_{c}", [P, N]) for c in "qk"]
        high = [pl.sb(f"high_{c}", [P, 2, N], F16) for c in "qk"]
        low = [pl.sb(f"low_{c}", [P, 2, N], F16) for c in "qk"]
        v = pl.sb("v", [P, 2, kts, P])
        part_max = pl.sb("part_max", [P, kts, 2, heads])
        row_max = pl.sb("row_max", [P, P])
        shift = pl.sb("shift", [P, 2, kts, P], F16)
        ones16 = pl.sb("ones16", [P, P], F16)
        ones = pl.sb("ones", [P, P])
        prob = pl.sb("prob", [P, RING, heads, BANK])
        denom = pl.sb("denom", [P, BANK])
        mixed = pl.sb("mixed", [P, 2, BANK])
        proj = pl.sb("proj", [P, 2, BANK])
        score = pl.ps("score", [P, 2, 2, BANK])
        side = pl.ps("side", [P, 2, BANK])
        o_sum = pl.ps("o_sum", [P, BANK])
        p_sum = pl.ps("p_sum", [P, BANK])

        const_in = pl.sem("const_in")
        unit_in = [pl.sem(f"unit_in{q}") for q in range(2)]
        wo_in = [pl.sem(f"wo_in{q}") for q in range(2)]
        filled = pl.sem("filled")
        side_full = pl.sem("side_full")
        side_free = pl.sem("side_free")
        row_maxed = pl.sem("row_maxed")
        high_done = pl.sem("high_done")
        low_done = pl.sem("low_done")
        score_full = pl.sem("score_full")
        exp_done = pl.sem("exp_done")
        pv_done = pl.sem("pv_done")
        norm = pl.sem("norm")
        out_ready = pl.sem("out_ready")
        added = pl.sem("added")
        CONSTS = 16 * (3 if rope is not None else 2)

        with nc.Block() as block:
            @block.sync
            def _(eng):
                eng.dma_start(ident[:, :], ident_d).then_inc(const_in, 16)
                eng.dma_start(rowmask[:, :], rows_d).then_inc(const_in, 16)
                if rope is not None:
                    eng.dma_start(rope[:, :, :], rope_d).then_inc(const_in, 16)

                def load(q, b, g):
                    eng.dma_start(xb[:, q, :], xn_t[:, bass.ds(b * N, N)]).then_inc(unit_in[q], 16)
                    eng.dma_start(wqkv[:, q, :, :], w_qkv[g, :, :, :]).then_inc(unit_in[q], 16)

                def load_out(q, g):
                    eng.dma_start(wo[:, q, :], w_out[g, :, :]).then_inc(wo_in[q], 16)

                for q in range(2):
                    load(q, 0, q)
                    load_out(q, q)
                with eng.Fori(1, units // 2) as i:
                    for q in range(2):
                        n = 2 * i + q
                        g = 2 * (i % (groups // 2)) + q
                        eng.wait_ge(low_done, 2 * (n - 1))
                        load(q, i // (groups // 2), g)
                        eng.wait_ge(added, 2 * (n - 1))
                        load_out(q, g)

            @block.tensor
            def _(eng):
                eng.wait_ge(const_in, CONSTS)
                eng.wait_ge(filled, 3)

                def body(n, q, base, order):
                    m, r = n + 1, 1 - q
                    for what, k, back, pos in order:
                        if what == "scores":
                            if k == 0:
                                eng.wait_ge(low_done, 2 * n + 2)
                                eng.wait_ge(side_free, base)
                            qs, keys = slice(k // kts * BANK, (k // kts + 1) * BANK), slice(k % kts * P, (k % kts + 1) * P)
                            for hp in range(pairs):
                                step = (n * events + k) * pairs + hp
                                slot = (k * pairs + hp) % 2
                                if not (isinstance(n, int) and n == 0 and k * pairs + hp < 2):
                                    eng.wait_ge(exp_done, step - 1)
                                terms = [(high[1], high[0]), (high[1], low[0]), (low[1], high[0]), (None, None)]
                                for t, (kk, qq) in enumerate(terms):
                                    for j in range(2):
                                        h = 2 * hp + j
                                        part = slice(h * rows, (h + 1) * rows)
                                        lhs = kk[part, q, keys] if kk is not None else ones16[part, :]
                                        rhs = qq[part, q, qs] if kk is not None else \
                                            shift[part, q, k // kts * 4:k // kts * 4 + 4, :].rearrange("p a b -> p (a b)")
                                        mm = eng.matmul(score[:, slot, j, :], lhs, rhs, start=(t == 0), stop=(t == 3))
                                mm.then_inc(score_full, 1)
                        elif what == "values":
                            u, uq = (n - 1, 1 - q) if back else (n, q)
                            half = 2 * u + k // kts
                            eng.wait_ge(exp_done, (u * events + k + 1) * pairs)
                            if k % kts == 0 and not (isinstance(half, int) and half == 0):
                                eng.wait_ge(out_ready, half)
                            for h in range(heads):
                                part = slice(h * rows, (h + 1) * rows)
                                for dst, lhs in ((o_sum, v[:, uq, k % kts, part]), (p_sum, ones[:, 0:rows])):
                                    mm = eng.matmul(dst[part, :], lhs, prob[:, k % RING, h, :],
                                                    start=(k % kts == 0), stop=(k % kts == kts - 1))
                            mm.then_inc(pv_done, 1)
                        else:
                            if not (isinstance(base, int) and base + pos == 0):
                                eng.wait_ge(side_free, base + pos)
                            if what == "v":
                                eng.wait_ge(unit_in[r], 16 * (m + 2 - r))
                                for kt in range(kts):
                                    mm = eng.matmul(side[:, kt // 4, kt % 4 * P:(kt % 4 + 1) * P],
                                                    xb[:, r, kt * P:(kt + 1) * P], wqkv[:, r, 2, :],
                                                    start=True, stop=True)
                            elif what in "qk":
                                for c in range(2):
                                    mm = eng.matmul(side[:, c, :], wqkv[:, r, "qk".index(what), :],
                                                    xb[:, r, c * BANK:(c + 1) * BANK], start=True, stop=True)
                            elif what == "max":
                                qt, kh, hp = maxima[k]
                                if k == 0:
                                    eng.wait_ge(high_done, 2 * m + 2)
                                for j in range(2):
                                    part = slice((2 * hp + j) * rows, (2 * hp + j + 1) * rows)
                                    mm = eng.matmul(side[:, j, :], high[0][part, r, qt * P:(qt + 1) * P],
                                                    high[1][part, r, kh * BANK:(kh + 1) * BANK], start=True, stop=True)
                            elif what == "shift":
                                eng.wait_ge(row_maxed, m + 1)
                                mm = eng.transpose(side[:, 0, 0:P], row_max[:, :], ident[:, :])
                            elif what == "out":
                                u, uq = (n - 1, 1 - q) if k == 1 and back == 0 else (n, q)
                                eng.wait_ge(wo_in[uq], 8 * (u + 2 - uq))
                                eng.wait_ge(out_ready, 2 * u + k + 1)
                                mm = eng.matmul(side[:, 0, :], wo[:, uq, :], mixed[:, k, :], start=True, stop=True)
                            mm.then_inc(side_full, 1)

                run(eng, body)

            @block.scalar
            def _(eng):
                def body(n, q, base, order):
                    m, r = n + 1, 1 - q
                    for what, k, back, pos in order:
                        if what in ("q", "k"):
                            c = "qk".index(what)
                            eng.wait_ge(side_free, base + pos + 1)
                            if not (isinstance(n, int) and n <= 0) and c == 0:
                                eng.wait_ge(score_full, events * pairs * n)
                            eng.activation(high[c][:, r, :], whole[c][:, :], ACT.Copy).then_inc(high_done, 1)
                        if what != "scores":
                            continue
                        for hp in range(pairs):
                            step = (n * events + k) * pairs + hp
                            slot = (k * pairs + hp) % 2
                            eng.wait_ge(score_full, step + 1)
                            if hp == 0 and not (isinstance(n, int) and n == 0 and k < RING):
                                eng.wait_ge(pv_done, n * events + k - RING + 1)
                            eng.activation(prob[:, k % RING, 2 * hp:2 * hp + 2, :], score[:, slot, :, :],
                                           ACT.Exp).then_inc(exp_done, 1)

                run(eng, body)

            @block.vector
            def _(eng):
                eng.memset(ones[:, :], 1.0).then_inc(filled, 1)
                eng.memset(ones16[:, :], 1.0).then_inc(filled, 1)
                eng.memset(row_max[:, :], 0.0).then_inc(filled, 1)
                eng.wait_ge(filled, 3)
                eng.wait_ge(const_in, CONSTS)
                cols = row_max[:, :].rearrange("p (h r) -> p r h", h=heads)[:, 0:kts, :]

                def body(n, q, base, order):
                    m, r = n + 1, 1 - q
                    fresh = isinstance(n, int) and n <= 0
                    for what, k, back, pos in order:
                        if what == "scores":
                            continue
                        if what == "values":
                            if k % kts != kts - 1:
                                continue
                            half = 2 * (n - 1 if back else n) + k // kts
                            eng.wait_ge(pv_done, kts * half + kts)
                            if not (isinstance(half, int) and half == 0):
                                eng.wait_ge(out_ready, half)
                            eng.tensor_scalar(denom[:, :], p_sum[:, :], eps, None, ALU.add).then_inc(norm, 1)
                            eng.wait_ge(norm, 2 * half + 1)
                            eng.reciprocal(denom[:, :], denom[:, :]).then_inc(norm, 1)
                            eng.wait_ge(norm, 2 * half + 2)
                            eng.tensor_tensor(mixed[:, k // kts, :], o_sum[:, :], denom[:, :], ALU.mult).then_inc(out_ready, 1)
                            continue
                        if what == "shift":
                            eng.wait_ge(side_free, base + pos)
                            eng.tensor_tensor(cols, part_max[:, :, 0, :], part_max[:, :, 1, :], ALU.max).then_inc(row_maxed, 1)
                        eng.wait_ge(side_full, base + pos + 1)
                        if what == "v":
                            if not fresh:
                                eng.wait_ge(pv_done, events * n)
                            op = eng.tensor_copy(v[:, r, :, :].rearrange("p a b -> p (a b)"), side[:, :, :].rearrange("p a b -> p (a b)"))
                        elif what in "qk":
                            c = "qk".index(what)
                            if not (isinstance(m, int) and m == 0):
                                eng.wait_ge(low_done, 2 * m - 1 + c)
                            out, src = whole[c][:, :], side[:, :, :].rearrange("p a b -> p (a b)")
                            if rope is not None:
                                op = eng.tensor_tensor(out, src, rope[:, c, :], ALU.mult)
                            else:
                                op = eng.tensor_scalar(out, src, scale if c == 0 else 1.0, None, ALU.mult)
                        elif what == "max":
                            qt, kh, hp = maxima[k]
                            if k == 0 and not (isinstance(m, int) and m == 0):
                                eng.wait_ge(row_maxed, m)
                            op = eng.tensor_reduce(part_max[:, qt, kh, 2 * hp:2 * hp + 2], side[:, :, :], AX.X, ALU.max)
                        elif what == "shift":
                            if not fresh:
                                eng.wait_ge(score_full, events * pairs * n)
                            op = eng.scalar_tensor_tensor(
                                out=shift[:, r, :, :], in0=side[:, 0:1, 0:P].broadcast_to([P, kts, P]), scalar=-1.0,
                                in1=rowmask[:, :].unsqueeze(2).broadcast_to([P, kts, P]), op0=ALU.mult, op1=ALU.mult)
                        elif what == "out":
                            half = 2 * (n - 1 if k == 1 and back == 0 else n) + k
                            if not (isinstance(half, int) and half < 2):
                                eng.wait_ge(added, half - 1)
                            op = eng.tensor_copy(proj[:, k, :], side[:, 0, :])
                        op.then_inc(side_free, 1)

                run(eng, body)

            @block.gpsimd
            def _(eng):
                def body(n, q, base, order):
                    m, r = n + 1, 1 - q
                    for what, k, back, pos in order:
                        if what in ("q", "k"):
                            c = "qk".index(what)
                            eng.wait_ge(high_done, 2 * m + c + 1)
                            eng.tensor_tensor(low[c][:, r, :], whole[c][:, :], high[c][:, r, :], ALU.subtract).then_inc(low_done, 1)
                        elif what == "out":
                            u = n - 1 if k == 1 and back == 0 else n
                            half = 2 * u + k
                            b = u // groups
                            at = bass.ds(b * N + k * BANK, BANK)
                            eng.wait_ge(side_free, base + pos + 1)
                            if not (isinstance(half, int) and half == 0):
                                eng.wait_ge(added, half)
                            eng.tensor_tensor(res_t[:, at], res_t[:, at], proj[:, k, :], ALU.add).then_inc(added, 1)

                run(eng, body)

        pl.close()


def whole_attention(nc, stage, res_t, xn_t, xp_t, w_d, bias_d, ident_d):
    qts = N // P
    scale = float(P) ** -0.5
    ORDER = [(what, t) for s in range(qts + 1) for what, t in (("scores", s), ("mix", s - 1)) if 0 <= t < qts]

    with ExitStack() as ctx:
        pl = Place(nc, ctx, stage)
        w = pl.sb("w", [P, 4, P])
        bias = pl.sb("bias", [P, 4])
        ident = pl.sb("ident", [P, P])
        xb = pl.sb("xb", [P, N])
        q = pl.sb("q", [P, N])
        k = pl.sb("k", [P, N])
        v = pl.sb("v", [P, qts, P])
        prob = pl.sb("prob", [P, 2, N])
        top = pl.sb("top", [P, 2])
        total = pl.sb("total", [P, 2])
        prob_t = pl.sb("prob_t", [P, 2, N])
        mixed = pl.sb("mixed", [P, 2, BANK])
        score = pl.ps("score", [P, 2, N])
        turned = pl.ps("turned", [P, N])
        mix = pl.ps("mix", [P, BANK])
        proj = pl.ps("proj", [P, BANK])
        const_in = pl.sem("const_in")
        x_in = pl.sem("x_in")
        projected = pl.sem("projected")
        q_ready = pl.sem("q_ready")
        kv_ready = pl.sem("kv_ready")
        score_full = pl.sem("score_full")
        maxed = pl.sem("maxed")
        negated = pl.sem("negated")
        exp_done = pl.sem("exp_done")
        inverted = pl.sem("inverted")
        prob_ready = pl.sem("prob_ready")
        turned_full = pl.sem("turned_full")
        turned_read = pl.sem("turned_read")
        mixed_tile = pl.sem("mixed_tile")
        mixed_half = pl.sem("mixed_half")
        proj_full = pl.sem("proj_full")
        xp_done = pl.sem("xp_done")
        res_done = pl.sem("res_done")

        def run(eng, body):
            body(0, True)
            with eng.Fori(1, B) as b:
                body(b, False)

        with nc.Block() as block:
            @block.sync
            def _(eng):
                eng.dma_start(w[:, :, :], w_d).then_inc(const_in, 16)
                eng.dma_start(bias[:, :], bias_d).then_inc(const_in, 16)
                eng.dma_start(ident[:, :], ident_d).then_inc(const_in, 16)
                eng.dma_start(xb[:, :], xn_t[:, 0:N]).then_inc(x_in, 16)
                with eng.Fori(1, B) as b:
                    eng.wait_ge(projected, 3 * b)
                    eng.dma_start(xb[:, :], xn_t[:, bass.ds(b * N, N)]).then_inc(x_in, 16)

            @block.tensor
            def _(eng):
                eng.wait_ge(const_in, 48)

                def body(b, first):
                    eng.wait_ge(x_in, 16 * b + 16)
                    if not first:
                        eng.wait_ge(exp_done, qts * b)
                        eng.wait_ge(turned_read, qts * b)
                    for c, dst in ((0, score[:, 0, :]), (1, score[:, 1, :])):
                        for h in range(2):
                            mm = eng.matmul(dst[:, h * BANK:(h + 1) * BANK], w[:, c, :], xb[:, h * BANK:(h + 1) * BANK],
                                            start=True, stop=True)
                        mm.then_inc(projected, 1)
                    for t in range(qts):
                        mm = eng.matmul(turned[:, t * P:(t + 1) * P], xb[:, t * P:(t + 1) * P], w[:, 2, :],
                                        start=True, stop=True)
                    mm.then_inc(projected, 1)
                    eng.wait_ge(q_ready, b + 1)
                    eng.wait_ge(kv_ready, 2 * b + 2)
                    for what, t in ORDER:
                        n = qts * b + t
                        if what == "scores":
                            if not (first and t < 2):
                                eng.wait_ge(exp_done, n - 1)
                            for h in range(2):
                                mm = eng.matmul(score[:, t % 2, h * BANK:(h + 1) * BANK], q[:, t * P:(t + 1) * P],
                                                k[:, h * BANK:(h + 1) * BANK], start=True, stop=True)
                            mm.then_inc(score_full, 1)
                            continue
                        eng.wait_ge(prob_ready, n + 1)
                        if not (first and t == 0):
                            eng.wait_ge(turned_read, n)
                        for kt in range(qts):
                            mm = eng.transpose(turned[:, kt * P:(kt + 1) * P], prob[:, t % 2, kt * P:(kt + 1) * P], ident[:, :])
                        mm.then_inc(turned_full, 1)
                        eng.wait_ge(turned_read, n + 1)
                        if t % 4 == 0 and not (first and t == 0):
                            eng.wait_ge(mixed_half, 2 * b + t // 4)
                        for kt in range(qts):
                            mm = eng.matmul(mix[:, t % 4 * P:(t % 4 + 1) * P], v[:, kt, :], prob_t[:, t % 2, kt * P:(kt + 1) * P],
                                            start=(kt == 0), stop=(kt == qts - 1))
                        mm.then_inc(mixed_tile, 1)
                        if t % 4 == 3:
                            half = 2 * b + t // 4
                            eng.wait_ge(mixed_half, half + 1)
                            if not (first and t == 3):
                                eng.wait_ge(xp_done, half)
                            eng.matmul(proj[:, :], w[:, 3, :], mixed[:, t // 4, :], start=True, stop=True).then_inc(proj_full, 1)

                run(eng, body)

            @block.scalar
            def _(eng):
                eng.wait_ge(const_in, 48)

                def body(b, first):
                    eng.wait_ge(projected, 3 * b + 2)
                    eng.activation(k[:, :], score[:, 1, :], ACT.Identity, bias=bias[:, 1:2]).then_inc(kv_ready, 1)
                    eng.wait_ge(projected, 3 * b + 3)
                    eng.activation(v[:, :, :].rearrange("p a b -> p (a b)"), turned[:, :], ACT.Copy).then_inc(kv_ready, 1)
                    for what, t in ORDER:
                        n = qts * b + t
                        if what == "scores":
                            eng.wait_ge(negated, n + 1)
                            if not (first and t < 2):
                                eng.wait_ge(turned_full, n - 1)
                            eng.activation(prob[:, t % 2, :], score[:, t % 2, :], ACT.Exp, bias=top[:, t % 2:t % 2 + 1],
                                           accum_out=total[:, t % 2:t % 2 + 1]).then_inc(exp_done, 1)
                        else:
                            eng.wait_ge(turned_full, n + 1)
                            if not (first and t < 2):
                                eng.wait_ge(mixed_tile, n - 1)
                            eng.activation(prob_t[:, t % 2, :], turned[:, :], ACT.Copy).then_inc(turned_read, 1)

                run(eng, body)

            @block.vector
            def _(eng):
                eng.wait_ge(const_in, 48)

                def body(b, first):
                    eng.wait_ge(projected, 3 * b + 1)
                    eng.tensor_scalar(q[:, :], score[:, 0, :], bias[:, 0:1], scale, ALU.add, ALU.mult).then_inc(q_ready, 1)
                    for what, t in ORDER:
                        n = qts * b + t
                        if what == "scores":
                            eng.wait_ge(score_full, n + 1)
                            if not (first and t < 2):
                                eng.wait_ge(exp_done, n - 1)
                            eng.tensor_reduce(top[:, t % 2:t % 2 + 1], score[:, t % 2, :], AX.X, ALU.max).then_inc(maxed, 1)
                            eng.wait_ge(maxed, n + 1)
                            eng.tensor_scalar(top[:, t % 2:t % 2 + 1], top[:, t % 2:t % 2 + 1], -1.0, None, ALU.mult).then_inc(negated, 1)
                            continue
                        eng.wait_ge(exp_done, n + 1)
                        eng.reciprocal(total[:, t % 2:t % 2 + 1], total[:, t % 2:t % 2 + 1]).then_inc(inverted, 1)
                        eng.wait_ge(inverted, n + 1)
                        eng.tensor_scalar(prob[:, t % 2, :], prob[:, t % 2, :], total[:, t % 2:t % 2 + 1], None, ALU.mult).then_inc(prob_ready, 1)
                        if t % 4 == 3:
                            half = 2 * b + t // 4
                            at = bass.ds(b * N + t // 4 * BANK, BANK)
                            eng.wait_ge(mixed_tile, n + 1)
                            if not (first and t < 8):
                                eng.wait_ge(proj_full, half - 1)
                            eng.tensor_scalar(mixed[:, t // 4, :], mix[:, :], bias[:, 2:3], None, ALU.add).then_inc(mixed_half, 1)
                            eng.wait_ge(proj_full, half + 1)
                            eng.scalar_tensor_tensor(out=xp_t[:, at], in0=proj[:, :], scalar=bias[:, 3:4], in1=xn_t[:, at],
                                                     op0=ALU.add, op1=ALU.add).then_inc(xp_done, 1)
                            eng.wait_ge(xp_done, half + 1)
                            eng.tensor_tensor(res_t[:, at], res_t[:, at], xp_t[:, at], ALU.add).then_inc(res_done, 1)

                run(eng, body)

        pl.close()


def linear_attention(nc, stage, res_t, xn_t, w_d, w_out_d, mask_d, eps):
    pairs = 8
    units = B * pairs
    tiles = N // P
    W = P + 2

    PREPARE = [("kv", i) for i in range(4)] + [("q", 0), ("state", 0)]

    def schedule(last):
        order = []
        for h in range(2):
            order.append(("mix", h))
            if not last:
                order += [("kv", 2 * h), ("kv", 2 * h + 1)]
                if h:
                    order.append(("q", 0))
            order.append(("out", h))
        if not last:
            order.append(("state", 0))
        return order

    def run(eng, body):
        body(-1, 1, PREPARE)
        body(0, 0, schedule(False))
        with eng.Fori(0, (units - 2) // 2) as i:
            body(2 * i + 1, 1, schedule(False))
            body(2 * i + 2, 0, schedule(False))
        body(units - 1, 1, schedule(True))

    with ExitStack() as ctx:
        pl = Place(nc, ctx, stage)
        xb = pl.sb("xb", [P, 2, N])
        w = pl.sb("w", [P, 2, 3 * P])
        wo = pl.sb("wo", [P, 2, P])
        mask = pl.sb("mask", [P, P])
        expk = pl.sb("expk", [P, 2, 2, P])
        relk = pl.sb("relk", [P, 2, 2, P])
        expq = pl.sb("expq", [P, N])
        relq = pl.sb("relq", [P, N])
        q_t = pl.sb("q_t", [P, 2, N])
        k_s = pl.sb("k_s", [P, tiles, P])
        v_s = pl.sb("v_s", [P, tiles, W])
        kv_blk = pl.sb("kv_blk", [P, 2, P])
        sum_blk = pl.sb("sum_blk", [P, 2, P])
        denom = pl.sb("denom", [P, BANK])
        mixed = pl.sb("mixed", [P, 2, BANK])
        q_ps = pl.ps("q_ps", [P, N])
        kv_ps = pl.ps("kv_ps", [P, 2, 2, 2, P])
        state = pl.ps("state", [P, BANK])
        num = pl.ps("num", [P, BANK])
        den = pl.ps("den", [P, BANK])
        out = pl.ps("out", [P, BANK])
        const_in = pl.sem("const_in")
        unit_in = [pl.sem(f"unit_in{r}") for r in range(2)]
        filled = pl.sem("filled")
        kv_full = pl.sem("kv_full")
        kv_read = pl.sem("kv_read")
        k_ready = pl.sem("k_ready")
        q_full = pl.sem("q_full")
        q_read = pl.sem("q_read")
        q_ready = pl.sem("q_ready")
        state_full = pl.sem("state_full")
        state_ready = pl.sem("state_ready")
        mix_full = pl.sem("mix_full")
        norm = pl.sem("norm")
        mixed_ready = pl.sem("mixed_ready")
        out_full = pl.sem("out_full")
        added = pl.sem("added")

        with nc.Block() as block:
            @block.sync
            def _(eng):
                eng.dma_start(mask[:, :], mask_d).then_inc(const_in, 16)

                def load(r, b, g):
                    eng.dma_start(xb[:, r, :], xn_t[:, bass.ds(b * N, N)]).then_inc(unit_in[r], 16)
                    eng.dma_start(w[:, r, :], w_d[g, :, :]).then_inc(unit_in[r], 16)
                    eng.dma_start(wo[:, r, :], w_out_d[g, :, :]).then_inc(unit_in[r], 16)

                for r in range(2):
                    load(r, 0, r)
                with eng.Fori(1, units // 2) as i:
                    for r in range(2):
                        eng.wait_ge(out_full, 2 * (2 * i + r - 1))
                        load(r, i // (pairs // 2), 2 * (i % (pairs // 2)) + r)

            @block.tensor
            def _(eng):
                eng.wait_ge(const_in, 16)
                eng.wait_ge(filled, 1)

                def body(n, q, order):
                    m, r = n + 1, 1 - q
                    for what, i in order:
                        if what == "kv":
                            if i == 0:
                                eng.wait_ge(unit_in[r], 24 * (m + 2 - r))
                            if not (isinstance(m, int) and m == 0 and i < 2):
                                eng.wait_ge(kv_read, 4 * m + i - 1)
                            for t in range(2):
                                tile = 2 * i + t
                                mm = eng.matmul(kv_ps[:, i % 2, t, :, :].rearrange("p a b -> p (a b)"),
                                                xb[:, r, tile * P:(tile + 1) * P], w[:, r, P:3 * P], start=True, stop=True)
                            mm.then_inc(kv_full, 1)
                        elif what == "q":
                            if not (isinstance(m, int) and m == 0):
                                eng.wait_ge(q_read, m)
                            for h in range(2):
                                mm = eng.matmul(q_ps[:, h * BANK:(h + 1) * BANK], w[:, r, 0:P],
                                                xb[:, r, h * BANK:(h + 1) * BANK], start=True, stop=True)
                            mm.then_inc(q_full, 1)
                        elif what == "state":
                            eng.wait_ge(k_ready, 4 * m + 4)
                            if not (isinstance(m, int) and m == 0):
                                eng.wait_ge(state_ready, 2 * m)
                            for t in range(tiles):
                                mm = eng.matmul(state[:, 0:W], k_s[:, t, :], v_s[:, t, :], start=(t == 0), stop=(t == tiles - 1))
                            mm.then_inc(state_full, 1)
                        elif what == "mix":
                            half = 2 * n + i
                            eng.wait_ge(state_ready, 2 * n + 2)
                            eng.wait_ge(q_ready, n + 1)
                            if not (isinstance(half, int) and half == 0):
                                eng.wait_ge(mixed_ready, half)
                            eng.matmul(den[:, :], sum_blk[:, q, :], q_t[:, q, i * BANK:(i + 1) * BANK], start=True, stop=True)
                            eng.matmul(num[:, :], kv_blk[:, q, :], q_t[:, q, i * BANK:(i + 1) * BANK],
                                       start=True, stop=True).then_inc(mix_full, 1)
                        elif what == "out":
                            half = 2 * n + i
                            eng.wait_ge(mixed_ready, half + 1)
                            if not (isinstance(half, int) and half == 0):
                                eng.wait_ge(added, half)
                            eng.matmul(out[:, :], wo[:, q, :], mixed[:, i, :], start=True, stop=True).then_inc(out_full, 1)

                run(eng, body)

            @block.scalar
            def _(eng):
                def body(n, q, order):
                    m, r = n + 1, 1 - q
                    for what, i in order:
                        if what == "kv":
                            eng.wait_ge(kv_full, 4 * m + i + 1)
                            if not (isinstance(m, int) and m == 0 and i < 2):
                                eng.wait_ge(k_ready, 4 * m + i - 1)
                            if i == 0 and not (isinstance(m, int) and m == 0):
                                eng.wait_ge(state_full, m)
                            eng.activation(expk[:, i % 2, :, :], kv_ps[:, i % 2, :, 0, :], ACT.Exp)
                            eng.activation(relk[:, i % 2, :, :], kv_ps[:, i % 2, :, 0, :], ACT.Relu)
                            eng.activation(v_s[:, 2 * i:2 * i + 2, 0:P], kv_ps[:, i % 2, :, 1, :], ACT.Copy).then_inc(kv_read, 1)
                        elif what == "q":
                            eng.wait_ge(q_full, m + 1)
                            if not (isinstance(m, int) and m == 0):
                                eng.wait_ge(q_ready, m)
                            eng.activation(expq[:, :], q_ps[:, :], ACT.Exp)
                            eng.activation(relq[:, :], q_ps[:, :], ACT.Relu).then_inc(q_read, 1)

                run(eng, body)

            @block.vector
            def _(eng):
                eng.memset(v_s[:, :, P:W], 1.0).then_inc(filled, 1)
                eng.wait_ge(const_in, 16)

                def body(n, q, order):
                    m, r = n + 1, 1 - q
                    for what, i in order:
                        if what == "kv":
                            eng.wait_ge(kv_read, 4 * m + i + 1)
                            if i == 0 and not (isinstance(m, int) and m == 0):
                                eng.wait_ge(state_full, m)
                            eng.scalar_tensor_tensor(out=k_s[:, 2 * i:2 * i + 2, :], in0=expk[:, i % 2, :, :], scalar=1.0,
                                                     in1=relk[:, i % 2, :, :], op0=ALU.min, op1=ALU.add).then_inc(k_ready, 1)
                        elif what == "q":
                            eng.wait_ge(q_read, m + 1)
                            if not (isinstance(n, int) and n <= 0):
                                eng.wait_ge(mix_full, 2 * n)
                            eng.scalar_tensor_tensor(out=q_t[:, r, :], in0=expq[:, :], scalar=1.0, in1=relq[:, :],
                                                     op0=ALU.min, op1=ALU.add).then_inc(q_ready, 1)
                        elif what == "state":
                            eng.wait_ge(state_full, m + 1)
                            if not (isinstance(n, int) and n <= 0):
                                eng.wait_ge(mix_full, 2 * n)
                            eng.tensor_tensor(kv_blk[:, r, :], state[:, 0:P], mask[:, :], ALU.mult).then_inc(state_ready, 1)
                            eng.tensor_scalar(sum_blk[:, r, :], mask[:, :], state[:, P:P + 1], None, ALU.mult).then_inc(state_ready, 1)
                        elif what == "mix":
                            half = 2 * n + i
                            eng.wait_ge(mix_full, half + 1)
                            if not (isinstance(half, int) and half == 0):
                                eng.wait_ge(mixed_ready, half)
                            eng.tensor_scalar(denom[:, :], den[:, :], eps, None, ALU.add).then_inc(norm, 1)
                            eng.wait_ge(norm, 2 * half + 1)
                            eng.reciprocal(denom[:, :], denom[:, :]).then_inc(norm, 1)
                            eng.wait_ge(norm, 2 * half + 2)
                            if not (isinstance(half, int) and half < 2):
                                eng.wait_ge(out_full, half - 1)
                            eng.tensor_tensor(mixed[:, i, :], num[:, :], denom[:, :], ALU.mult).then_inc(mixed_ready, 1)
                        elif what == "out":
                            half = 2 * n + i
                            at = bass.ds((n // pairs) * N + i * BANK, BANK)
                            eng.wait_ge(out_full, half + 1)
                            if not (isinstance(half, int) and half == 0):
                                eng.wait_ge(added, half)
                            eng.tensor_tensor(res_t[:, at], res_t[:, at], out[:, :], ALU.add).then_inc(added, 1)

                run(eng, body)

        pl.close()


def recurrent_mixing(nc, stage, res_t, xn_t, d):
    GROUPS = 4
    HV = 8

    with ExitStack() as ctx:
        pl = Place(nc, ctx, stage)
        shape = {"cols": [P, 20], "w_x1": [P, 160], "w_x2": [P, P], "w_x2b": [32, P], "w_w1": [P, 64],
                 "w_w2": [64, GROUPS, P], "w_r": [P, GROUPS, P], "w_k": [P, GROUPS, P], "w_v": [P, GROUPS, P],
                 "w_g": [P, P], "w_o": [P, P], "pick": [P, 32], "blocks": [P, P]}
        c = {n: pl.sb(n, s) for n, s in shape.items()}
        MU, XB, DB, U, GW, GB = 0, 1, 6, 10, 14, 15
        cols = c["cols"]
        xs = pl.sb("xs", [P, N + 1])
        x = xs[:, 1:N + 1]
        delta = pl.sb("delta", [P, N])
        z = pl.sb("z", [P, N])
        low = pl.sb("low", [P, N])
        low5 = pl.sb("low5", [32, N])
        mixed = pl.sb("mixed", [P, 5, N])
        wt = pl.sb("wt", [64, N])
        gs = pl.sb("gs", [P, N])
        vs = pl.sb("vs", [P, 2, N])
        decay = pl.sb("decay", [P, 2, N])
        kv = pl.sb("kv", [P, N])
        st = pl.sb("st", [P, N + 1])
        rs = pl.sb("rs", [P, 2, N])
        cen = pl.sb("cen", [P, N])
        sq = pl.sb("sq", [P, N])
        std = pl.sb("std", [P, N])
        work = [pl.ps(f"work{i}", [P, N]) for i in range(3)]
        o_ps = pl.ps("o_ps", [P, N])

        JOBS = [("low", "act", "low"), ("low5", "act", "low5")] \
            + [(f"mu{i}", "dve", f"mu{i}") for i in range(5)] \
            + [("tanh_w", "act", "wt"), ("g", "act", "gs")]
        for j in range(GROUPS):
            JOBS += [(f"v{j}", "act", f"vs{j}"), (f"w{j}", "act", f"ew{j}"), (f"k{j}", "dve", f"kv{j}"), (f"r{j}", "dve", f"rs{j}")]
        JOBS += [("mean", "dve", "cen"), ("var", "dve", "eps"), ("out", "dve", "res")]
        slot = {name: work[i % 3] for i, (name, _, _) in enumerate(JOBS)}
        PE = [name for name, _, _ in JOBS]
        for j in range(GROUPS):
            PE.insert(PE.index(f"r{j}") + (1 if j == GROUPS - 1 else 3), f"o{j}")
        ACTS = ["low", "low5", "wt", "gs"] + [s + str(j) for j in range(GROUPS) for s in ("vs", "ew", "decay")] + ["o", "sq", "std"]
        DVES = ["delta", "z"] + [f"mu{i}" for i in range(5)] \
            + [s + str(j) for j in range(GROUPS) for s in ("kv", "scan", "u", "rs")] \
            + ["cen", "eps", "rstd", "norm", "affine", "gated", "res"]
        POOLS = [f"x{i}" for i in range(5)]
        const_in = pl.sem("const_in")
        filled = pl.sem("filled")
        x_in = pl.sem("x_in")
        pe = Steps(pl.sem("pe_done"), PE)
        act = Steps(pl.sem("act_done"), ACTS)
        dve = Steps(pl.sem("dve_done"), DVES)
        pool = Steps(pl.sem("pool_done"), POOLS)
        reader = {"act": act, "dve": dve}

        def run(eng, body):
            body(0)
            with eng.Fori(1, B) as b:
                body(b)

        def before(b):
            return -1 if isinstance(b, int) else b - 1

        with nc.Block() as block:
            @block.sync
            def _(eng):
                for n in shape:
                    eng.dma_start(c[n][tuple(slice(None) for _ in shape[n])], d[n]).then_inc(const_in, 16)
                eng.wait_ge(filled, 2)
                eng.dma_start(x, xn_t[:, 0:N]).then_inc(x_in, 16)
                with eng.Fori(1, B) as b:
                    pool.wait(eng, "x4", b - 1)
                    eng.dma_start(x, xn_t[:, bass.ds(b * N, N)]).then_inc(x_in, 16)

            @block.tensor
            def _(eng):
                eng.wait_ge(const_in, 16 * len(shape))

                def product(b, name, lhs, rhs, dst=None, rows=P):
                    if dst is None:
                        i = [n for n, _, _ in JOBS].index(name)
                        same = [k for k in range(len(JOBS)) if k % 3 == i % 3]
                        at = same.index(i)
                        _, who, step = JOBS[same[at - 1]]
                        reader[who].wait(eng, step, b if at else before(b))
                        dst = slot[name]
                    for h in range(2):
                        mm = eng.matmul(dst[0:rows, h * BANK:(h + 1) * BANK], lhs, rhs[:, h * BANK:(h + 1) * BANK],
                                        start=True, stop=True)
                    mm.then_inc(pe.sem, 1)

                def body(b):
                    for name in PE:
                        j = int(name[-1]) if name[-1].isdigit() and name not in ("low5",) else 0
                        if name == "low":
                            dve.wait(eng, "z", b)
                            product(b, name, c["w_x1"][:, 0:P], z)
                        elif name == "low5":
                            product(b, name, c["w_x1"][:, P:160], z, rows=32)
                        elif name.startswith("mu"):
                            act.wait(eng, "low5" if j == 4 else "low", b)
                            if j < 4:
                                product(b, name, c["w_x2"][32 * j:32 * j + 32, :], low[32 * j:32 * j + 32, :])
                            else:
                                product(b, name, c["w_x2b"][:, :], low5)
                        elif name == "tanh_w":
                            pool.wait(eng, "x1", b)
                            product(b, name, c["w_w1"][:, :], mixed[:, 1, :], rows=64)
                        elif name == "g":
                            pool.wait(eng, "x4", b)
                            product(b, name, c["w_g"][:, :], mixed[:, 4, :])
                        elif name[0] == "v" and name != "var":
                            product(b, name, c["w_v"][:, j, :], mixed[:, 3, :])
                        elif name[0] == "w":
                            act.wait(eng, "wt", b)
                            product(b, name, c["w_w2"][:, j, :], wt)
                        elif name[0] == "k":
                            product(b, name, c["w_k"][:, j, :], mixed[:, 2, :])
                        elif name[0] == "r":
                            product(b, name, c["w_r"][:, j, :], mixed[:, 0, :])
                        elif name[0] == "o" and name != "out":
                            dve.wait(eng, f"rs{j}", b)
                            act.wait(eng, "o", before(b))
                            for h in range(2):
                                mm = eng.matmul(o_ps[32 * j:32 * j + 32, h * BANK:(h + 1) * BANK], c["pick"][:, :],
                                                rs[:, j % 2, h * BANK:(h + 1) * BANK], start=True, stop=True)
                            mm.then_inc(pe.sem, 1)
                        elif name == "mean":
                            act.wait(eng, "o", b)
                            product(b, name, c["blocks"][:, :], z)
                        elif name == "var":
                            act.wait(eng, "sq", b)
                            product(b, name, c["blocks"][:, :], sq)
                        elif name == "out":
                            dve.wait(eng, "gated", b)
                            product(b, name, c["w_o"][:, :], cen)

                run(eng, body)

            @block.scalar
            def _(eng):
                eng.wait_ge(const_in, 16 * len(shape))

                def body(b):
                    prev = before(b)
                    pe.wait(eng, "low", b)
                    pe.wait(eng, "mu3", prev)
                    eng.activation(low[:, :], slot["low"][:, :], ACT.Tanh).then_inc(act.sem, 1)
                    pe.wait(eng, "low5", b)
                    eng.activation(low5[:, :], slot["low5"][0:32, :], ACT.Tanh).then_inc(act.sem, 1)
                    pe.wait(eng, "tanh_w", b)
                    pe.wait(eng, f"w{GROUPS - 1}", prev)
                    eng.activation(wt[:, :], slot["tanh_w"][0:64, :], ACT.Tanh).then_inc(act.sem, 1)
                    pe.wait(eng, "g", b)
                    dve.wait(eng, "gated", prev)
                    eng.activation(gs[:, :], slot["g"][:, :], ACT.Silu).then_inc(act.sem, 1)
                    for j in range(GROUPS):
                        pe.wait(eng, f"v{j}", b)
                        if j >= 2:
                            dve.wait(eng, f"scan{j - 2}", b)
                        eng.activation(vs[:, j % 2, :], slot[f"v{j}"][:, :], ACT.Copy).then_inc(act.sem, 1)
                        pe.wait(eng, f"w{j}", b)
                        eng.activation(decay[:, j % 2, :], slot[f"w{j}"][:, :], ACT.Exp,
                                       bias=cols[:, DB + j:DB + j + 1]).then_inc(act.sem, 1)
                        act.wait(eng, f"ew{j}", b)
                        eng.activation(decay[:, j % 2, :], decay[:, j % 2, :], ACT.Exp, scale=-1.0).then_inc(act.sem, 1)
                    pe.wait(eng, f"o{GROUPS - 1}", b)
                    eng.activation(z[:, :], o_ps[:, :], ACT.Copy).then_inc(act.sem, 1)
                    dve.wait(eng, "cen", b)
                    eng.activation(sq[:, :], cen[:, :], ACT.Square).then_inc(act.sem, 1)
                    dve.wait(eng, "eps", b)
                    eng.activation(std[:, :], std[:, :], ACT.Sqrt).then_inc(act.sem, 1)

                run(eng, body)

            @block.gpsimd
            def _(eng):
                def body(b):
                    for i in range(5):
                        dve.wait(eng, f"mu{i}", b)
                        eng.tensor_tensor(mixed[:, i, :], mixed[:, i, :], x, ALU.add).then_inc(pool.sem, 1)

                run(eng, body)

            @block.vector
            def _(eng):
                eng.memset(xs[:, 0:1], 0.0).then_inc(filled, 1)
                eng.memset(st[:, 0:1], 0.0).then_inc(filled, 1)
                eng.wait_ge(filled, 2)
                eng.wait_ge(const_in, 16 * len(shape))

                def body(b):
                    prev = before(b)
                    eng.wait_ge(x_in, 16 * b + 16)
                    dve.wait(eng, "res", prev)
                    eng.tensor_tensor(delta[:, :], xs[:, 0:N], x, ALU.subtract).then_inc(dve.sem, 1)
                    dve.wait(eng, "delta", b)
                    eng.scalar_tensor_tensor(out=z[:, :], in0=delta[:, :], scalar=cols[:, MU:MU + 1], in1=x,
                                             op0=ALU.mult, op1=ALU.add).then_inc(dve.sem, 1)
                    for i in range(5):
                        pe.wait(eng, f"mu{i}", b)
                        if i == 0:
                            pe.wait(eng, f"r{GROUPS - 1}", prev)
                        eng.scalar_tensor_tensor(out=mixed[:, i, :], in0=slot[f"mu{i}"][:, :], scalar=cols[:, XB + i:XB + i + 1],
                                                 in1=delta[:, :], op0=ALU.add, op1=ALU.mult).then_inc(dve.sem, 1)
                    for j in range(GROUPS):
                        act.wait(eng, f"vs{j}", b)
                        pe.wait(eng, f"k{j}", b)
                        if j:
                            dve.wait(eng, f"u{j - 1}", b)
                        eng.tensor_tensor(kv[:, :], slot[f"k{j}"][:, :], vs[:, j % 2, :], ALU.mult).then_inc(dve.sem, 1)
                        act.wait(eng, f"decay{j}", b)
                        dve.wait(eng, f"kv{j}", b)
                        eng.tensor_tensor_scan(st[:, 1:N + 1], decay[:, j % 2, :], kv[:, :], 0.0, ALU.mult, ALU.add).then_inc(dve.sem, 1)
                        dve.wait(eng, f"scan{j}", b)
                        if j >= 2:
                            pe.wait(eng, f"o{j - 2}", b)
                        eng.scalar_tensor_tensor(out=rs[:, j % 2, :], in0=kv[:, :], scalar=cols[:, U + j:U + j + 1],
                                                 in1=st[:, 0:N], op0=ALU.mult, op1=ALU.add).then_inc(dve.sem, 1)
                        dve.wait(eng, f"u{j}", b)
                        pe.wait(eng, f"r{j}", b)
                        eng.tensor_tensor(rs[:, j % 2, :], rs[:, j % 2, :], slot[f"r{j}"][:, :], ALU.mult).then_inc(dve.sem, 1)
                    pe.wait(eng, "mean", b)
                    eng.tensor_tensor(cen[:, :], z[:, :], slot["mean"][:, :], ALU.subtract).then_inc(dve.sem, 1)
                    pe.wait(eng, "var", b)
                    eng.tensor_scalar(std[:, :], slot["var"][:, :], 1e-5, None, ALU.add).then_inc(dve.sem, 1)
                    act.wait(eng, "std", b)
                    eng.reciprocal(std[:, :], std[:, :]).then_inc(dve.sem, 1)
                    dve.wait(eng, "rstd", b)
                    eng.tensor_tensor(cen[:, :], cen[:, :], std[:, :], ALU.mult).then_inc(dve.sem, 1)
                    dve.wait(eng, "norm", b)
                    eng.tensor_scalar(cen[:, :], cen[:, :], cols[:, GW:GW + 1], cols[:, GB:GB + 1], ALU.mult, ALU.add).then_inc(dve.sem, 1)
                    dve.wait(eng, "affine", b)
                    act.wait(eng, "gs", b)
                    eng.tensor_tensor(cen[:, :], cen[:, :], gs[:, :], ALU.mult).then_inc(dve.sem, 1)
                    pe.wait(eng, "out", b)
                    at = bass.ds(b * N, N)
                    eng.tensor_tensor(res_t[:, at], res_t[:, at], slot["out"][:, :], ALU.add).then_inc(dve.sem, 1)

                run(eng, body)

        pl.close()


def route(nc, stage, x_t, w_d, bias_d, tri_d, ident_d, gates_d, E, top, norm_eps, squash, extra, extra_value, capacity):
    EX = E + extra
    GB = BANK // E

    with ExitStack() as ctx:
        pl = Place(nc, ctx, stage)
        w = pl.sb("w", [P, E])
        bias = pl.sb("bias", [P, E])
        ident = pl.sb("ident", [P, P])
        score = pl.sb("score", [P, NT, E])
        gates = pl.sb("gates", [P, NT, EX])
        small = [pl.sb(f"small{i}", [P, NT]) for i in range(2)]
        tmp = [pl.sb(f"tmp{i}", [P, NT, E]) for i in range(3)] if top else None
        keep = pl.sb("keep", [P, NT, E]) if top else None
        best = pl.sb("best", [P, NT, 8]) if top else None
        chosen = [pl.sb(f"chosen{i}", [P, NT, E]) for i in range(2 if capacity else 1)] if top else None
        gates_t = pl.sb("gates_t", [EX, T])
        logit = pl.ps("logit", [P, NT // GB if NT >= GB else 1, BANK])

        def tile_logits(t):
            return logit[:, t // GB, t % GB * E:(t % GB + 1) * E]

        banks = max(1, NT // GB)
        all_logits = logit[:, :, 0:min(BANK, NT * E)].rearrange("p a (b e) -> p (a b) e", e=E)
        turned = pl.ps("turned", [EX, 2, BANK])
        const_in = pl.sem("const_in")
        logits_full = pl.sem("logits_full")
        vec = pl.sem("vec")
        act_done = pl.sem("act_done")
        turned_full = pl.sem("turned_full")
        turned_free = pl.sem("turned_free")
        stored = pl.sem("stored")
        if capacity:
            marks = pl.sb("marks", [P, NT, 2 * E], BF16)
            tri = pl.sb("tri", [P, P])
            tri16 = pl.sb("tri16", [P, P], BF16)
            ones16 = pl.sb("ones16", [P, P], BF16)
            totals = pl.sb("totals", [P, 2 * E, NT])
            before = pl.sb("before", [P, 2 * E, NT])
            keep_e = pl.sb("keep_e", [P, 2 * E, NT])
            rank = pl.ps("rank", [P, NT, 2 * E])
            count = pl.ps("count", [P, NT, 2 * E])
            counted = pl.sem("counted")
            marked = pl.sem("marked")
        CONSTS = 16 * (2 + (bias_d is not None) + bool(capacity))
        exp_in = pl.sem("exp_in")
        gates_ready = pl.sem("gates_ready")

        with nc.Block() as block:
            @block.sync
            def _(eng):
                eng.dma_start(w[:, :], w_d).then_inc(const_in, 16)
                eng.dma_start(ident[:, :], ident_d).then_inc(const_in, 16)
                if bias_d is not None:
                    eng.dma_start(bias[:, :], bias_d.broadcast_to([P, E])).then_inc(const_in, 16)
                if capacity:
                    eng.dma_start(tri[:, :], tri_d).then_inc(const_in, 16)
                eng.wait_ge(turned_free, CH)
                eng.dma_start(gates_d, gates_t[:, :]).then_inc(stored, 16)
                eng.wait_ge(stored, 16)

            @block.tensor
            def _(eng):
                eng.wait_ge(const_in, CONSTS)
                for t in range(NT):
                    mm = eng.matmul(tile_logits(t), x_t[:, t * P:(t + 1) * P], w[:, :], start=True, stop=True)
                mm.then_inc(logits_full, 1)
                if capacity:
                    eng.wait_ge(marked, 1)
                    eng.matmul(rank[:, :, :].rearrange("p a b -> p (a b)"), tri16[:, :], marks[:, :, :].rearrange("p a b -> p (a b)"), start=True, stop=True)
                    eng.matmul(count[:, :, :].rearrange("p a b -> p (a b)"), ones16[:, :], marks[:, :, :].rearrange("p a b -> p (a b)"), start=True, stop=True).then_inc(counted, 1)
                eng.wait_ge(gates_ready, 1)
                for c in range(CH):
                    if c >= 2:
                        eng.wait_ge(turned_free, c - 1)
                    for t in range(4):
                        mm = eng.transpose(turned[:, c % 2, t * P:(t + 1) * P], gates[:, 4 * c + t, :], ident[:, :])
                    mm.then_inc(turned_full, 1)

            @block.scalar
            def _(eng):
                eng.wait_ge(exp_in, 1)
                eng.activation(score[:, :, :], score[:, :, :], ACT.Exp if squash == "softmax" else ACT.Sigmoid).then_inc(act_done, 1)

            @block.vector
            def _(eng):
                count_vec = [0]

                def then(op):
                    count_vec[0] += 1
                    op.then_inc(vec, 1)
                    eng.wait_ge(vec, count_vec[0])

                def wide(a):
                    return a.unsqueeze(2).broadcast_to([P, NT, E])

                def flat(a):
                    return a[:, :, :].rearrange("p a b -> p (a b)")

                if top:
                    then(eng.memset(keep[:, :, :], 1.0))
                    then(eng.memset(keep[:, :, 0:1], 0.0))
                if extra:
                    then(eng.memset(gates[:, :, E:EX], extra_value))
                eng.wait_ge(const_in, CONSTS)
                if capacity:
                    then(eng.memset(keep_e[:, :, :], 1.0))
                    then(eng.memset(keep_e[:, :, 0:1], 0.0))
                    then(eng.memset(ones16[:, :], 1.0))
                    then(eng.tensor_copy(tri16[:, :], tri[:, :]))
                eng.wait_ge(logits_full, 1)
                if bias_d is not None:
                    then(eng.tensor_tensor(score[:, :, :], all_logits, bias[:, :].unsqueeze(1).broadcast_to([P, NT, E]), ALU.add))
                else:
                    then(eng.tensor_copy(score[:, :, :], all_logits))
                if squash == "softmax":
                    then(eng.tensor_reduce(small[0][:, :], score[:, :, :], AX.X, ALU.max))
                    eng.tensor_tensor(score[:, :, :], score[:, :, :], wide(small[0][:, :]), ALU.subtract).then_inc(exp_in, 1)
                    eng.wait_ge(act_done, 1)
                    then(eng.tensor_reduce(small[0][:, :], score[:, :, :], AX.X, ALU.add))
                    then(eng.reciprocal(small[0][:, :], small[0][:, :]))
                    then(eng.tensor_tensor(score[:, :, :], score[:, :, :], wide(small[0][:, :]), ALU.mult))
                else:
                    eng.engine_nop().then_inc(exp_in, 1) if False else eng.sem_inc(exp_in, 1)
                    eng.wait_ge(act_done, 1)

                def select(k, dst):
                    for t in range(NT):
                        op = eng.max(best[:, t, :], score[:, t, :])
                    then(op)
                    limit = best[:, :, k - 1:k].broadcast_to([P, NT, E])
                    then(eng.tensor_tensor(tmp[0][:, :, :], score[:, :, :], limit, ALU.is_gt))
                    then(eng.tensor_tensor(tmp[1][:, :, :], score[:, :, :], limit, ALU.is_equal))
                    then(eng.tensor_reduce(small[0][:, :], tmp[0][:, :, :], AX.X, ALU.add))
                    then(eng.tensor_tensor_scan(flat(tmp[2]), flat(keep), flat(tmp[1]), 0.0, ALU.mult, ALU.add))
                    then(eng.tensor_tensor(tmp[2][:, :, :], tmp[2][:, :, :], wide(small[0][:, :]), ALU.add))
                    then(eng.tensor_scalar(tmp[2][:, :, :], tmp[2][:, :, :], float(k), None, ALU.is_le))
                    then(eng.tensor_tensor(tmp[2][:, :, :], tmp[2][:, :, :], tmp[1][:, :, :], ALU.mult))
                    then(eng.tensor_tensor(dst[:, :, :], tmp[2][:, :, :], tmp[0][:, :, :], ALU.add))

                out = gates[:, :, 0:E]
                if not top:
                    then(eng.tensor_copy(out, score[:, :, :]))
                else:
                    select(top, chosen[0])
                    then(eng.tensor_tensor(tmp[0][:, :, :], score[:, :, :], chosen[0][:, :, :], ALU.mult))
                    then(eng.tensor_reduce(small[0][:, :], tmp[0][:, :, :], AX.X, ALU.add))
                    then(eng.tensor_scalar(small[0][:, :], small[0][:, :], norm_eps, None, ALU.add))
                    then(eng.reciprocal(small[1][:, :], small[0][:, :]))
                    if not capacity:
                        then(eng.tensor_tensor(out, tmp[0][:, :, :], wide(small[1][:, :]), ALU.mult))
                    else:
                        select(1, chosen[1])
                        then(eng.tensor_tensor(chosen[0][:, :, :], chosen[0][:, :, :], chosen[1][:, :, :], ALU.subtract))
                        then(eng.tensor_copy(marks[:, :, 0:E], chosen[1][:, :, :]))
                        eng.tensor_copy(marks[:, :, E:2 * E], chosen[0][:, :, :]).then_inc(marked, 1)
                        eng.wait_ge(counted, 1)
                        then(eng.tensor_copy(totals[:, :, :], count[:, :, :].rearrange("p t e -> p e t")))
                        then(eng.tensor_tensor_scan(flat(before), flat(keep_e), flat(totals), 0.0, ALU.mult, ALU.add))
                        then(eng.tensor_copy(small[0][:, 0:E], before[:, 0:E, NT - 1:NT].rearrange("p a b -> p (a b)")))
                        then(eng.tensor_tensor(before[:, :, :], before[:, :, :], totals[:, :, :], ALU.subtract))
                        then(eng.tensor_tensor(before[:, E:2 * E, :], before[:, E:2 * E, :],
                                               small[0][:, 0:E].unsqueeze(2).broadcast_to([P, E, NT]), ALU.add))
                        for j in range(2):
                            dst = tmp[2 - j]
                            then(eng.tensor_tensor(dst[:, :, :], rank[:, :, j * E:(j + 1) * E],
                                                   before[:, j * E:(j + 1) * E, :].rearrange("p e t -> p t e"), ALU.add))
                            then(eng.tensor_scalar(dst[:, :, :], dst[:, :, :], float(capacity), None, ALU.is_le))
                            then(eng.tensor_tensor(dst[:, :, :], dst[:, :, :], chosen[1 - j][:, :, :], ALU.mult))
                        then(eng.tensor_tensor(tmp[2][:, :, :], tmp[2][:, :, :], tmp[1][:, :, :], ALU.add))
                        then(eng.tensor_tensor(tmp[2][:, :, :], tmp[2][:, :, :], score[:, :, :], ALU.mult))
                        then(eng.tensor_tensor(out, tmp[2][:, :, :], wide(small[1][:, :]), ALU.mult))
                eng.sem_inc(gates_ready, 1)
                for c in range(CH):
                    eng.wait_ge(turned_full, c + 1)
                    eng.tensor_copy(gates_t[:, c * BANK:(c + 1) * BANK], turned[:, c % 2, :]).then_inc(turned_free, 1)

        pl.close()


def experts(nc, stage, res_t, x_t, w_in, b_in, w_out, gates_d, b_out, units, J, act, gated):
    steps = CH * J
    LAG = 2
    HB = 2 if gated else 4
    HR = 4

    def run(eng, body):
        body(0, 0, True, units == 1)
        loops = (units - 2) // 2
        with eng.Fori(0, loops) as i:
            body(2 * i + 1, 1, False, False)
            body(2 * i + 2, 0, False, False)
        for n in range(2 * loops + 1, units):
            body(n, n % 2, False, n == units - 1)

    def schedule(first, last):
        order = []
        for s in range(steps + (LAG if last else 0)):
            if s < steps:
                order.append(("hidden", s, 0))
            if s >= LAG:
                order.append(("out", s - LAG, 0))
            elif not first:
                order.append(("out", steps + s - LAG, 1))
        return order

    with ExitStack() as ctx:
        pl = Place(nc, ctx, stage)
        G = 2 if gated else 1
        win = pl.sb("win", [P, 2, G * J, P])
        bin_ = pl.sb("bin", [P, 2, J]) if b_in is not None else None
        wout = pl.sb("wout", [P, 2, J, P])
        gate = pl.sb("gate", [P, 2, T])
        acted = pl.sb("acted", [P, HR, BANK])
        scaled = pl.sb("scaled", [P, HR, BANK])
        hidden = pl.ps("hidden", [P, HB, BANK])
        upper = pl.ps("upper", [P, HB, BANK]) if gated else None
        out = pl.ps("out", [P, 2, BANK])
        bout = pl.sb("bout", [units, P]) if b_out is not None else None
        rows = pl.sb("rows", [units, T]) if b_out is not None else None

        const_in = pl.sem("const_in")
        win_in = [pl.sem(f"win_in{q}") for q in range(2)]
        wout_in = [pl.sem(f"wout_in{q}") for q in range(2)]
        hidden_full = pl.sem("hidden_full")
        act_done = pl.sem("act_done")
        upped = pl.sem("upped")
        scaled_done = pl.sem("scaled_done")
        out_used = pl.sem("out_used")
        summed = pl.sem("summed")
        CONSTS = 32

        with nc.Block() as block:
            @block.sync
            def _(eng):
                if b_out is not None:
                    eng.dma_start(bout[:, :], b_out).then_inc(const_in, 16)
                    eng.dma_start(rows[:, :], gates_d[0:units, :]).then_inc(const_in, 16)

                def load(n, q):
                    eng.dma_start(win[:, q, :, :], w_in[n, :, :, :]).then_inc(win_in[q], 16)
                    if b_in is not None:
                        eng.dma_start(bin_[:, q, :], b_in[n, :, :]).then_inc(win_in[q], 16)
                    if gated:
                        for h in range(2):
                            eng.dma_start(gate[h * 64:h * 64 + 64, q, :], gates_d[bass.ds(2 * n + h, 1), :].broadcast_to([64, T])).then_inc(win_in[q], 16)
                    else:
                        eng.dma_start(gate[:, q, :], gates_d[bass.ds(n, 1), :].broadcast_to([P, T])).then_inc(win_in[q], 16)
                    eng.dma_start(wout[:, q, :, :], w_out[n, :, :, :]).then_inc(wout_in[q], 16)

                for n in range(min(2, units)):
                    load(n, n)

                def reload(n, q):
                    eng.wait_ge(out_used, steps * (n - 1))
                    load(n, q)

                with eng.Fori(1, units // 2) as i:
                    for q in range(2):
                        reload(2 * i + q, q)
                if units % 2:
                    reload(units - 1, (units - 1) % 2)

            INS = 16 * (2 + (b_in is not None) + gated)

            @block.tensor
            def _(eng):
                def body(n, q, first, last):
                    for what, s, back in schedule(first, last):
                        u, uq = (n - 1, 1 - q) if back else (n, q)
                        c, j = s // J, s % J
                        step = u * steps + s
                        if what == "hidden":
                            if s == 0:
                                eng.wait_ge(win_in[q], (n + 2 - q) * (INS // 2))
                            if not (first and s < HB):
                                eng.wait_ge(upped if gated else act_done, step - HB + 1)
                            for g in range(G):
                                mm = eng.matmul((upper if g else hidden)[:, s % HB, :], win[:, q, g * J + j, :],
                                                x_t[:, c * BANK:(c + 1) * BANK], start=True, stop=True)
                            mm.then_inc(hidden_full, 1)
                        else:
                            if s == 0:
                                eng.wait_ge(wout_in[uq], (u + 2 - uq) * 8)
                            if j == 0 and not (first and c < 2):
                                eng.wait_ge(summed, u * CH + c - 1)
                            eng.wait_ge(scaled_done, step + 1)
                            eng.matmul(out[:, c % 2, :], wout[:, uq, j, :], scaled[:, s % HR, :],
                                       start=(j == 0), stop=(j == J - 1)).then_inc(out_used, 1)

                run(eng, body)
                if b_out is not None:
                    eng.wait_ge(const_in, CONSTS)
                    for c in range(CH):
                        eng.wait_ge(summed, units * CH + c - 1)
                        eng.matmul(out[:, c % 2, :], bout[:, :], rows[:, c * BANK:(c + 1) * BANK],
                                   start=True, stop=True).then_inc(out_used, 1)

            @block.scalar
            def _(eng):
                def body(n, q, first, last):
                    for what, s, back in schedule(first, last):
                        if what != "hidden":
                            continue
                        j, step = s % J, n * steps + s
                        if s == 0:
                            eng.wait_ge(win_in[q], (n + 2 - q) * (INS // 2))
                        eng.wait_ge(hidden_full, step + 1)
                        if not (first and s < HR):
                            eng.wait_ge(scaled_done, step - HR + 1)
                        if b_in is not None:
                            eng.activation(acted[:, s % HR, :], hidden[:, s % HB, :], act,
                                           bias=bin_[:, q, j:j + 1]).then_inc(act_done, 1)
                        else:
                            eng.activation(acted[:, s % HR, :], hidden[:, s % HB, :], act).then_inc(act_done, 1)

                run(eng, body)

            @block.gpsimd
            def _(eng):
                def body(n, q, first, last):
                    for what, s, back in schedule(first, last):
                        if what != "hidden":
                            continue
                        step = n * steps + s
                        c = s // J
                        if s == 0:
                            eng.wait_ge(win_in[q], (n + 2 - q) * (INS // 2))
                        eng.wait_ge(upped if gated else act_done, step + 1)
                        if not (first and s < HR):
                            eng.wait_ge(out_used, step - HR + 1)
                        eng.tensor_tensor(scaled[:, s % HR, :], acted[:, s % HR, :],
                                          gate[:, q, c * BANK:(c + 1) * BANK], ALU.mult).then_inc(scaled_done, 1)

                run(eng, body)

            @block.vector
            def _(eng):
                def body(n, q, first, last):
                    for what, s, back in schedule(first, last):
                        u = n - 1 if back else n
                        step = u * steps + s
                        if what == "hidden" and gated:
                            eng.wait_ge(act_done, step + 1)
                            eng.tensor_tensor(acted[:, s % HR, :], acted[:, s % HR, :], upper[:, s % HB, :],
                                              ALU.mult).then_inc(upped, 1)
                        if what == "out" and s % J == J - 1:
                            c = s // J
                            eng.wait_ge(out_used, step + 1)
                            at = slice(c * BANK, (c + 1) * BANK)
                            if not first:
                                eng.wait_ge(summed, u * CH + c)
                            eng.tensor_tensor(res_t[:, at], res_t[:, at], out[:, c % 2, :], ALU.add).then_inc(summed, 1)

                run(eng, body)
                if b_out is not None:
                    for c in range(CH):
                        eng.wait_ge(out_used, units * steps + c + 1)
                        at = slice(c * BANK, (c + 1) * BANK)
                        eng.tensor_tensor(res_t[:, at], res_t[:, at], out[:, c % 2, :], ALU.add).then_inc(summed, 1)

        pl.close()


EXPERTS = 8
SMALL_EXPERTS = 64
SMALL = 64
CAPACITY = 2 * T // EXPERTS


def program(nc, d, out):
    gates = nc.dram_tensor("gates", (SMALL_EXPERTS + 2, T), F32, kind="Internal").ap()
    with ExitStack() as ctx:
        pl = Place(nc, ctx, "all")
        res_t = pl.sb("res_t", [P, T])
        xn_t = pl.sb("xn_t", [P, T])
        x_in = pl.sem("x_in")
        stored = pl.sem("stored")

        with nc.Block() as block:
            @block.sync
            def _(eng):
                eng.dma_start(res_t[:, :], d["x"]).then_inc(x_in, 16)
                eng.wait_ge(x_in, 16)

        layer_norm(nc, "n0", res_t, xn_t, d["avg"], d["bias0"])
        head_attention(nc, "a0", res_t, xn_t, d["w_qkv0"], d["w_o0"], d["ident"], d["rows2"], None,
                       groups=8, heads=2, scale=64 ** -0.5, eps=1e-10)
        with nc.sbuf_tensor("xp_t", [P, T], F32) as xp_t:
            whole_attention(nc, "b0", res_t, xn_t, xp_t, d["w_b0"], d["bias_b0"], d["ident"])
            route(nc, "r0", xp_t, d["w_g0"], d["b_g0"], None, d["ident"], gates[0:EXPERTS, :], EXPERTS,
                  top=0, norm_eps=0.0, squash="softmax", extra=0, extra_value=0.0, capacity=0)
            experts(nc, "e0", res_t, xp_t, d["w1_0"], d["b1_0"], d["w2_0"], gates[0:EXPERTS, :], d["b2_0"],
                    units=EXPERTS, J=4, act=ACT.Relu, gated=False)

        layer_norm(nc, "n1", res_t, xn_t, d["avg"], None)
        head_attention(nc, "a1", res_t, xn_t, d["w_qkv1"], d["w_o1"], d["ident"], d["rows4"], d["rope"],
                       groups=4, heads=4, scale=1.0, eps=0.0)
        route(nc, "r1", xn_t, d["w_g1"], None, None, d["ident"], gates[0:EXPERTS + 1, :], EXPERTS,
              top=2, norm_eps=1e-9, squash="softmax", extra=1, extra_value=0.1, capacity=0)
        experts(nc, "e1", res_t, xn_t, d["w1_1"], d["b1_1"], d["w2_1"], gates[0:EXPERTS + 1, :], d["b2_1"],
                units=EXPERTS + 1, J=4, act=ACT.Silu, gated=False)

        layer_norm(nc, "n2", res_t, xn_t, d["avg"], d["bias2"])
        linear_attention(nc, "a2", res_t, xn_t, d["w_qkv2"], d["w_o2"], d["mask2"], eps=1e-6)
        route(nc, "r2", xn_t, d["w_g2"], None, d["tri"], d["ident"], gates[0:EXPERTS, :], EXPERTS,
              top=2, norm_eps=0.0, squash="softmax", extra=0, extra_value=0.0, capacity=CAPACITY)
        experts(nc, "e2", res_t, xn_t, d["w1_2"], d["b1_2"], d["w2_2"], gates[0:EXPERTS, :], d["b2_2"],
                units=EXPERTS, J=4, act=ACT.Relu, gated=False)

        layer_norm(nc, "n3", res_t, xn_t, d["avg"], None)
        recurrent_mixing(nc, "a3", res_t, xn_t, {n[:-1]: a for n, a in d.items() if n.endswith("3") and n != "bias3"})
        route(nc, "r3", xn_t, d["w_route"], None, None, d["ident"], gates, SMALL_EXPERTS,
              top=8, norm_eps=1e-9, squash="sigmoid", extra=2, extra_value=1.0, capacity=0)
        experts(nc, "e3", res_t, xn_t, d["w1_small"], None, d["w2_small"], gates, None,
                units=SMALL_EXPERTS // 2 + 1, J=1, act=ACT.Silu, gated=True)

        with nc.Block() as block:
            @block.sync
            def _(eng):
                eng.dma_start(out, res_t[:, :]).then_inc(stored, 16)
                eng.wait_ge(stored, 16)


def lay_out(a):
    def mixture(w1, b1, w2, b2, tag):
        e = w1.shape[0]
        return {f"w1_{tag}": w1.reshape(e, P, 4, P), f"b1_{tag}": b1.reshape(e, 4, P).transpose(0, 2, 1),
                f"w2_{tag}": w2.reshape(e, 4, P, P).transpose(0, 2, 1, 3), f"b2_{tag}": b2.reshape(e, P)}

    def with_shared(w, shared):
        return np.concatenate([w, shared[None]])

    wqkv0 = np.stack([a[f"L0_attn_W{n}"].reshape(8, P, P).transpose(0, 2, 1) for n in "qkv"], 2)

    def lead(w):
        out = np.zeros((4, P, 4, 32), w.dtype)
        out[:, :, :, 0:8] = w.reshape(4, 4, 8, P).transpose(0, 3, 1, 2)
        return out.reshape(4, P, P)

    def even(w):
        return w.reshape(16, 8, P)[:, np.arange(8) // 2 * 2]
    wqkv1 = np.stack([lead(even(a["L1_attn_Wq"])), lead(even(a["L1_attn_Wk"])), lead(a["L1_attn_Wv"])], 2)
    w_o1 = np.zeros((4, 4, 32, P), np.float32)
    w_o1[:, :, 0:8] = a["L1_attn_Wo"].T.reshape(4, 4, 8, P)
    freqs = np.exp(np.arange(0, 8, 2, dtype=np.float32) * np.float32(-np.log(10000.0) / 8))
    angles = np.arange(N, dtype=np.float32)[None] * freqs[:, None]
    table = np.zeros((8, N), np.float32)
    table[0::2], table[1::2] = np.cos(angles), -np.sin(angles)
    rope = np.zeros((4, 32, 2, N), np.float32)
    rope[:, 0:8, 0], rope[:, 0:8, 1] = table / np.float32(np.sqrt(8.0)), table

    entry = np.arange(4 * P).reshape(4, P)
    key_of, value_of = entry // 8, entry // 32 * 8 + entry % 8
    cols3 = np.zeros((P, 20), np.float32)
    cols3[:, 0], cols3[:, 1:6] = a["L3_attn_mu_x"], a["L3_attn_x_bias"].T
    cols3[:, 6:10], cols3[:, 10:14] = a["L3_attn_b_w2"][key_of].T, a["L3_attn_u"].reshape(64)[key_of].T
    cols3[:, 14], cols3[:, 15] = a["L3_attn_gn_w"], a["L3_attn_gn_b"]
    x2 = a["L3_attn_W_x2"].transpose(1, 2, 0)

    def side_by_side(w, shared):
        w = np.concatenate([w, shared[None], np.zeros_like(shared)[None]])
        return w.reshape(33, 2, P, SMALL).transpose(0, 2, 1, 3).reshape(33, P, P)
    down = a["L3_ffn_shared_down_w"]

    p, j = np.arange(P)[:, None], np.arange(P)[None]
    return {
        "x": a["L0_attn_x"].reshape(T, P).T, "avg": np.full((P, P), 1.0 / P, np.float32),
        "ident": np.eye(P, dtype=np.float32), "tri": (p <= j).astype(np.float32),
        "rows2": (p % 64 == j[:, :8]).astype(np.float32), "rows4": (p % 32 == j[:, :8]).astype(np.float32),
        "bias0": a["L0_attn_bo"].reshape(P, 1), "w_qkv0": wqkv0, "w_o0": a["L0_attn_Wo"].T.reshape(8, P, P),
        "w_b0": np.stack([a[f"L0_ffn_W{n}"] for n in "qkvo"], 1), "bias_b0": np.stack([a[f"L0_ffn_b{n}"] for n in "qkvo"], 1),
        "w_g0": a["L0_ffn_Wg"], "b_g0": a["L0_ffn_bg"].reshape(1, EXPERTS),
        **mixture(a["L0_ffn_W1"], a["L0_ffn_b1"], a["L0_ffn_W2"], a["L0_ffn_b2"], "0"),
        "w_qkv1": wqkv1, "w_o1": w_o1.reshape(4, P, P), "rope": rope.reshape(P, 2, N), "w_g1": a["L1_ffn_Wg"],
        **mixture(with_shared(a["L1_ffn_W1"], a["L1_ffn_Ws1"]), with_shared(a["L1_ffn_b1"], a["L1_ffn_bs1"]),
                  with_shared(a["L1_ffn_W2"], a["L1_ffn_Ws2"]), with_shared(a["L1_ffn_b2"], a["L1_ffn_bs2"]), "1"),
        "bias2": a["L2_attn_bout"].reshape(P, 1),
        "w_qkv2": a["L2_attn_Wqkv"].reshape(P, 3, 8, P).transpose(2, 0, 1, 3).reshape(8, P, 3 * P),
        "w_o2": a["L2_attn_Wout"].reshape(8, P, P), "mask2": (p // 64 == j // 64).astype(np.float32),
        "w_g2": a["L2_ffn_gate_w"].T,
        **mixture(a["L2_ffn_fc1_w"].transpose(0, 2, 1), a["L2_ffn_fc1_b"], a["L2_ffn_fc2_w"], a["L2_ffn_fc2_b"], "2"),
        "cols3": cols3, "w_x13": a["L3_attn_W_x1"], "w_x23": x2[:4].reshape(P, P), "w_x2b3": x2[4],
        "w_w13": a["L3_attn_W_w1"], "w_w23": a["L3_attn_W_w2"][:, key_of], "w_r3": a["L3_attn_W_r"][:, key_of],
        "w_k3": a["L3_attn_W_k"][:, key_of], "w_v3": a["L3_attn_W_v"][:, value_of], "w_g3": a["L3_attn_W_g"],
        "w_o3": a["L3_attn_W_o"], "pick3": (p // 32 * 8 + p % 8 == j[:, :32]).astype(np.float32),
        "blocks3": (p // 8 == j // 8).astype(np.float32) / 8,
        "w_route": a["L3_ffn_router_w"],
        "w1_small": np.stack([side_by_side(a["L3_ffn_expert_gate_k"], a["L3_ffn_shared_gate_w"]),
                              side_by_side(a["L3_ffn_expert_up_k"], a["L3_ffn_shared_up_w"])], 2),
        "w2_small": np.concatenate([a["L3_ffn_expert_down_k"], down[None], np.zeros_like(down)[None]]).reshape(33, P, 1, P),
    }


def kernel(**inputs):
    import concourse.bacc as bacc
    from concourse.bass_utils import run_bass_kernel_spmd

    laid = lay_out({n: np.asarray(v) for n, v in inputs.items()})
    arrays = {f"in_{n}": np.ascontiguousarray(v) for n, v in laid.items()}
    nc = bacc.Bacc("TRN2", target_bir_lowering=False, num_devices=1)
    operands = {n: nc.dram_tensor(f"in_{n}", arrays[f"in_{n}"].shape, mybir.dt.from_np(arrays[f"in_{n}"].dtype), kind="ExternalInput").ap()
                for n in laid}
    out = nc.dram_tensor("out_t", (P, T), F32, kind="ExternalOutput").ap()
    program(nc, operands, out)
    result = run_bass_kernel_spmd(nc, [arrays], core_ids=[0]).results[0]["out_t"]
    return np.ascontiguousarray(result.T).reshape(B, N, P)
```

```python
from contextlib import ExitStack

import numpy as np
import concourse.bass as bass
from concourse import mybir

F32 = mybir.dt.float32
F16 = mybir.dt.float16
BF16 = mybir.dt.bfloat16
ALU = mybir.AluOpType
ACT = mybir.ActivationFunctionType
AX = mybir.AxisListType

P = 128
B, N = 4, 1024
T = B * N
BANK = 512
CH = T // BANK
NT = T // P


class Place:

    def __init__(self, nc, ctx, stage):
        self.nc, self.ctx, self.stage, self.sems = nc, ctx, stage, []

    def sb(self, name, shape, dt=F32):
        return self.ctx.enter_context(self.nc.sbuf_tensor(f"{self.stage}_{name}", shape, dt))

    def ps(self, name, shape, dt=F32):
        return self.ctx.enter_context(self.nc.psum_tensor(f"{self.stage}_{name}", shape, dt))

    def sem(self, name):
        self.sems.append(self.ctx.enter_context(self.nc.semaphore(f"{self.stage}_{name}")))
        return self.sems[-1]

    def close(self):
        with self.nc.Block() as block:
            @block.sync
            def _(eng):
                for s in self.sems:
                    eng.sem_clear(s)


class Steps:

    def __init__(self, sem, names):
        self.sem, self.names, self.place = sem, names, {n: i + 1 for i, n in enumerate(names)}
        assert len(self.place) == len(names)

    def wait(self, eng, name, rnd):
        if isinstance(rnd, int) and rnd < 0:
            return
        eng.wait_ge(self.sem, rnd * len(self.names) + self.place[name])


def layer_norm(nc, stage, res_t, xn_t, avg_d, bias_d):
    with ExitStack() as ctx:
        pl = Place(nc, ctx, stage)
        avg = pl.sb("avg", [P, P])
        bias = pl.sb("bias", [P, 1])
        cen = pl.sb("cen", [P, 2, BANK])
        sq = pl.sb("sq", [P, 2, BANK])
        std = pl.sb("std", [P, 2, BANK])
        mean = pl.ps("mean", [P, 2, BANK])
        var = pl.ps("var", [P, 2, BANK])
        const_in = pl.sem("const_in")
        mean_full = pl.sem("mean_full")
        centred = pl.sem("centred")
        squared = pl.sem("squared")
        var_full = pl.sem("var_full")
        eps_added = pl.sem("eps_added")
        rooted = pl.sem("rooted")
        inverted = pl.sem("inverted")
        done = pl.sem("done")

        with nc.Block() as block:
            @block.sync
            def _(eng):
                eng.dma_start(avg[:, :], avg_d).then_inc(const_in, 16)
                if bias_d is not None:
                    eng.dma_start(bias[:, :], bias_d).then_inc(const_in, 16)
                eng.wait_ge(const_in, 32 if bias_d is not None else 16)

            @block.tensor
            def _(eng):
                eng.wait_ge(const_in, 32 if bias_d is not None else 16)
                for c in range(CH + 1):
                    if c < CH:
                        if c >= 2:
                            eng.wait_ge(centred, c - 1)
                        eng.matmul(mean[:, c % 2, :], avg[:, :], res_t[:, c * BANK:(c + 1) * BANK],
                                   start=True, stop=True).then_inc(mean_full, 1)
                    if c >= 1:
                        eng.wait_ge(squared, c)
                        if c >= 3:
                            eng.wait_ge(eps_added, c - 2)
                        eng.matmul(var[:, (c - 1) % 2, :], avg[:, :], sq[:, (c - 1) % 2, :],
                                   start=True, stop=True).then_inc(var_full, 1)

            @block.scalar
            def _(eng):
                for c in range(CH + 1):
                    if c < CH:
                        eng.wait_ge(centred, c + 1)
                        if c >= 2:
                            eng.wait_ge(var_full, c - 1)
                        eng.activation(sq[:, c % 2, :], cen[:, c % 2, :], ACT.Square).then_inc(squared, 1)
                    if c >= 1:
                        eng.wait_ge(eps_added, c)
                        eng.activation(std[:, (c - 1) % 2, :], std[:, (c - 1) % 2, :], ACT.Sqrt).then_inc(rooted, 1)

            @block.vector
            def _(eng):
                if bias_d is not None:
                    eng.wait_ge(const_in, 32)
                for c in range(CH + 2):
                    if c < CH:
                        eng.wait_ge(mean_full, c + 1)
                        if c >= 2:
                            eng.wait_ge(done, c - 1)
                        at = slice(c * BANK, (c + 1) * BANK)
                        eng.tensor_tensor(cen[:, c % 2, :], res_t[:, at], mean[:, c % 2, :], ALU.subtract).then_inc(centred, 1)
                    if 1 <= c <= CH:
                        k = c - 1
                        eng.wait_ge(var_full, k + 1)
                        if k >= 2:
                            eng.wait_ge(done, k - 1)
                        eng.tensor_scalar(std[:, k % 2, :], var[:, k % 2, :], 1e-5, None, ALU.add).then_inc(eps_added, 1)
                        eng.wait_ge(rooted, k + 1)
                        eng.reciprocal(std[:, k % 2, :], std[:, k % 2, :]).then_inc(inverted, 1)
                        at = slice(k * BANK, (k + 1) * BANK)
                        if bias_d is not None:
                            eng.wait_ge(centred, k + 1)
                            eng.tensor_scalar(res_t[:, at], res_t[:, at], bias[:, 0:1], None, ALU.add)
                        eng.wait_ge(inverted, k + 1)
                        eng.tensor_tensor(xn_t[:, at], cen[:, k % 2, :], std[:, k % 2, :], ALU.mult).then_inc(done, 1)

        pl.close()


def head_attention(nc, stage, res_t, xn_t, w_qk, w_v, w_out, ident_d, consts_d, rope_d, pick_d,
                   groups, heads, scale, eps):
    small = heads == 4
    rows = P // heads
    units = B * groups
    kts = N // P
    events = N // BANK * kts
    pairs = heads // 2
    LAG = 2
    RING = 4
    projections = ["q0", "k0"] if small else ["q0", "k0", "q1", "k1"]
    maxima = [(h, qt) for h in range(heads) for qt in range(kts)]
    prep = ["v"] + projections + [("max", m) for m in range(len(maxima))] + ["shift"]
    PREP = len(prep)
    after = ["sums", "out"] if small else ["out"]
    BY_ACT = ("v", "sums", "out")
    CHUNKS = 4

    def schedule(first, last):
        jobs = []
        if not last:
            start = 2 * LAG
            jobs += [(start + i, job) for i, job in enumerate(["v"] + projections)]
            start += len(projections) + 3
            room = 2 * events - 2 - start
            jobs += [(start + m * room // len(maxima), ("max", m)) for m in range(len(maxima))]
            jobs.append((2 * events - 1, "shift"))
        for k, at in ([] if first else [(1, 2 * LAG)]) + [(0, 2 * (kts + LAG))]:
            if small:
                jobs.append((at + 1, ("sums", k)))
            jobs += [(at + 2 + i, (f"divide{i}", k)) for i in range(CHUNKS)]
            jobs.append((at + 2 + CHUNKS + 1, ("out", k)))
        jobs.sort(key=lambda j: j[0])
        order, state = [], [0, 0, 0, "dve"]

        def add(what, k, back):
            order.append((what, k, back, tuple(state)))
            if not what.startswith("divide"):
                by_act = what in BY_ACT
                state[:] = [state[0] + 1, state[1] + by_act, state[2] + (not by_act), "act" if by_act else "dve"]

        for g in range(2 * (events + (LAG if last else 0))):
            e = g // 2
            if g % 2 == 0 and e < events:
                order.append(("scores", e, 0, None))
            if e >= LAG:
                order.append((f"values{g % 2}", e - LAG, 0, None))
            elif not first:
                order.append((f"values{g % 2}", events + e - LAG, 1, None))
            for at, job in jobs:
                if at == g:
                    what, k = job if isinstance(job, tuple) else (job, 0)
                    add(what, k, int(what[0] in "sdo" and what != "shift" and k == 1))
        if last:
            for what in (["sums"] if small else []) + [f"divide{i}" for i in range(CHUNKS)] + ["out"]:
                add(what, 1, 0)
        return order

    def prepare():
        order, state = [], [0, 0, 0, "dve"]
        for job in prep:
            what, k = job if isinstance(job, tuple) else (job, 0)
            order.append((what, k, 0, tuple(state)))
            by_act = what in BY_ACT
            state[:] = [state[0] + 1, state[1] + by_act, state[2] + (not by_act), "act" if by_act else "dve"]
        return order

    def run(eng, body):
        short = len(after)

        def base(n):
            return (n * (PREP + 2 * short) + PREP - short, n * (1 + 2 * short) + 1 - short, n * (PREP - 1) + PREP - 1)
        body(-1, 1, (0, 0, 0), prepare())
        body(0, 0, (PREP, 1, PREP - 1), schedule(True, False))
        with eng.Fori(0, (units - 2) // 2) as i:
            body(2 * i + 1, 1, base(2 * i + 1), schedule(False, False))
            body(2 * i + 2, 0, base(2 * i + 2), schedule(False, False))
        body(units - 1, 1, base(units - 1), schedule(False, True))

    def known(n, below):
        return isinstance(n, int) and n < below

    with ExitStack() as ctx:
        pl = Place(nc, ctx, stage)
        QC = len(projections)
        xb = pl.sb("xb", [P, 2, N])
        wqk = pl.sb("wqk", [P, 2, QC, P])
        wv = pl.sb("wv", [P, 2, heads * rows if not small else 32])
        wo = pl.sb("wo", [P, 2, P])
        ident = pl.sb("ident", [P, P])
        consts = pl.sb("consts", [P, 16])
        rowmask = consts[:, 0:kts]
        rope = pl.sb("rope", [P, 2, N]) if small else None
        pick = pl.sb("pick", [P, P]) if small else None
        whole = [pl.sb(f"whole_{c}", [P, N]) for c in "qk"] if small else None
        part = [pl.sb(f"part_{c}", [P, N], F16) for c in "qk"] if small else None
        bare = pl.sb("bare", [P, N], F16) if small else None
        spread = pl.sb("spread", [P, kts, P], F16) if small else None
        QH = 1 if small else 2
        qa = pl.sb("qa", [P, 2, QH, N], F16)
        ka = pl.sb("ka", [P, 2, QH, N], F16)
        qb = None if small else pl.sb("qb", [P, 2, 2, N], F16)
        kb = None if small else pl.sb("kb", [P, 2, 2, N], F16)
        v = pl.sb("v", [P, 2, kts, heads, 32 if small else P])
        row_max = pl.sb("row_max", [P, QH, P])
        prob = pl.sb("prob", [P, RING, heads, BANK])
        raw = pl.sb("raw", [P, BANK])
        denom = pl.sb("denom", [P, BANK])
        mixed = pl.sb("mixed", [P, 2, BANK])
        proj = pl.sb("proj", [P, 2, BANK])
        score = pl.ps("score", [P, 2, 2, BANK])
        side = pl.ps("side", [P, 2, BANK])
        o_ps = pl.ps("o_ps", [P, QH, BANK])
        side_flat = side[:, :, :].rearrange("p a b -> p (a b)")

        const_in = pl.sem("const_in")
        unit_in = [pl.sem(f"unit_in{q}") for q in range(2)]
        wo_in = [pl.sem(f"wo_in{q}") for q in range(2)]
        filled = pl.sem("filled")
        side_full = pl.sem("side_full")
        act_freed = pl.sem("act_freed")
        dve_freed = pl.sem("dve_freed")
        high_done = pl.sem("high_done")
        weighed = pl.sem("weighed")
        stacked = pl.sem("stacked")
        score_full = pl.sem("score_full")
        exp_done = pl.sem("exp_done")
        pv_done = pl.sem("pv_done")
        raw_ready = pl.sem("raw_ready")
        inverted = pl.sem("inverted")
        spread_done = pl.sem("spread_done")
        out_ready = pl.sem("out_ready")
        added = pl.sem("added")
        CONSTS = 16 * (4 if small else 2)

        with nc.Block() as block:
            @block.sync
            def _(eng):
                eng.dma_start(ident[:, :], ident_d).then_inc(const_in, 16)
                eng.dma_start(consts[:, :], consts_d).then_inc(const_in, 16)
                if small:
                    eng.dma_start(rope[:, :, :], rope_d).then_inc(const_in, 16)
                    eng.dma_start(pick[:, :], pick_d).then_inc(const_in, 16)

                def load(q, b, g):
                    eng.dma_start(xb[:, q, :], xn_t[:, bass.ds(b * N, N)]).then_inc(unit_in[q], 16)
                    eng.dma_start(wqk[:, q, :, :], w_qk[g, :, :, :]).then_inc(unit_in[q], 16)
                    eng.dma_start(wv[:, q, :], w_v[g, :, :]).then_inc(unit_in[q], 16)

                def load_out(q, g):
                    eng.dma_start(wo[:, q, :], w_out[g, :, :]).then_inc(wo_in[q], 16)

                for q in range(2):
                    load(q, 0, q)
                    load_out(q, q)
                with eng.Fori(1, units // 2) as i:
                    for q in range(2):
                        n = 2 * i + q
                        g = 2 * (i % (groups // 2)) + q
                        eng.wait_ge(high_done, QC * (n - 1))
                        load(q, i // (groups // 2), g)
                        eng.wait_ge(added, 2 * (n - 1))
                        load_out(q, g)

            @block.tensor
            def _(eng):
                eng.wait_ge(const_in, CONSTS)
                eng.wait_ge(filled, 1)

                def body(n, q, base, order):
                    m, r = n + 1, 1 - q
                    for what, k, back, done in order:
                        if what == "scores":
                            if k == 0:
                                eng.wait_ge(dve_freed, base[2])
                            qs, keys = slice(k // kts * BANK, (k // kts + 1) * BANK), slice(k % kts * P, (k % kts + 1) * P)
                            for hp in range(pairs):
                                step = (n * events + k) * pairs + hp
                                slot = (k * pairs + hp) % 2
                                if not known(n, 1) or k * pairs + hp >= 2:
                                    eng.wait_ge(exp_done, step - 1)
                                for j in range(2):
                                    if small:
                                        at = slice((2 * hp + j) * 32, (2 * hp + j + 1) * 32)
                                        mm = eng.matmul(score[:, slot, j, :], ka[at, q, 0, keys], qa[at, q, 0, qs], start=True, stop=True)
                                    else:
                                        eng.matmul(score[:, slot, j, :], ka[:, q, j, keys], qa[:, q, j, qs], start=True, stop=False)
                                        mm = eng.matmul(score[:, slot, j, :], kb[:, q, j, keys], qb[:, q, j, qs], start=False, stop=True)
                                mm.then_inc(score_full, 1)
                        elif what in ("values0", "values1"):
                            u, uq = (n - 1, 1 - q) if back else (n, q)
                            half, second = 2 * u + k // kts, what == "values1"
                            if not second:
                                eng.wait_ge(exp_done, (u * events + k + 1) * pairs)
                                if k % kts == 0 and not known(half, 1):
                                    eng.wait_ge(raw_ready, half)
                            for h in range(second * pairs, (second + 1) * pairs):
                                dst = o_ps[32 * h:32 * h + 32, 0, :] if small else o_ps[:, h, :]
                                mm = eng.matmul(dst, v[:, uq, k % kts, h, :], prob[:, k % RING, h, :],
                                                start=(k % kts == 0), stop=(k % kts == kts - 1))
                            if second:
                                mm.then_inc(pv_done, 1)
                        elif not what.startswith("divide"):
                            if not known(base[0] + done[0], 1):
                                if done[3] == "act":
                                    eng.wait_ge(act_freed, base[1] + done[1])
                                else:
                                    eng.wait_ge(dve_freed, base[2] + done[2])
                            if what == "v":
                                eng.wait_ge(unit_in[r], 24 * (m + 2 - r))
                                width = 32 if small else P
                                for kt in range(kts):
                                    mm = eng.matmul(side_flat[:, kt * width:(kt + 1) * width],
                                                    xb[:, r, kt * P:(kt + 1) * P], wv[:, r, :], start=True, stop=True)
                            elif what in projections:
                                for c in range(2):
                                    mm = eng.matmul(side[:, c, :], wqk[:, r, projections.index(what), :],
                                                    xb[:, r, c * BANK:(c + 1) * BANK], start=True, stop=True)
                            elif what == "max":
                                h, qt = maxima[k]
                                if small and k == 0:
                                    eng.wait_ge(stacked, 2 * m + 2)
                                for c in range(2):
                                    at, qq = (slice(h * 32, h * 32 + 32), bare[:, qt * P:(qt + 1) * P]) if small \
                                        else (slice(0, P), qa[:, r, h, qt * P:(qt + 1) * P])
                                    mm = eng.matmul(side[:, c, :], qq[at, :], ka[at, r, 0 if small else h, c * BANK:(c + 1) * BANK],
                                                    start=True, stop=True)
                            elif what == "shift":
                                for h in range(QH):
                                    mm = eng.transpose(side[:, h, 0:P], row_max[:, h, :], ident[:, :])
                            elif what == "sums":
                                u = n - 1 if back else n
                                eng.wait_ge(raw_ready, 2 * u + k + 1)
                                mm = eng.matmul(side[:, 0, :], pick[:, :], raw[:, :], start=True, stop=True)
                            elif what == "out":
                                u, uq = (n - 1, 1 - q) if back else (n, q)
                                eng.wait_ge(wo_in[uq], 8 * (u + 2 - uq))
                                eng.wait_ge(out_ready, CHUNKS * (2 * u + k + 1))
                                mm = eng.matmul(side[:, 0, :], wo[:, uq, :], mixed[:, k, :], start=True, stop=True)
                            mm.then_inc(side_full, 1)

                run(eng, body)

            @block.scalar
            def _(eng):
                eng.wait_ge(filled, 1)
                eng.wait_ge(const_in, CONSTS)

                def body(n, q, base, order):
                    m, r = n + 1, 1 - q
                    for what, k, back, done in order:
                        if what in projections:
                            c = projections.index(what)
                            if small:
                                eng.wait_ge(dve_freed, base[2] + done[2] + 1)
                                if not known(m, 1):
                                    eng.wait_ge(stacked, 2 * m - 1 + c)
                                eng.activation(part[c][:, :], whole[c][:, :], ACT.Copy).then_inc(high_done, 1)
                                eng.wait_ge(high_done, QC * m + c + 1)
                                eng.activation(whole[c][:, :], whole[c][:, :], ACT.Identity, scale=consts[:, 9 + 3 * c:10 + 3 * c],
                                               bias=consts[:, 10 + 3 * c:11 + 3 * c]).then_inc(weighed, 1)
                            else:
                                eng.wait_ge(side_full, base[0] + done[0] + 1)
                                if not known(n, 1):
                                    eng.wait_ge(score_full, events * pairs * n)
                                dst = (qa if c % 2 == 0 else ka)[:, r, c // 2, :]
                                eng.activation(dst, side_flat, ACT.Copy).then_inc(high_done, 1)
                        elif what == "scores":
                            for hp in range(pairs):
                                step = (n * events + k) * pairs + hp
                                slot = (k * pairs + hp) % 2
                                eng.wait_ge(score_full, step + 1)
                                if hp == 0 and not (known(n, 1) and k < RING):
                                    eng.wait_ge(pv_done, n * events + k - RING + 1)
                                eng.activation(prob[:, k % RING, 2 * hp:2 * hp + 2, :], score[:, slot, :, :],
                                               ACT.Exp, scale=scale).then_inc(exp_done, 1)
                        elif what == "values1" and k % kts == kts - 1:
                            half = 2 * (n - 1 if back else n) + k // kts
                            eng.wait_ge(pv_done, kts * half + kts)
                            if not known(half, 1):
                                eng.wait_ge(out_ready, CHUNKS * half)
                            if small:
                                eng.activation(raw[:, :], o_ps[:, 0, :], ACT.Copy).then_inc(raw_ready, 1)
                            else:
                                eng.activation(raw[0:64, :], o_ps[0:64, 0, :], ACT.Copy)
                                eng.activation(raw[64:128, :], o_ps[64:128, 1, :], ACT.Copy)
                                eng.activation(denom[0:64, :], o_ps[64:128, 0, :], ACT.Copy, bias=eps)
                                eng.activation(denom[64:128, :], o_ps[0:64, 1, :], ACT.Copy, bias=eps).then_inc(raw_ready, 1)
                        elif what in BY_ACT:
                            eng.wait_ge(side_full, base[0] + done[0] + 1)
                            if what == "v":
                                if not known(n, 1):
                                    eng.wait_ge(pv_done, events * n)
                                if small:
                                    src = side_flat[:, 0:kts * 32].rearrange("p (a b c) -> p a b c", a=kts, b=4)
                                    op = eng.activation(v[:, r, :, :, 0:8], src, ACT.Copy)
                                else:
                                    src = side_flat.rearrange("p (a b) -> p a b", a=kts)
                                    eng.activation(v[:, r, :, 0, 0:64], src[:, :, 0:64], ACT.Copy)
                                    op = eng.activation(v[:, r, :, 1, 64:128], src[:, :, 64:128], ACT.Copy)
                            elif what == "sums":
                                half = 2 * (n - 1 if back else n) + k
                                if not known(half, 1):
                                    eng.wait_ge(out_ready, CHUNKS * half)
                                op = eng.activation(denom[:, :], side[:, 0, :], ACT.Copy)
                            elif what == "out":
                                half = 2 * (n - 1 if back else n) + k
                                if not known(half, 2):
                                    eng.wait_ge(added, half - 1)
                                op = eng.activation(proj[:, k, :], side[:, 0, :], ACT.Copy)
                            op.then_inc(act_freed, 1)

                run(eng, body)

            @block.vector
            def _(eng):
                eng.memset(row_max[:, :, :], 0.0)
                if not small:
                    eng.memset(kb[64:128, :, :, :], 1.0)
                eng.memset(v[:, :, :, :, :], 1.0).then_inc(filled, 1)
                eng.wait_ge(filled, 1)
                eng.wait_ge(const_in, CONSTS)

                def body(n, q, base, order):
                    m, r = n + 1, 1 - q
                    for what, k, back, done in order:
                        if what in ("scores", "values0", "values1") or what in BY_ACT:
                            continue
                        if what.startswith("divide"):
                            half, i = 2 * (n - 1 if back else n) + k, int(what[-1])
                            at = slice(i * BANK // CHUNKS, (i + 1) * BANK // CHUNKS)
                            if i == 0:
                                if small:
                                    eng.wait_ge(act_freed, base[1] + done[1])
                                else:
                                    eng.wait_ge(raw_ready, half + 1)
                            eng.reciprocal(denom[:, at], denom[:, at]).then_inc(inverted, 1)
                            if i == 0 and not known(half, 2):
                                eng.wait_ge(added, half - 1)
                            eng.wait_ge(inverted, CHUNKS * half + i + 1)
                            eng.tensor_tensor(mixed[:, k, at], raw[:, at], denom[:, at], ALU.mult).then_inc(out_ready, 1)
                            continue
                        eng.wait_ge(side_full, base[0] + done[0] + 1)
                        if what in projections and small:
                            c = projections.index(what)
                            if not known(m, 1):
                                eng.wait_ge(stacked, 2 * m - 1 + c)
                            op = eng.tensor_tensor(whole[c][:, :], side_flat, rope[:, c, :], ALU.mult)
                        elif what in projections:
                            c = projections.index(what)
                            h = c // 2
                            eng.wait_ge(high_done, QC * m + c + 1)
                            if c % 2 == 0:
                                eng.tensor_copy(qb[0:64, r, h, :], qa[0:64, r, h, :])
                                op = eng.tensor_tensor(qa[64:128, r, h, :], side_flat[64:128, :], qa[64:128, r, h, :], ALU.subtract)
                            else:
                                op = eng.tensor_tensor(kb[0:64, r, h, :], side_flat[0:64, :], ka[0:64, r, h, :], ALU.subtract)
                        elif what == "max":
                            h, qt = maxima[k]
                            col = 32 * h + 24 + qt if small else 64 + qt
                            op = eng.tensor_reduce(row_max[:, 0 if small else h, col:col + 1], side_flat, AX.X, ALU.max)
                        elif what == "shift":
                            if small:
                                mask = rowmask.unsqueeze(2).broadcast_to([P, kts, P])
                                eng.scalar_tensor_tensor(out=spread[:, :, :], in0=side[:, 0:1, 0:P].broadcast_to([P, kts, P]), scalar=-1.0,
                                                         in1=mask, op0=ALU.mult, op1=ALU.mult).then_inc(spread_done, 1)
                                eng.wait_ge(spread_done, m + 1)
                                if not known(n, 1):
                                    eng.wait_ge(score_full, events * pairs * n)
                                op = eng.tensor_tensor(qa[:, r, 0, :], bare[:, :], spread[:, :, :].rearrange("p a b -> p (a b)"), ALU.add)
                            else:
                                mask = rowmask[64:128, :].unsqueeze(2).broadcast_to([64, kts, P])
                                for h in range(2):
                                    op = eng.scalar_tensor_tensor(
                                        out=qb[64:128, r, h, :].rearrange("p (a b) -> p a b", a=kts),
                                        in0=side[64:128, h:h + 1, 0:P].broadcast_to([64, kts, P]), scalar=-1.0,
                                        in1=mask, op0=ALU.mult, op1=ALU.mult)
                        op.then_inc(dve_freed, 1)
                        if what in projections and small:
                            c = projections.index(what)
                            eng.wait_ge(weighed, QC * m + c + 1)
                            if c == 1 and not known(n, 1):
                                eng.wait_ge(score_full, events * pairs * n)
                            dst = ka[:, r, 0, :] if c else bare[:, :]
                            eng.scalar_tensor_tensor(out=dst, in0=part[c][:, :], scalar=consts[:, 8 + 3 * c:9 + 3 * c],
                                                     in1=whole[c][:, :], op0=ALU.mult, op1=ALU.add).then_inc(stacked, 1)

                run(eng, body)

            @block.gpsimd
            def _(eng):
                def body(n, q, base, order):
                    for what, k, back, done in order:
                        if what == "out":
                            u = n - 1 if back else n
                            half = 2 * u + k
                            at = bass.ds((u // groups) * N + k * BANK, BANK)
                            eng.wait_ge(act_freed, base[1] + done[1] + 1)
                            if not known(half, 1):
                                eng.wait_ge(added, half)
                            eng.tensor_tensor(res_t[:, at], res_t[:, at], proj[:, k, :], ALU.add).then_inc(added, 1)

                run(eng, body)

        pl.close()


def whole_attention(nc, stage, res_t, xn_t, xp_t, w_d, bias_d, ident_d):
    qts = N // P
    scale = float(P) ** -0.5
    ORDER = [(what, t) for s in range(qts + 1) for what, t in (("scores", s), ("mix", s - 1)) if 0 <= t < qts]

    with ExitStack() as ctx:
        pl = Place(nc, ctx, stage)
        w = pl.sb("w", [P, 4, P])
        bias = pl.sb("bias", [P, 4])
        ident = pl.sb("ident", [P, P])
        xb = pl.sb("xb", [P, N])
        q = pl.sb("q", [P, N])
        k = pl.sb("k", [P, N])
        v = pl.sb("v", [P, qts, P])
        prob = pl.sb("prob", [P, 2, N])
        top = pl.sb("top", [P, 2])
        total = pl.sb("total", [P, 2])
        prob_t = pl.sb("prob_t", [P, 2, N])
        mixed = pl.sb("mixed", [P, 2, BANK])
        score = pl.ps("score", [P, 2, N])
        turned = pl.ps("turned", [P, N])
        mix = pl.ps("mix", [P, BANK])
        proj = pl.ps("proj", [P, BANK])
        const_in = pl.sem("const_in")
        x_in = pl.sem("x_in")
        projected = pl.sem("projected")
        q_ready = pl.sem("q_ready")
        kv_ready = pl.sem("kv_ready")
        score_full = pl.sem("score_full")
        maxed = pl.sem("maxed")
        negated = pl.sem("negated")
        exp_done = pl.sem("exp_done")
        inverted = pl.sem("inverted")
        prob_ready = pl.sem("prob_ready")
        turned_full = pl.sem("turned_full")
        turned_read = pl.sem("turned_read")
        mixed_tile = pl.sem("mixed_tile")
        mixed_half = pl.sem("mixed_half")
        proj_full = pl.sem("proj_full")
        xp_done = pl.sem("xp_done")
        res_done = pl.sem("res_done")

        def run(eng, body):
            body(0, True)
            with eng.Fori(1, B) as b:
                body(b, False)

        with nc.Block() as block:
            @block.sync
            def _(eng):
                eng.dma_start(w[:, :, :], w_d).then_inc(const_in, 16)
                eng.dma_start(bias[:, :], bias_d).then_inc(const_in, 16)
                eng.dma_start(ident[:, :], ident_d).then_inc(const_in, 16)
                eng.dma_start(xb[:, :], xn_t[:, 0:N]).then_inc(x_in, 16)
                with eng.Fori(1, B) as b:
                    eng.wait_ge(projected, 3 * b)
                    eng.dma_start(xb[:, :], xn_t[:, bass.ds(b * N, N)]).then_inc(x_in, 16)

            @block.tensor
            def _(eng):
                eng.wait_ge(const_in, 48)

                def body(b, first):
                    eng.wait_ge(x_in, 16 * b + 16)
                    if not first:
                        eng.wait_ge(exp_done, qts * b)
                        eng.wait_ge(turned_read, qts * b)
                    for c, dst in ((0, score[:, 0, :]), (1, score[:, 1, :])):
                        for h in range(2):
                            mm = eng.matmul(dst[:, h * BANK:(h + 1) * BANK], w[:, c, :], xb[:, h * BANK:(h + 1) * BANK],
                                            start=True, stop=True)
                        mm.then_inc(projected, 1)
                    for t in range(qts):
                        mm = eng.matmul(turned[:, t * P:(t + 1) * P], xb[:, t * P:(t + 1) * P], w[:, 2, :],
                                        start=True, stop=True)
                    mm.then_inc(projected, 1)
                    eng.wait_ge(q_ready, b + 1)
                    eng.wait_ge(kv_ready, 2 * b + 2)
                    for what, t in ORDER:
                        n = qts * b + t
                        if what == "scores":
                            if not (first and t < 2):
                                eng.wait_ge(exp_done, n - 1)
                            for h in range(2):
                                mm = eng.matmul(score[:, t % 2, h * BANK:(h + 1) * BANK], q[:, t * P:(t + 1) * P],
                                                k[:, h * BANK:(h + 1) * BANK], start=True, stop=True)
                            mm.then_inc(score_full, 1)
                            continue
                        eng.wait_ge(prob_ready, n + 1)
                        if not (first and t == 0):
                            eng.wait_ge(turned_read, n)
                        for kt in range(qts):
                            mm = eng.transpose(turned[:, kt * P:(kt + 1) * P], prob[:, t % 2, kt * P:(kt + 1) * P], ident[:, :])
                        mm.then_inc(turned_full, 1)
                        eng.wait_ge(turned_read, n + 1)
                        if t % 4 == 0 and not (first and t == 0):
                            eng.wait_ge(mixed_half, 2 * b + t // 4)
                        for kt in range(qts):
                            mm = eng.matmul(mix[:, t % 4 * P:(t % 4 + 1) * P], v[:, kt, :], prob_t[:, t % 2, kt * P:(kt + 1) * P],
                                            start=(kt == 0), stop=(kt == qts - 1))
                        mm.then_inc(mixed_tile, 1)
                        if t % 4 == 3:
                            half = 2 * b + t // 4
                            eng.wait_ge(mixed_half, half + 1)
                            if not (first and t == 3):
                                eng.wait_ge(xp_done, half)
                            eng.matmul(proj[:, :], w[:, 3, :], mixed[:, t // 4, :], start=True, stop=True).then_inc(proj_full, 1)

                run(eng, body)

            @block.scalar
            def _(eng):
                eng.wait_ge(const_in, 48)

                def body(b, first):
                    eng.wait_ge(projected, 3 * b + 2)
                    eng.activation(k[:, :], score[:, 1, :], ACT.Identity, bias=bias[:, 1:2]).then_inc(kv_ready, 1)
                    eng.wait_ge(projected, 3 * b + 3)
                    eng.activation(v[:, :, :].rearrange("p a b -> p (a b)"), turned[:, :], ACT.Copy).then_inc(kv_ready, 1)
                    for what, t in ORDER:
                        n = qts * b + t
                        if what == "scores":
                            eng.wait_ge(negated, n + 1)
                            if not (first and t < 2):
                                eng.wait_ge(turned_full, n - 1)
                            eng.activation(prob[:, t % 2, :], score[:, t % 2, :], ACT.Exp, bias=top[:, t % 2:t % 2 + 1],
                                           accum_out=total[:, t % 2:t % 2 + 1]).then_inc(exp_done, 1)
                        else:
                            eng.wait_ge(turned_full, n + 1)
                            if not (first and t < 2):
                                eng.wait_ge(mixed_tile, n - 1)
                            eng.activation(prob_t[:, t % 2, :], turned[:, :], ACT.Copy).then_inc(turned_read, 1)

                run(eng, body)

            @block.vector
            def _(eng):
                eng.wait_ge(const_in, 48)

                def body(b, first):
                    eng.wait_ge(projected, 3 * b + 1)
                    eng.tensor_scalar(q[:, :], score[:, 0, :], bias[:, 0:1], scale, ALU.add, ALU.mult).then_inc(q_ready, 1)
                    for what, t in ORDER:
                        n = qts * b + t
                        if what == "scores":
                            eng.wait_ge(score_full, n + 1)
                            if not (first and t < 2):
                                eng.wait_ge(exp_done, n - 1)
                            eng.tensor_reduce(top[:, t % 2:t % 2 + 1], score[:, t % 2, :], AX.X, ALU.max).then_inc(maxed, 1)
                            eng.wait_ge(maxed, n + 1)
                            eng.tensor_scalar(top[:, t % 2:t % 2 + 1], top[:, t % 2:t % 2 + 1], -1.0, None, ALU.mult).then_inc(negated, 1)
                            continue
                        eng.wait_ge(exp_done, n + 1)
                        eng.reciprocal(total[:, t % 2:t % 2 + 1], total[:, t % 2:t % 2 + 1]).then_inc(inverted, 1)
                        eng.wait_ge(inverted, n + 1)
                        eng.tensor_scalar(prob[:, t % 2, :], prob[:, t % 2, :], total[:, t % 2:t % 2 + 1], None, ALU.mult).then_inc(prob_ready, 1)
                        if t % 4 == 3:
                            half = 2 * b + t // 4
                            at = bass.ds(b * N + t // 4 * BANK, BANK)
                            eng.wait_ge(mixed_tile, n + 1)
                            if not (first and t < 8):
                                eng.wait_ge(proj_full, half - 1)
                            eng.tensor_scalar(mixed[:, t // 4, :], mix[:, :], bias[:, 2:3], None, ALU.add).then_inc(mixed_half, 1)
                            eng.wait_ge(proj_full, half + 1)
                            eng.scalar_tensor_tensor(out=xp_t[:, at], in0=proj[:, :], scalar=bias[:, 3:4], in1=xn_t[:, at],
                                                     op0=ALU.add, op1=ALU.add).then_inc(xp_done, 1)
                            eng.wait_ge(xp_done, half + 1)
                            eng.tensor_tensor(res_t[:, at], res_t[:, at], xp_t[:, at], ALU.add).then_inc(res_done, 1)

                run(eng, body)

        pl.close()


def linear_attention(nc, stage, res_t, xn_t, w_d, w_out_d, mask_d, eps):
    pairs = 8
    units = B * pairs
    tiles = N // P
    W = P + 2

    PREPARE = [("kv", i) for i in range(4)] + [("q", 0), ("state", 0)]

    def schedule(last):
        order = []
        for h in range(2):
            order.append(("mix", h))
            if not last:
                order += [("kv", 2 * h), ("kv", 2 * h + 1)]
                if h:
                    order.append(("q", 0))
            order.append(("out", h))
        if not last:
            order.append(("state", 0))
        return order

    def run(eng, body):
        body(-1, 1, PREPARE)
        body(0, 0, schedule(False))
        with eng.Fori(0, (units - 2) // 2) as i:
            body(2 * i + 1, 1, schedule(False))
            body(2 * i + 2, 0, schedule(False))
        body(units - 1, 1, schedule(True))

    with ExitStack() as ctx:
        pl = Place(nc, ctx, stage)
        xb = pl.sb("xb", [P, 2, N])
        w = pl.sb("w", [P, 2, 3 * P])
        wo = pl.sb("wo", [P, 2, P])
        mask = pl.sb("mask", [P, P])
        expk = pl.sb("expk", [P, 2, 2, P])
        relk = pl.sb("relk", [P, 2, 2, P])
        expq = pl.sb("expq", [P, N])
        relq = pl.sb("relq", [P, N])
        q_t = pl.sb("q_t", [P, 2, N])
        k_s = pl.sb("k_s", [P, tiles, P])
        v_s = pl.sb("v_s", [P, tiles, W])
        kv_blk = pl.sb("kv_blk", [P, 2, P])
        sum_blk = pl.sb("sum_blk", [P, 2, P])
        denom = pl.sb("denom", [P, BANK])
        mixed = pl.sb("mixed", [P, 2, BANK])
        q_ps = pl.ps("q_ps", [P, N])
        kv_ps = pl.ps("kv_ps", [P, 2, 2, 2, P])
        state = pl.ps("state", [P, BANK])
        num = pl.ps("num", [P, BANK])
        den = pl.ps("den", [P, BANK])
        out = pl.ps("out", [P, BANK])
        const_in = pl.sem("const_in")
        unit_in = [pl.sem(f"unit_in{r}") for r in range(2)]
        filled = pl.sem("filled")
        kv_full = pl.sem("kv_full")
        kv_read = pl.sem("kv_read")
        k_ready = pl.sem("k_ready")
        q_full = pl.sem("q_full")
        q_read = pl.sem("q_read")
        q_ready = pl.sem("q_ready")
        state_full = pl.sem("state_full")
        state_ready = pl.sem("state_ready")
        mix_full = pl.sem("mix_full")
        norm = pl.sem("norm")
        mixed_ready = pl.sem("mixed_ready")
        out_full = pl.sem("out_full")
        added = pl.sem("added")

        with nc.Block() as block:
            @block.sync
            def _(eng):
                eng.dma_start(mask[:, :], mask_d).then_inc(const_in, 16)

                def load(r, b, g):
                    eng.dma_start(xb[:, r, :], xn_t[:, bass.ds(b * N, N)]).then_inc(unit_in[r], 16)
                    eng.dma_start(w[:, r, :], w_d[g, :, :]).then_inc(unit_in[r], 16)
                    eng.dma_start(wo[:, r, :], w_out_d[g, :, :]).then_inc(unit_in[r], 16)

                for r in range(2):
                    load(r, 0, r)
                with eng.Fori(1, units // 2) as i:
                    for r in range(2):
                        eng.wait_ge(out_full, 2 * (2 * i + r - 1))
                        load(r, i // (pairs // 2), 2 * (i % (pairs // 2)) + r)

            @block.tensor
            def _(eng):
                eng.wait_ge(const_in, 16)
                eng.wait_ge(filled, 1)

                def body(n, q, order):
                    m, r = n + 1, 1 - q
                    for what, i in order:
                        if what == "kv":
                            if i == 0:
                                eng.wait_ge(unit_in[r], 24 * (m + 2 - r))
                            if not (isinstance(m, int) and m == 0 and i < 2):
                                eng.wait_ge(kv_read, 4 * m + i - 1)
                            for t in range(2):
                                tile = 2 * i + t
                                mm = eng.matmul(kv_ps[:, i % 2, t, :, :].rearrange("p a b -> p (a b)"),
                                                xb[:, r, tile * P:(tile + 1) * P], w[:, r, P:3 * P], start=True, stop=True)
                            mm.then_inc(kv_full, 1)
                        elif what == "q":
                            if not (isinstance(m, int) and m == 0):
                                eng.wait_ge(q_read, m)
                            for h in range(2):
                                mm = eng.matmul(q_ps[:, h * BANK:(h + 1) * BANK], w[:, r, 0:P],
                                                xb[:, r, h * BANK:(h + 1) * BANK], start=True, stop=True)
                            mm.then_inc(q_full, 1)
                        elif what == "state":
                            eng.wait_ge(k_ready, 4 * m + 4)
                            if not (isinstance(m, int) and m == 0):
                                eng.wait_ge(state_ready, 2 * m)
                            for t in range(tiles):
                                mm = eng.matmul(state[:, 0:W], k_s[:, t, :], v_s[:, t, :], start=(t == 0), stop=(t == tiles - 1))
                            mm.then_inc(state_full, 1)
                        elif what == "mix":
                            half = 2 * n + i
                            eng.wait_ge(state_ready, 2 * n + 2)
                            eng.wait_ge(q_ready, n + 1)
                            if not (isinstance(half, int) and half == 0):
                                eng.wait_ge(mixed_ready, half)
                            eng.matmul(den[:, :], sum_blk[:, q, :], q_t[:, q, i * BANK:(i + 1) * BANK], start=True, stop=True)
                            eng.matmul(num[:, :], kv_blk[:, q, :], q_t[:, q, i * BANK:(i + 1) * BANK],
                                       start=True, stop=True).then_inc(mix_full, 1)
                        elif what == "out":
                            half = 2 * n + i
                            eng.wait_ge(mixed_ready, half + 1)
                            if not (isinstance(half, int) and half == 0):
                                eng.wait_ge(added, half)
                            eng.matmul(out[:, :], wo[:, q, :], mixed[:, i, :], start=True, stop=True).then_inc(out_full, 1)

                run(eng, body)

            @block.scalar
            def _(eng):
                def body(n, q, order):
                    m, r = n + 1, 1 - q
                    for what, i in order:
                        if what == "kv":
                            eng.wait_ge(kv_full, 4 * m + i + 1)
                            if not (isinstance(m, int) and m == 0 and i < 2):
                                eng.wait_ge(k_ready, 4 * m + i - 1)
                            if i == 0 and not (isinstance(m, int) and m == 0):
                                eng.wait_ge(state_full, m)
                            eng.activation(expk[:, i % 2, :, :], kv_ps[:, i % 2, :, 0, :], ACT.Exp)
                            eng.activation(relk[:, i % 2, :, :], kv_ps[:, i % 2, :, 0, :], ACT.Relu)
                            eng.activation(v_s[:, 2 * i:2 * i + 2, 0:P], kv_ps[:, i % 2, :, 1, :], ACT.Copy).then_inc(kv_read, 1)
                        elif what == "q":
                            eng.wait_ge(q_full, m + 1)
                            if not (isinstance(m, int) and m == 0):
                                eng.wait_ge(q_ready, m)
                            eng.activation(expq[:, :], q_ps[:, :], ACT.Exp)
                            eng.activation(relq[:, :], q_ps[:, :], ACT.Relu).then_inc(q_read, 1)

                run(eng, body)

            @block.vector
            def _(eng):
                eng.memset(v_s[:, :, P:W], 1.0).then_inc(filled, 1)
                eng.wait_ge(const_in, 16)

                def body(n, q, order):
                    m, r = n + 1, 1 - q
                    for what, i in order:
                        if what == "kv":
                            eng.wait_ge(kv_read, 4 * m + i + 1)
                            if i == 0 and not (isinstance(m, int) and m == 0):
                                eng.wait_ge(state_full, m)
                            eng.scalar_tensor_tensor(out=k_s[:, 2 * i:2 * i + 2, :], in0=expk[:, i % 2, :, :], scalar=1.0,
                                                     in1=relk[:, i % 2, :, :], op0=ALU.min, op1=ALU.add).then_inc(k_ready, 1)
                        elif what == "q":
                            eng.wait_ge(q_read, m + 1)
                            if not (isinstance(n, int) and n <= 0):
                                eng.wait_ge(mix_full, 2 * n)
                            eng.scalar_tensor_tensor(out=q_t[:, r, :], in0=expq[:, :], scalar=1.0, in1=relq[:, :],
                                                     op0=ALU.min, op1=ALU.add).then_inc(q_ready, 1)
                        elif what == "state":
                            eng.wait_ge(state_full, m + 1)
                            if not (isinstance(n, int) and n <= 0):
                                eng.wait_ge(mix_full, 2 * n)
                            eng.tensor_tensor(kv_blk[:, r, :], state[:, 0:P], mask[:, :], ALU.mult).then_inc(state_ready, 1)
                            eng.tensor_scalar(sum_blk[:, r, :], mask[:, :], state[:, P:P + 1], None, ALU.mult).then_inc(state_ready, 1)
                        elif what == "mix":
                            half = 2 * n + i
                            eng.wait_ge(mix_full, half + 1)
                            if not (isinstance(half, int) and half == 0):
                                eng.wait_ge(mixed_ready, half)
                            eng.tensor_scalar(denom[:, :], den[:, :], eps, None, ALU.add).then_inc(norm, 1)
                            eng.wait_ge(norm, 2 * half + 1)
                            eng.reciprocal(denom[:, :], denom[:, :]).then_inc(norm, 1)
                            eng.wait_ge(norm, 2 * half + 2)
                            if not (isinstance(half, int) and half < 2):
                                eng.wait_ge(out_full, half - 1)
                            eng.tensor_tensor(mixed[:, i, :], num[:, :], denom[:, :], ALU.mult).then_inc(mixed_ready, 1)
                        elif what == "out":
                            half = 2 * n + i
                            at = bass.ds((n // pairs) * N + i * BANK, BANK)
                            eng.wait_ge(out_full, half + 1)
                            if not (isinstance(half, int) and half == 0):
                                eng.wait_ge(added, half)
                            eng.tensor_tensor(res_t[:, at], res_t[:, at], out[:, :], ALU.add).then_inc(added, 1)

                run(eng, body)

        pl.close()


def recurrent_mixing(nc, stage, res_t, xn_t, d):
    GROUPS = 4
    HV = 8

    with ExitStack() as ctx:
        pl = Place(nc, ctx, stage)
        shape = {"cols": [P, 20], "w_x1": [P, 160], "w_x2": [P, P], "w_x2b": [32, P], "w_w1": [P, 64],
                 "w_w2": [64, GROUPS, P], "w_r": [P, GROUPS, P], "w_k": [P, GROUPS, P], "w_v": [P, GROUPS, P],
                 "w_g": [P, P], "w_o": [P, P], "pick": [P, 32], "blocks": [P, P]}
        c = {n: pl.sb(n, s) for n, s in shape.items()}
        MU, XB, DB, U, GW, GB = 0, 1, 6, 10, 14, 15
        cols = c["cols"]
        xs = pl.sb("xs", [P, N + 1])
        x = xs[:, 1:N + 1]
        delta = pl.sb("delta", [P, N])
        z = pl.sb("z", [P, N])
        low = pl.sb("low", [P, N])
        low5 = pl.sb("low5", [32, N])
        mixed = pl.sb("mixed", [P, 5, N])
        wt = pl.sb("wt", [64, N])
        gs = pl.sb("gs", [P, N])
        vs = pl.sb("vs", [P, 2, N])
        decay = pl.sb("decay", [P, 2, N])
        kv = pl.sb("kv", [P, N])
        st = pl.sb("st", [P, N + 1])
        rs = pl.sb("rs", [P, 2, N])
        cen = pl.sb("cen", [P, N])
        sq = pl.sb("sq", [P, N])
        std = pl.sb("std", [P, N])
        work = [pl.ps(f"work{i}", [P, N]) for i in range(3)]
        o_ps = pl.ps("o_ps", [P, N])

        JOBS = [("low", "act", "low"), ("low5", "act", "low5")] \
            + [(f"mu{i}", "dve", f"mu{i}") for i in range(5)] \
            + [("tanh_w", "act", "wt"), ("g", "act", "gs")]
        for j in range(GROUPS):
            JOBS += [(f"v{j}", "act", f"vs{j}"), (f"w{j}", "act", f"ew{j}"), (f"k{j}", "dve", f"kv{j}"), (f"r{j}", "dve", f"rs{j}")]
        JOBS += [("mean", "dve", "cen"), ("var", "dve", "eps"), ("out", "dve", "res")]
        slot = {name: work[i % 3] for i, (name, _, _) in enumerate(JOBS)}
        PE = [name for name, _, _ in JOBS]
        for j in range(GROUPS):
            PE.insert(PE.index(f"r{j}") + (1 if j == GROUPS - 1 else 3), f"o{j}")
        ACTS = ["low", "low5", "wt", "gs"] + [s + str(j) for j in range(GROUPS) for s in ("vs", "ew", "decay")] + ["o", "sq", "std"]
        DVES = ["delta", "z"] + [f"mu{i}" for i in range(5)] \
            + [s + str(j) for j in range(GROUPS) for s in ("kv", "scan", "u", "rs")] \
            + ["cen", "eps", "rstd", "norm", "affine", "gated", "res"]
        POOLS = [f"x{i}" for i in range(5)]
        const_in = pl.sem("const_in")
        filled = pl.sem("filled")
        x_in = pl.sem("x_in")
        pe = Steps(pl.sem("pe_done"), PE)
        act = Steps(pl.sem("act_done"), ACTS)
        dve = Steps(pl.sem("dve_done"), DVES)
        pool = Steps(pl.sem("pool_done"), POOLS)
        reader = {"act": act, "dve": dve}

        def run(eng, body):
            body(0)
            with eng.Fori(1, B) as b:
                body(b)

        def before(b):
            return -1 if isinstance(b, int) else b - 1

        with nc.Block() as block:
            @block.sync
            def _(eng):
                for n in shape:
                    eng.dma_start(c[n][tuple(slice(None) for _ in shape[n])], d[n]).then_inc(const_in, 16)
                eng.wait_ge(filled, 2)
                eng.dma_start(x, xn_t[:, 0:N]).then_inc(x_in, 16)
                with eng.Fori(1, B) as b:
                    pool.wait(eng, "x4", b - 1)
                    eng.dma_start(x, xn_t[:, bass.ds(b * N, N)]).then_inc(x_in, 16)

            @block.tensor
            def _(eng):
                eng.wait_ge(const_in, 16 * len(shape))

                def product(b, name, lhs, rhs, dst=None, rows=P):
                    if dst is None:
                        i = [n for n, _, _ in JOBS].index(name)
                        same = [k for k in range(len(JOBS)) if k % 3 == i % 3]
                        at = same.index(i)
                        _, who, step = JOBS[same[at - 1]]
                        reader[who].wait(eng, step, b if at else before(b))
                        dst = slot[name]
                    for h in range(2):
                        mm = eng.matmul(dst[0:rows, h * BANK:(h + 1) * BANK], lhs, rhs[:, h * BANK:(h + 1) * BANK],
                                        start=True, stop=True)
                    mm.then_inc(pe.sem, 1)

                def body(b):
                    for name in PE:
                        j = int(name[-1]) if name[-1].isdigit() and name not in ("low5",) else 0
                        if name == "low":
                            dve.wait(eng, "z", b)
                            product(b, name, c["w_x1"][:, 0:P], z)
                        elif name == "low5":
                            product(b, name, c["w_x1"][:, P:160], z, rows=32)
                        elif name.startswith("mu"):
                            act.wait(eng, "low5" if j == 4 else "low", b)
                            if j < 4:
                                product(b, name, c["w_x2"][32 * j:32 * j + 32, :], low[32 * j:32 * j + 32, :])
                            else:
                                product(b, name, c["w_x2b"][:, :], low5)
                        elif name == "tanh_w":
                            pool.wait(eng, "x1", b)
                            product(b, name, c["w_w1"][:, :], mixed[:, 1, :], rows=64)
                        elif name == "g":
                            pool.wait(eng, "x4", b)
                            product(b, name, c["w_g"][:, :], mixed[:, 4, :])
                        elif name[0] == "v" and name != "var":
                            product(b, name, c["w_v"][:, j, :], mixed[:, 3, :])
                        elif name[0] == "w":
                            act.wait(eng, "wt", b)
                            product(b, name, c["w_w2"][:, j, :], wt)
                        elif name[0] == "k":
                            product(b, name, c["w_k"][:, j, :], mixed[:, 2, :])
                        elif name[0] == "r":
                            product(b, name, c["w_r"][:, j, :], mixed[:, 0, :])
                        elif name[0] == "o" and name != "out":
                            dve.wait(eng, f"rs{j}", b)
                            act.wait(eng, "o", before(b))
                            for h in range(2):
                                mm = eng.matmul(o_ps[32 * j:32 * j + 32, h * BANK:(h + 1) * BANK], c["pick"][:, :],
                                                rs[:, j % 2, h * BANK:(h + 1) * BANK], start=True, stop=True)
                            mm.then_inc(pe.sem, 1)
                        elif name == "mean":
                            act.wait(eng, "o", b)
                            product(b, name, c["blocks"][:, :], z)
                        elif name == "var":
                            act.wait(eng, "sq", b)
                            product(b, name, c["blocks"][:, :], sq)
                        elif name == "out":
                            dve.wait(eng, "gated", b)
                            product(b, name, c["w_o"][:, :], cen)

                run(eng, body)

            @block.scalar
            def _(eng):
                eng.wait_ge(const_in, 16 * len(shape))

                def body(b):
                    prev = before(b)
                    pe.wait(eng, "low", b)
                    pe.wait(eng, "mu3", prev)
                    eng.activation(low[:, :], slot["low"][:, :], ACT.Tanh).then_inc(act.sem, 1)
                    pe.wait(eng, "low5", b)
                    eng.activation(low5[:, :], slot["low5"][0:32, :], ACT.Tanh).then_inc(act.sem, 1)
                    pe.wait(eng, "tanh_w", b)
                    pe.wait(eng, f"w{GROUPS - 1}", prev)
                    eng.activation(wt[:, :], slot["tanh_w"][0:64, :], ACT.Tanh).then_inc(act.sem, 1)
                    pe.wait(eng, "g", b)
                    dve.wait(eng, "gated", prev)
                    eng.activation(gs[:, :], slot["g"][:, :], ACT.Silu).then_inc(act.sem, 1)
                    for j in range(GROUPS):
                        pe.wait(eng, f"v{j}", b)
                        if j >= 2:
                            dve.wait(eng, f"scan{j - 2}", b)
                        eng.activation(vs[:, j % 2, :], slot[f"v{j}"][:, :], ACT.Copy).then_inc(act.sem, 1)
                        pe.wait(eng, f"w{j}", b)
                        eng.activation(decay[:, j % 2, :], slot[f"w{j}"][:, :], ACT.Exp,
                                       bias=cols[:, DB + j:DB + j + 1]).then_inc(act.sem, 1)
                        act.wait(eng, f"ew{j}", b)
                        eng.activation(decay[:, j % 2, :], decay[:, j % 2, :], ACT.Exp, scale=-1.0).then_inc(act.sem, 1)
                    pe.wait(eng, f"o{GROUPS - 1}", b)
                    eng.activation(z[:, :], o_ps[:, :], ACT.Copy).then_inc(act.sem, 1)
                    dve.wait(eng, "cen", b)
                    eng.activation(sq[:, :], cen[:, :], ACT.Square).then_inc(act.sem, 1)
                    dve.wait(eng, "eps", b)
                    eng.activation(std[:, :], std[:, :], ACT.Sqrt).then_inc(act.sem, 1)

                run(eng, body)

            @block.gpsimd
            def _(eng):
                def body(b):
                    for i in range(5):
                        dve.wait(eng, f"mu{i}", b)
                        eng.tensor_tensor(mixed[:, i, :], mixed[:, i, :], x, ALU.add).then_inc(pool.sem, 1)

                run(eng, body)

            @block.vector
            def _(eng):
                eng.memset(xs[:, 0:1], 0.0).then_inc(filled, 1)
                eng.memset(st[:, 0:1], 0.0).then_inc(filled, 1)
                eng.wait_ge(filled, 2)
                eng.wait_ge(const_in, 16 * len(shape))

                def body(b):
                    prev = before(b)
                    eng.wait_ge(x_in, 16 * b + 16)
                    dve.wait(eng, "res", prev)
                    eng.tensor_tensor(delta[:, :], xs[:, 0:N], x, ALU.subtract).then_inc(dve.sem, 1)
                    dve.wait(eng, "delta", b)
                    eng.scalar_tensor_tensor(out=z[:, :], in0=delta[:, :], scalar=cols[:, MU:MU + 1], in1=x,
                                             op0=ALU.mult, op1=ALU.add).then_inc(dve.sem, 1)
                    for i in range(5):
                        pe.wait(eng, f"mu{i}", b)
                        if i == 0:
                            pe.wait(eng, f"r{GROUPS - 1}", prev)
                        eng.scalar_tensor_tensor(out=mixed[:, i, :], in0=slot[f"mu{i}"][:, :], scalar=cols[:, XB + i:XB + i + 1],
                                                 in1=delta[:, :], op0=ALU.add, op1=ALU.mult).then_inc(dve.sem, 1)
                    for j in range(GROUPS):
                        act.wait(eng, f"vs{j}", b)
                        pe.wait(eng, f"k{j}", b)
                        if j:
                            dve.wait(eng, f"u{j - 1}", b)
                        eng.tensor_tensor(kv[:, :], slot[f"k{j}"][:, :], vs[:, j % 2, :], ALU.mult).then_inc(dve.sem, 1)
                        act.wait(eng, f"decay{j}", b)
                        dve.wait(eng, f"kv{j}", b)
                        eng.tensor_tensor_scan(st[:, 1:N + 1], decay[:, j % 2, :], kv[:, :], 0.0, ALU.mult, ALU.add).then_inc(dve.sem, 1)
                        dve.wait(eng, f"scan{j}", b)
                        if j >= 2:
                            pe.wait(eng, f"o{j - 2}", b)
                        eng.scalar_tensor_tensor(out=rs[:, j % 2, :], in0=kv[:, :], scalar=cols[:, U + j:U + j + 1],
                                                 in1=st[:, 0:N], op0=ALU.mult, op1=ALU.add).then_inc(dve.sem, 1)
                        dve.wait(eng, f"u{j}", b)
                        pe.wait(eng, f"r{j}", b)
                        eng.tensor_tensor(rs[:, j % 2, :], rs[:, j % 2, :], slot[f"r{j}"][:, :], ALU.mult).then_inc(dve.sem, 1)
                    pe.wait(eng, "mean", b)
                    eng.tensor_tensor(cen[:, :], z[:, :], slot["mean"][:, :], ALU.subtract).then_inc(dve.sem, 1)
                    pe.wait(eng, "var", b)
                    eng.tensor_scalar(std[:, :], slot["var"][:, :], 1e-5, None, ALU.add).then_inc(dve.sem, 1)
                    act.wait(eng, "std", b)
                    eng.reciprocal(std[:, :], std[:, :]).then_inc(dve.sem, 1)
                    dve.wait(eng, "rstd", b)
                    eng.tensor_tensor(cen[:, :], cen[:, :], std[:, :], ALU.mult).then_inc(dve.sem, 1)
                    dve.wait(eng, "norm", b)
                    eng.tensor_scalar(cen[:, :], cen[:, :], cols[:, GW:GW + 1], cols[:, GB:GB + 1], ALU.mult, ALU.add).then_inc(dve.sem, 1)
                    dve.wait(eng, "affine", b)
                    act.wait(eng, "gs", b)
                    eng.tensor_tensor(cen[:, :], cen[:, :], gs[:, :], ALU.mult).then_inc(dve.sem, 1)
                    pe.wait(eng, "out", b)
                    at = bass.ds(b * N, N)
                    eng.tensor_tensor(res_t[:, at], res_t[:, at], slot["out"][:, :], ALU.add).then_inc(dve.sem, 1)

                run(eng, body)

        pl.close()


def route(nc, stage, x_t, w_d, bias_d, tri_d, ident_d, gates_d, E, top, norm_eps, squash, extra, extra_value, capacity):
    EX = E + extra
    GB = BANK // E

    with ExitStack() as ctx:
        pl = Place(nc, ctx, stage)
        w = pl.sb("w", [P, E])
        bias = pl.sb("bias", [P, E])
        ident = pl.sb("ident", [P, P])
        score = pl.sb("score", [P, NT, E])
        gates = pl.sb("gates", [P, NT, EX])
        small = [pl.sb(f"small{i}", [P, NT]) for i in range(2)]
        tmp = [pl.sb(f"tmp{i}", [P, NT, E]) for i in range(3)] if top else None
        keep = pl.sb("keep", [P, NT, E]) if top else None
        best = pl.sb("best", [P, NT, 8]) if top else None
        chosen = [pl.sb(f"chosen{i}", [P, NT, E]) for i in range(2 if capacity else 1)] if top else None
        gates_t = pl.sb("gates_t", [EX, T])
        logit = pl.ps("logit", [P, NT // GB if NT >= GB else 1, BANK])

        def tile_logits(t):
            return logit[:, t // GB, t % GB * E:(t % GB + 1) * E]

        banks = max(1, NT // GB)
        all_logits = logit[:, :, 0:min(BANK, NT * E)].rearrange("p a (b e) -> p (a b) e", e=E)
        turned = pl.ps("turned", [EX, 2, BANK])
        const_in = pl.sem("const_in")
        logits_full = pl.sem("logits_full")
        vec = pl.sem("vec")
        act_done = pl.sem("act_done")
        turned_full = pl.sem("turned_full")
        turned_free = pl.sem("turned_free")
        stored = pl.sem("stored")
        if capacity:
            marks = pl.sb("marks", [P, NT, 2 * E], BF16)
            tri = pl.sb("tri", [P, P])
            tri16 = pl.sb("tri16", [P, P], BF16)
            ones16 = pl.sb("ones16", [P, P], BF16)
            totals = pl.sb("totals", [P, 2 * E, NT])
            before = pl.sb("before", [P, 2 * E, NT])
            keep_e = pl.sb("keep_e", [P, 2 * E, NT])
            rank = pl.ps("rank", [P, NT, 2 * E])
            count = pl.ps("count", [P, NT, 2 * E])
            counted = pl.sem("counted")
            marked = pl.sem("marked")
        CONSTS = 16 * (2 + (bias_d is not None) + bool(capacity))
        exp_in = pl.sem("exp_in")
        gates_ready = pl.sem("gates_ready")

        with nc.Block() as block:
            @block.sync
            def _(eng):
                eng.dma_start(w[:, :], w_d).then_inc(const_in, 16)
                eng.dma_start(ident[:, :], ident_d).then_inc(const_in, 16)
                if bias_d is not None:
                    eng.dma_start(bias[:, :], bias_d.broadcast_to([P, E])).then_inc(const_in, 16)
                if capacity:
                    eng.dma_start(tri[:, :], tri_d).then_inc(const_in, 16)
                eng.wait_ge(turned_free, CH)
                eng.dma_start(gates_d, gates_t[:, :]).then_inc(stored, 16)
                eng.wait_ge(stored, 16)

            @block.tensor
            def _(eng):
                eng.wait_ge(const_in, CONSTS)
                for t in range(NT):
                    mm = eng.matmul(tile_logits(t), x_t[:, t * P:(t + 1) * P], w[:, :], start=True, stop=True)
                mm.then_inc(logits_full, 1)
                if capacity:
                    eng.wait_ge(marked, 1)
                    eng.matmul(rank[:, :, :].rearrange("p a b -> p (a b)"), tri16[:, :], marks[:, :, :].rearrange("p a b -> p (a b)"), start=True, stop=True)
                    eng.matmul(count[:, :, :].rearrange("p a b -> p (a b)"), ones16[:, :], marks[:, :, :].rearrange("p a b -> p (a b)"), start=True, stop=True).then_inc(counted, 1)
                eng.wait_ge(gates_ready, 1)
                for c in range(CH):
                    if c >= 2:
                        eng.wait_ge(turned_free, c - 1)
                    for t in range(4):
                        mm = eng.transpose(turned[:, c % 2, t * P:(t + 1) * P], gates[:, 4 * c + t, :], ident[:, :])
                    mm.then_inc(turned_full, 1)

            @block.scalar
            def _(eng):
                eng.wait_ge(exp_in, 1)
                eng.activation(score[:, :, :], score[:, :, :], ACT.Exp if squash == "softmax" else ACT.Sigmoid).then_inc(act_done, 1)

            @block.vector
            def _(eng):
                count_vec = [0]

                def then(op):
                    count_vec[0] += 1
                    op.then_inc(vec, 1)
                    eng.wait_ge(vec, count_vec[0])

                def wide(a):
                    return a.unsqueeze(2).broadcast_to([P, NT, E])

                def flat(a):
                    return a[:, :, :].rearrange("p a b -> p (a b)")

                if top:
                    then(eng.memset(keep[:, :, :], 1.0))
                    then(eng.memset(keep[:, :, 0:1], 0.0))
                if extra:
                    then(eng.memset(gates[:, :, E:EX], extra_value))
                eng.wait_ge(const_in, CONSTS)
                if capacity:
                    then(eng.memset(keep_e[:, :, :], 1.0))
                    then(eng.memset(keep_e[:, :, 0:1], 0.0))
                    then(eng.memset(ones16[:, :], 1.0))
                    then(eng.tensor_copy(tri16[:, :], tri[:, :]))
                eng.wait_ge(logits_full, 1)
                if bias_d is not None:
                    then(eng.tensor_tensor(score[:, :, :], all_logits, bias[:, :].unsqueeze(1).broadcast_to([P, NT, E]), ALU.add))
                else:
                    then(eng.tensor_copy(score[:, :, :], all_logits))
                if squash == "softmax":
                    then(eng.tensor_reduce(small[0][:, :], score[:, :, :], AX.X, ALU.max))
                    eng.tensor_tensor(score[:, :, :], score[:, :, :], wide(small[0][:, :]), ALU.subtract).then_inc(exp_in, 1)
                    eng.wait_ge(act_done, 1)
                    then(eng.tensor_reduce(small[0][:, :], score[:, :, :], AX.X, ALU.add))
                    then(eng.reciprocal(small[0][:, :], small[0][:, :]))
                    then(eng.tensor_tensor(score[:, :, :], score[:, :, :], wide(small[0][:, :]), ALU.mult))
                else:
                    eng.engine_nop().then_inc(exp_in, 1) if False else eng.sem_inc(exp_in, 1)
                    eng.wait_ge(act_done, 1)

                def select(k, dst):
                    for t in range(NT):
                        op = eng.max(best[:, t, :], score[:, t, :])
                    then(op)
                    limit = best[:, :, k - 1:k].broadcast_to([P, NT, E])
                    then(eng.tensor_tensor(tmp[0][:, :, :], score[:, :, :], limit, ALU.is_gt))
                    then(eng.tensor_tensor(tmp[1][:, :, :], score[:, :, :], limit, ALU.is_equal))
                    then(eng.tensor_reduce(small[0][:, :], tmp[0][:, :, :], AX.X, ALU.add))
                    then(eng.tensor_tensor_scan(flat(tmp[2]), flat(keep), flat(tmp[1]), 0.0, ALU.mult, ALU.add))
                    then(eng.tensor_tensor(tmp[2][:, :, :], tmp[2][:, :, :], wide(small[0][:, :]), ALU.add))
                    then(eng.tensor_scalar(tmp[2][:, :, :], tmp[2][:, :, :], float(k), None, ALU.is_le))
                    then(eng.tensor_tensor(tmp[2][:, :, :], tmp[2][:, :, :], tmp[1][:, :, :], ALU.mult))
                    then(eng.tensor_tensor(dst[:, :, :], tmp[2][:, :, :], tmp[0][:, :, :], ALU.add))

                out = gates[:, :, 0:E]
                if not top:
                    then(eng.tensor_copy(out, score[:, :, :]))
                else:
                    select(top, chosen[0])
                    then(eng.tensor_tensor(tmp[0][:, :, :], score[:, :, :], chosen[0][:, :, :], ALU.mult))
                    then(eng.tensor_reduce(small[0][:, :], tmp[0][:, :, :], AX.X, ALU.add))
                    then(eng.tensor_scalar(small[0][:, :], small[0][:, :], norm_eps, None, ALU.add))
                    then(eng.reciprocal(small[1][:, :], small[0][:, :]))
                    if not capacity:
                        then(eng.tensor_tensor(out, tmp[0][:, :, :], wide(small[1][:, :]), ALU.mult))
                    else:
                        select(1, chosen[1])
                        then(eng.tensor_tensor(chosen[0][:, :, :], chosen[0][:, :, :], chosen[1][:, :, :], ALU.subtract))
                        then(eng.tensor_copy(marks[:, :, 0:E], chosen[1][:, :, :]))
                        eng.tensor_copy(marks[:, :, E:2 * E], chosen[0][:, :, :]).then_inc(marked, 1)
                        eng.wait_ge(counted, 1)
                        then(eng.tensor_copy(totals[:, :, :], count[:, :, :].rearrange("p t e -> p e t")))
                        then(eng.tensor_tensor_scan(flat(before), flat(keep_e), flat(totals), 0.0, ALU.mult, ALU.add))
                        then(eng.tensor_copy(small[0][:, 0:E], before[:, 0:E, NT - 1:NT].rearrange("p a b -> p (a b)")))
                        then(eng.tensor_tensor(before[:, :, :], before[:, :, :], totals[:, :, :], ALU.subtract))
                        then(eng.tensor_tensor(before[:, E:2 * E, :], before[:, E:2 * E, :],
                                               small[0][:, 0:E].unsqueeze(2).broadcast_to([P, E, NT]), ALU.add))
                        for j in range(2):
                            dst = tmp[2 - j]
                            then(eng.tensor_tensor(dst[:, :, :], rank[:, :, j * E:(j + 1) * E],
                                                   before[:, j * E:(j + 1) * E, :].rearrange("p e t -> p t e"), ALU.add))
                            then(eng.tensor_scalar(dst[:, :, :], dst[:, :, :], float(capacity), None, ALU.is_le))
                            then(eng.tensor_tensor(dst[:, :, :], dst[:, :, :], chosen[1 - j][:, :, :], ALU.mult))
                        then(eng.tensor_tensor(tmp[2][:, :, :], tmp[2][:, :, :], tmp[1][:, :, :], ALU.add))
                        then(eng.tensor_tensor(tmp[2][:, :, :], tmp[2][:, :, :], score[:, :, :], ALU.mult))
                        then(eng.tensor_tensor(out, tmp[2][:, :, :], wide(small[1][:, :]), ALU.mult))
                eng.sem_inc(gates_ready, 1)
                for c in range(CH):
                    eng.wait_ge(turned_full, c + 1)
                    eng.tensor_copy(gates_t[:, c * BANK:(c + 1) * BANK], turned[:, c % 2, :]).then_inc(turned_free, 1)

        pl.close()


def experts(nc, stage, res_t, x_t, w_in, b_in, w_out, gates_d, b_out, units, J, act, gated):
    steps = CH * J
    LAG = 2
    HB = 2 if gated else 4
    HR = 4

    def run(eng, body):
        body(0, 0, True, units == 1)
        loops = (units - 2) // 2
        with eng.Fori(0, loops) as i:
            body(2 * i + 1, 1, False, False)
            body(2 * i + 2, 0, False, False)
        for n in range(2 * loops + 1, units):
            body(n, n % 2, False, n == units - 1)

    def schedule(first, last):
        order = []
        for s in range(steps + (LAG if last else 0)):
            if s < steps:
                order.append(("hidden", s, 0))
            if s >= LAG:
                order.append(("out", s - LAG, 0))
            elif not first:
                order.append(("out", steps + s - LAG, 1))
        return order

    with ExitStack() as ctx:
        pl = Place(nc, ctx, stage)
        G = 2 if gated else 1
        win = pl.sb("win", [P, 2, G * J, P])
        bin_ = pl.sb("bin", [P, 2, J]) if b_in is not None else None
        wout = pl.sb("wout", [P, 2, J, P])
        gate = pl.sb("gate", [P, 2, T])
        acted = pl.sb("acted", [P, HR, BANK])
        scaled = pl.sb("scaled", [P, HR, BANK])
        hidden = pl.ps("hidden", [P, HB, BANK])
        upper = pl.ps("upper", [P, HB, BANK]) if gated else None
        out = pl.ps("out", [P, 2, BANK])
        bout = pl.sb("bout", [units, P]) if b_out is not None else None
        rows = pl.sb("rows", [units, T]) if b_out is not None else None

        const_in = pl.sem("const_in")
        win_in = [pl.sem(f"win_in{q}") for q in range(2)]
        wout_in = [pl.sem(f"wout_in{q}") for q in range(2)]
        hidden_full = pl.sem("hidden_full")
        act_done = pl.sem("act_done")
        upped = pl.sem("upped")
        scaled_done = pl.sem("scaled_done")
        out_used = pl.sem("out_used")
        summed = pl.sem("summed")
        CONSTS = 32

        with nc.Block() as block:
            @block.sync
            def _(eng):
                if b_out is not None:
                    eng.dma_start(bout[:, :], b_out).then_inc(const_in, 16)
                    eng.dma_start(rows[:, :], gates_d[0:units, :]).then_inc(const_in, 16)

                def load(n, q):
                    eng.dma_start(win[:, q, :, :], w_in[n, :, :, :]).then_inc(win_in[q], 16)
                    if b_in is not None:
                        eng.dma_start(bin_[:, q, :], b_in[n, :, :]).then_inc(win_in[q], 16)
                    if gated:
                        for h in range(2):
                            eng.dma_start(gate[h * 64:h * 64 + 64, q, :], gates_d[bass.ds(2 * n + h, 1), :].broadcast_to([64, T])).then_inc(win_in[q], 16)
                    else:
                        eng.dma_start(gate[:, q, :], gates_d[bass.ds(n, 1), :].broadcast_to([P, T])).then_inc(win_in[q], 16)
                    eng.dma_start(wout[:, q, :, :], w_out[n, :, :, :]).then_inc(wout_in[q], 16)

                for n in range(min(2, units)):
                    load(n, n)

                def reload(n, q):
                    eng.wait_ge(out_used, steps * (n - 1))
                    load(n, q)

                with eng.Fori(1, units // 2) as i:
                    for q in range(2):
                        reload(2 * i + q, q)
                if units % 2:
                    reload(units - 1, (units - 1) % 2)

            INS = 16 * (2 + (b_in is not None) + gated)

            @block.tensor
            def _(eng):
                def body(n, q, first, last):
                    for what, s, back in schedule(first, last):
                        u, uq = (n - 1, 1 - q) if back else (n, q)
                        c, j = s // J, s % J
                        step = u * steps + s
                        if what == "hidden":
                            if s == 0:
                                eng.wait_ge(win_in[q], (n + 2 - q) * (INS // 2))
                            if not (first and s < HB):
                                eng.wait_ge(upped if gated else act_done, step - HB + 1)
                            for g in range(G):
                                mm = eng.matmul((upper if g else hidden)[:, s % HB, :], win[:, q, g * J + j, :],
                                                x_t[:, c * BANK:(c + 1) * BANK], start=True, stop=True)
                            mm.then_inc(hidden_full, 1)
                        else:
                            if s == 0:
                                eng.wait_ge(wout_in[uq], (u + 2 - uq) * 8)
                            if j == 0 and not (first and c < 2):
                                eng.wait_ge(summed, u * CH + c - 1)
                            eng.wait_ge(scaled_done, step + 1)
                            eng.matmul(out[:, c % 2, :], wout[:, uq, j, :], scaled[:, s % HR, :],
                                       start=(j == 0), stop=(j == J - 1)).then_inc(out_used, 1)

                run(eng, body)
                if b_out is not None:
                    eng.wait_ge(const_in, CONSTS)
                    for c in range(CH):
                        eng.wait_ge(summed, units * CH + c - 1)
                        eng.matmul(out[:, c % 2, :], bout[:, :], rows[:, c * BANK:(c + 1) * BANK],
                                   start=True, stop=True).then_inc(out_used, 1)

            @block.scalar
            def _(eng):
                def body(n, q, first, last):
                    for what, s, back in schedule(first, last):
                        if what != "hidden":
                            continue
                        j, step = s % J, n * steps + s
                        if s == 0:
                            eng.wait_ge(win_in[q], (n + 2 - q) * (INS // 2))
                        eng.wait_ge(hidden_full, step + 1)
                        if not (first and s < HR):
                            eng.wait_ge(scaled_done, step - HR + 1)
                        if b_in is not None:
                            eng.activation(acted[:, s % HR, :], hidden[:, s % HB, :], act,
                                           bias=bin_[:, q, j:j + 1]).then_inc(act_done, 1)
                        else:
                            eng.activation(acted[:, s % HR, :], hidden[:, s % HB, :], act).then_inc(act_done, 1)

                run(eng, body)

            @block.gpsimd
            def _(eng):
                def body(n, q, first, last):
                    for what, s, back in schedule(first, last):
                        if what != "hidden":
                            continue
                        step = n * steps + s
                        c = s // J
                        if s == 0:
                            eng.wait_ge(win_in[q], (n + 2 - q) * (INS // 2))
                        eng.wait_ge(upped if gated else act_done, step + 1)
                        if not (first and s < HR):
                            eng.wait_ge(out_used, step - HR + 1)
                        eng.tensor_tensor(scaled[:, s % HR, :], acted[:, s % HR, :],
                                          gate[:, q, c * BANK:(c + 1) * BANK], ALU.mult).then_inc(scaled_done, 1)

                run(eng, body)

            @block.vector
            def _(eng):
                def body(n, q, first, last):
                    for what, s, back in schedule(first, last):
                        u = n - 1 if back else n
                        step = u * steps + s
                        if what == "hidden" and gated:
                            eng.wait_ge(act_done, step + 1)
                            eng.tensor_tensor(acted[:, s % HR, :], acted[:, s % HR, :], upper[:, s % HB, :],
                                              ALU.mult).then_inc(upped, 1)
                        if what == "out" and s % J == J - 1:
                            c = s // J
                            eng.wait_ge(out_used, step + 1)
                            at = slice(c * BANK, (c + 1) * BANK)
                            if not first:
                                eng.wait_ge(summed, u * CH + c)
                            eng.tensor_tensor(res_t[:, at], res_t[:, at], out[:, c % 2, :], ALU.add).then_inc(summed, 1)

                run(eng, body)
                if b_out is not None:
                    for c in range(CH):
                        eng.wait_ge(out_used, units * steps + c + 1)
                        at = slice(c * BANK, (c + 1) * BANK)
                        eng.tensor_tensor(res_t[:, at], res_t[:, at], out[:, c % 2, :], ALU.add).then_inc(summed, 1)

        pl.close()


EXPERTS = 8
SMALL_EXPERTS = 64
SMALL = 64
CAPACITY = 2 * T // EXPERTS


def program(nc, d, out):
    gates = nc.dram_tensor("gates", (SMALL_EXPERTS + 2, T), F32, kind="Internal").ap()
    with ExitStack() as ctx:
        pl = Place(nc, ctx, "all")
        res_t = pl.sb("res_t", [P, T])
        xn_t = pl.sb("xn_t", [P, T])
        x_in = pl.sem("x_in")
        stored = pl.sem("stored")

        with nc.Block() as block:
            @block.sync
            def _(eng):
                eng.dma_start(res_t[:, :], d["x"]).then_inc(x_in, 16)
                eng.wait_ge(x_in, 16)

        layer_norm(nc, "n0", res_t, xn_t, d["avg"], d["bias0"])
        head_attention(nc, "a0", res_t, xn_t, d["w_qk0"], d["w_v0"], d["w_o0"], d["ident"], d["consts0"], None, None,
                       groups=8, heads=2, scale=64 ** -0.5, eps=1e-10)
        with nc.sbuf_tensor("xp_t", [P, T], F32) as xp_t:
            whole_attention(nc, "b0", res_t, xn_t, xp_t, d["w_b0"], d["bias_b0"], d["ident"])
            route(nc, "r0", xp_t, d["w_g0"], d["b_g0"], None, d["ident"], gates[0:EXPERTS, :], EXPERTS,
                  top=0, norm_eps=0.0, squash="softmax", extra=0, extra_value=0.0, capacity=0)
            experts(nc, "e0", res_t, xp_t, d["w1_0"], d["b1_0"], d["w2_0"], gates[0:EXPERTS, :], d["b2_0"],
                    units=EXPERTS, J=4, act=ACT.Relu, gated=False)

        layer_norm(nc, "n1", res_t, xn_t, d["avg"], None)
        head_attention(nc, "a1", res_t, xn_t, d["w_qk1"], d["w_v1"], d["w_o1"], d["ident"], d["consts1"], d["rope"], d["pick1"],
                       groups=4, heads=4, scale=1.0, eps=0.0)
        route(nc, "r1", xn_t, d["w_g1"], None, None, d["ident"], gates[0:EXPERTS + 1, :], EXPERTS,
              top=2, norm_eps=1e-9, squash="softmax", extra=1, extra_value=0.1, capacity=0)
        experts(nc, "e1", res_t, xn_t, d["w1_1"], d["b1_1"], d["w2_1"], gates[0:EXPERTS + 1, :], d["b2_1"],
                units=EXPERTS + 1, J=4, act=ACT.Silu, gated=False)

        layer_norm(nc, "n2", res_t, xn_t, d["avg"], d["bias2"])
        linear_attention(nc, "a2", res_t, xn_t, d["w_qkv2"], d["w_o2"], d["mask2"], eps=1e-6)
        route(nc, "r2", xn_t, d["w_g2"], None, d["tri"], d["ident"], gates[0:EXPERTS, :], EXPERTS,
              top=2, norm_eps=0.0, squash="softmax", extra=0, extra_value=0.0, capacity=CAPACITY)
        experts(nc, "e2", res_t, xn_t, d["w1_2"], d["b1_2"], d["w2_2"], gates[0:EXPERTS, :], d["b2_2"],
                units=EXPERTS, J=4, act=ACT.Relu, gated=False)

        layer_norm(nc, "n3", res_t, xn_t, d["avg"], None)
        recurrent_mixing(nc, "a3", res_t, xn_t, {n[:-1]: a for n, a in d.items() if n.endswith("3") and n != "bias3"})
        route(nc, "r3", xn_t, d["w_route"], None, None, d["ident"], gates, SMALL_EXPERTS,
              top=8, norm_eps=1e-9, squash="sigmoid", extra=2, extra_value=1.0, capacity=0)
        experts(nc, "e3", res_t, xn_t, d["w1_small"], None, d["w2_small"], gates, None,
                units=SMALL_EXPERTS // 2 + 1, J=1, act=ACT.Silu, gated=True)

        with nc.Block() as block:
            @block.sync
            def _(eng):
                eng.dma_start(out, res_t[:, :]).then_inc(stored, 16)
                eng.wait_ge(stored, 16)


def lay_out(a):
    def mixture(w1, b1, w2, b2, tag):
        e = w1.shape[0]
        return {f"w1_{tag}": w1.reshape(e, P, 4, P), f"b1_{tag}": b1.reshape(e, 4, P).transpose(0, 2, 1),
                f"w2_{tag}": w2.reshape(e, 4, P, P).transpose(0, 2, 1, 3), f"b2_{tag}": b2.reshape(e, P)}

    def with_shared(w, shared):
        return np.concatenate([w, shared[None]])

    p, j = np.arange(P)[:, None], np.arange(P)[None]

    w_qk0 = np.stack([a[f"L0_attn_W{n}"].reshape(8, 2, 64, P).transpose(0, 3, 1, 2) for n in "qk"], 3)
    w_qk0 = np.broadcast_to(w_qk0[:, :, :, :, None], (8, P, 2, 2, 2, 64)).reshape(8, P, 4, P)
    consts0 = np.zeros((P, 16), np.float32)
    consts0[:, 0:8] = p - 64 == j[:, 0:8]

    def lead(w):
        out = np.zeros((4, P, 4, 4, 8), w.dtype)
        out[:, :, :, 0:3] = w.reshape(4, 4, 8, P).transpose(0, 3, 1, 2)[:, :, :, None]
        return out.reshape(4, P, P)

    def even(w):
        return w.reshape(16, 8, P)[:, np.arange(8) // 2 * 2]
    w_qk1 = np.stack([lead(even(a["L1_attn_Wq"])), lead(even(a["L1_attn_Wk"]))], 2)
    w_o1 = np.zeros((4, 4, 32, P), np.float32)
    w_o1[:, :, 0:8] = a["L1_attn_Wo"].T.reshape(4, 4, 8, P)
    freqs = np.exp(np.arange(0, 8, 2, dtype=np.float32) * np.float32(-np.log(10000.0) / 8))
    angles = np.arange(N, dtype=np.float32)[None] * freqs[:, None]
    table = np.zeros((8, N), np.float32)
    table[0::2], table[1::2] = np.cos(angles), -np.sin(angles)
    rope = np.zeros((4, 4, 8, 2, N), np.float32)
    rope[:, 0:3, :, 0], rope[:, 0:3, :, 1] = table / np.float32(np.sqrt(8.0)), table
    part = p[:, 0] % 32 // 8
    consts1 = np.zeros((P, 16), np.float32)
    consts1[:, 0:8] = p % 32 - 24 == j[:, 0:8]
    consts1[:, 8], consts1[:, 9] = (part % 2 == 0) * 1.0 - (part == 1), part == 1
    consts1[:, 11], consts1[:, 12], consts1[:, 13] = (part <= 1) * 1.0 - (part == 2), part == 2, part == 3

    entry = np.arange(4 * P).reshape(4, P)
    key_of, value_of = entry // 8, entry // 32 * 8 + entry % 8
    cols3 = np.zeros((P, 20), np.float32)
    cols3[:, 0], cols3[:, 1:6] = a["L3_attn_mu_x"], a["L3_attn_x_bias"].T
    cols3[:, 6:10], cols3[:, 10:14] = a["L3_attn_b_w2"][key_of].T, a["L3_attn_u"].reshape(64)[key_of].T
    cols3[:, 14], cols3[:, 15] = a["L3_attn_gn_w"], a["L3_attn_gn_b"]
    x2 = a["L3_attn_W_x2"].transpose(1, 2, 0)

    def side_by_side(w, shared):
        w = np.concatenate([w, shared[None], np.zeros_like(shared)[None]])
        return w.reshape(33, 2, P, SMALL).transpose(0, 2, 1, 3).reshape(33, P, P)
    down = a["L3_ffn_shared_down_w"]

    return {
        "x": a["L0_attn_x"].reshape(T, P).T, "avg": np.full((P, P), 1.0 / P, np.float32),
        "ident": np.eye(P, dtype=np.float32), "tri": (p <= j).astype(np.float32),
        "consts0": consts0, "consts1": consts1, "pick1": (p == j // 32 * 32 + 8).astype(np.float32),
        "bias0": a["L0_attn_bo"].reshape(P, 1), "w_qk0": w_qk0,
        "w_v0": a["L0_attn_Wv"].reshape(8, P, P).transpose(0, 2, 1), "w_o0": a["L0_attn_Wo"].T.reshape(8, P, P),
        "w_b0": np.stack([a[f"L0_ffn_W{n}"] for n in "qkvo"], 1), "bias_b0": np.stack([a[f"L0_ffn_b{n}"] for n in "qkvo"], 1),
        "w_g0": a["L0_ffn_Wg"], "b_g0": a["L0_ffn_bg"].reshape(1, EXPERTS),
        **mixture(a["L0_ffn_W1"], a["L0_ffn_b1"], a["L0_ffn_W2"], a["L0_ffn_b2"], "0"),
        "w_qk1": w_qk1, "w_v1": a["L1_attn_Wv"].reshape(4, 32, P).transpose(0, 2, 1), "w_o1": w_o1.reshape(4, P, P), "rope": rope.reshape(P, 2, N), "w_g1": a["L1_ffn_Wg"],
        **mixture(with_shared(a["L1_ffn_W1"], a["L1_ffn_Ws1"]), with_shared(a["L1_ffn_b1"], a["L1_ffn_bs1"]),
                  with_shared(a["L1_ffn_W2"], a["L1_ffn_Ws2"]), with_shared(a["L1_ffn_b2"], a["L1_ffn_bs2"]), "1"),
        "bias2": a["L2_attn_bout"].reshape(P, 1),
        "w_qkv2": a["L2_attn_Wqkv"].reshape(P, 3, 8, P).transpose(2, 0, 1, 3).reshape(8, P, 3 * P),
        "w_o2": a["L2_attn_Wout"].reshape(8, P, P), "mask2": (p // 64 == j // 64).astype(np.float32),
        "w_g2": a["L2_ffn_gate_w"].T,
        **mixture(a["L2_ffn_fc1_w"].transpose(0, 2, 1), a["L2_ffn_fc1_b"], a["L2_ffn_fc2_w"], a["L2_ffn_fc2_b"], "2"),
        "cols3": cols3, "w_x13": a["L3_attn_W_x1"], "w_x23": x2[:4].reshape(P, P), "w_x2b3": x2[4],
        "w_w13": a["L3_attn_W_w1"], "w_w23": a["L3_attn_W_w2"][:, key_of], "w_r3": a["L3_attn_W_r"][:, key_of],
        "w_k3": a["L3_attn_W_k"][:, key_of], "w_v3": a["L3_attn_W_v"][:, value_of], "w_g3": a["L3_attn_W_g"],
        "w_o3": a["L3_attn_W_o"], "pick3": (p // 32 * 8 + p % 8 == j[:, :32]).astype(np.float32),
        "blocks3": (p // 8 == j // 8).astype(np.float32) / 8,
        "w_route": a["L3_ffn_router_w"],
        "w1_small": np.stack([side_by_side(a["L3_ffn_expert_gate_k"], a["L3_ffn_shared_gate_w"]),
                              side_by_side(a["L3_ffn_expert_up_k"], a["L3_ffn_shared_up_w"])], 2),
        "w2_small": np.concatenate([a["L3_ffn_expert_down_k"], down[None], np.zeros_like(down)[None]]).reshape(33, P, 1, P),
    }


def kernel(**inputs):
    import concourse.bacc as bacc
    from concourse.bass_utils import run_bass_kernel_spmd

    laid = lay_out({n: np.asarray(v) for n, v in inputs.items()})
    arrays = {f"in_{n}": np.ascontiguousarray(v) for n, v in laid.items()}
    nc = bacc.Bacc("TRN2", target_bir_lowering=False, num_devices=1)
    operands = {n: nc.dram_tensor(f"in_{n}", arrays[f"in_{n}"].shape, mybir.dt.from_np(arrays[f"in_{n}"].dtype), kind="ExternalInput").ap()
                for n in laid}
    out = nc.dram_tensor("out_t", (P, T), F32, kind="ExternalOutput").ap()
    program(nc, operands, out)
    result = run_bass_kernel_spmd(nc, [arrays], core_ids=[0]).results[0]["out_t"]
    return np.ascontiguousarray(result.T).reshape(B, N, P)
```

```python
from contextlib import ExitStack

import numpy as np
import concourse.bass as bass
from concourse import mybir

F32 = mybir.dt.float32
F16 = mybir.dt.float16
BF16 = mybir.dt.bfloat16
ALU = mybir.AluOpType
ACT = mybir.ActivationFunctionType
AX = mybir.AxisListType

P = 128
B, N = 4, 1024
T = B * N
BANK = 512
CH = T // BANK
NT = T // P


class Place:

    def __init__(self, nc, ctx, stage):
        self.nc, self.ctx, self.stage, self.sems = nc, ctx, stage, []

    def sb(self, name, shape, dt=F32):
        return self.ctx.enter_context(self.nc.sbuf_tensor(f"{self.stage}_{name}", shape, dt))

    def ps(self, name, shape, dt=F32):
        return self.ctx.enter_context(self.nc.psum_tensor(f"{self.stage}_{name}", shape, dt))

    def sem(self, name):
        self.sems.append(self.ctx.enter_context(self.nc.semaphore(f"{self.stage}_{name}")))
        return self.sems[-1]

    def close(self):
        with self.nc.Block() as block:
            @block.sync
            def _(eng):
                for s in self.sems:
                    eng.sem_clear(s)


class Steps:

    def __init__(self, sem, names):
        self.sem, self.names, self.place = sem, names, {n: i + 1 for i, n in enumerate(names)}
        assert len(self.place) == len(names)

    def wait(self, eng, name, rnd):
        if isinstance(rnd, int) and rnd < 0:
            return
        eng.wait_ge(self.sem, rnd * len(self.names) + self.place[name])


def layer_norm(nc, stage, res_t, xn_t, avg_d, ident_d, bias_d):
    LAG = 2
    with ExitStack() as ctx:
        pl = Place(nc, ctx, stage)
        avg = pl.sb("avg", [P, P])
        ident = pl.sb("ident", [P, P])
        ones = pl.sb("ones", [P, P])
        bias = pl.sb("bias", [P, 1])
        sq = pl.sb("sq", [P, 4, BANK])
        std = pl.sb("std", [P, NT])
        diag = pl.sb("diag", [P, 4, 4, P])
        mean = pl.ps("mean", [P, 4, BANK])
        var = pl.ps("var", [P, NT])
        rstd = pl.ps("rstd", [P, 2, BANK])
        const_in = pl.sem("const_in")
        filled = pl.sem("filled")
        mean_full = pl.sem("mean_full")
        centred = pl.sem("centred")
        squared = pl.sem("squared")
        var_full = pl.sem("var_full")
        eps_added = pl.sem("eps_added")
        rooted = pl.sem("rooted")
        inverted = pl.sem("inverted")
        spread = pl.sem("spread")
        rstd_full = pl.sem("rstd_full")
        done = pl.sem("done")
        CONSTS = 32 if bias_d is None else 48

        def chunk(c):
            return slice(c * BANK, (c + 1) * BANK)

        with nc.Block() as block:
            @block.sync
            def _(eng):
                eng.dma_start(avg[:, :], avg_d).then_inc(const_in, 16)
                eng.dma_start(ident[:, :], ident_d).then_inc(const_in, 16)
                if bias_d is not None:
                    eng.dma_start(bias[:, :], bias_d).then_inc(const_in, 16)
                eng.wait_ge(const_in, CONSTS)

            @block.tensor
            def _(eng):
                eng.wait_ge(const_in, CONSTS)
                for c in range(CH + LAG):
                    if c < CH:
                        if c >= 4:
                            eng.wait_ge(centred, c - 3)
                        eng.matmul(mean[:, c % 4, :], avg[:, :], res_t[:, chunk(c)], start=True, stop=True).then_inc(mean_full, 1)
                    if c >= LAG:
                        k = c - LAG
                        eng.wait_ge(squared, k + 1)
                        for t in range(4):
                            mm = eng.matmul(var[:, 4 * k + t:4 * k + t + 1], sq[:, k % 4, t * P:(t + 1) * P], avg[:, 0:1],
                                            start=True, stop=True)
                        mm.then_inc(var_full, 1)
                eng.wait_ge(filled, 1)
                for c in range(CH):
                    eng.wait_ge(spread, c + 1)
                    if c >= 2:
                        eng.wait_ge(done, c - 1)
                    eng.matmul(rstd[:, c % 2, :], ones[:, :], diag[:, c % 4, :, :].rearrange("p a b -> p (a b)"),
                               start=True, stop=True).then_inc(rstd_full, 1)

            @block.scalar
            def _(eng):
                for c in range(CH):
                    eng.wait_ge(centred, c + 1)
                    if c >= 4:
                        eng.wait_ge(var_full, c - 3)
                    eng.activation(sq[:, c % 4, :], xn_t[:, chunk(c)], ACT.Square).then_inc(squared, 1)
                eng.wait_ge(eps_added, 1)
                eng.activation(std[:, :], std[:, :], ACT.Sqrt).then_inc(rooted, 1)

            @block.vector
            def _(eng):
                eng.memset(ones[:, :], 1.0).then_inc(filled, 1)
                for c in range(CH):
                    eng.wait_ge(mean_full, c + 1)
                    eng.tensor_tensor(xn_t[:, chunk(c)], res_t[:, chunk(c)], mean[:, c % 4, :], ALU.subtract).then_inc(centred, 1)
                eng.wait_ge(var_full, CH)
                eng.tensor_scalar(std[:, :], var[:, :], 1e-5, None, ALU.add).then_inc(eps_added, 1)
                if bias_d is not None:
                    eng.wait_ge(const_in, CONSTS)
                    eng.wait_ge(centred, CH)
                    eng.tensor_scalar(res_t[:, :], res_t[:, :], bias[:, 0:1], None, ALU.add)
                eng.wait_ge(rooted, 1)
                eng.reciprocal(std[:, :], std[:, :]).then_inc(inverted, 1)
                for c in range(CH):
                    eng.wait_ge(rstd_full, c + 1)
                    eng.tensor_tensor(xn_t[:, chunk(c)], xn_t[:, chunk(c)], rstd[:, c % 2, :], ALU.mult).then_inc(done, 1)

            @block.gpsimd
            def _(eng):
                eng.wait_ge(const_in, CONSTS)
                eng.wait_ge(inverted, 1)
                for c in range(CH):
                    if c >= 4:
                        eng.wait_ge(rstd_full, c - 3)
                    eng.tensor_tensor(diag[:, c % 4, :, :], ident[:, :].unsqueeze(1).broadcast_to([P, 4, P]),
                                      std[:, 4 * c:4 * c + 4].unsqueeze(2).broadcast_to([P, 4, P]), ALU.mult).then_inc(spread, 1)

        pl.close()


def head_attention(nc, stage, res_t, xn_t, w_qk, w_v, w_out, ident_d, consts_d, rope_d, pick_d,
                   groups, heads, scale, eps):
    small = heads == 4
    rows = P // heads
    units = B * groups
    kts = N // P
    events = N // BANK * kts
    pairs = heads // 2
    SLOTS = 3 if small else 2
    STEPS = events * heads
    WHOLE = 4
    LAG = 2
    RING = 4
    projections = ["q0", "k0"] if small else ["q0", "k0", "q1", "k1"]
    maxima = [(h, qt) for h in range(heads) for qt in range(kts)]
    loads = ["v", "q0", "k0"] if small else ["q0", "k0", "v", "q1", "k1"]
    prep = loads + [("max", m) for m in range(len(maxima))] + ["shift"]
    PREP = len(prep)
    after = ["sums", "out"] if small else ["out"]
    BY_ACT = ("v", "sums", "out")
    CHUNKS = 4

    def count(state, by_act):
        state[:3] = [state[0] + 1, state[1] + by_act, state[2] + (not by_act)]
        state[3] = [state[3][1], ("act", state[1]) if by_act else ("dve", state[2])]

    def schedule(first, last):
        jobs = []
        if not last:
            jobs.append((1, "split"))
            start = 2 * LAG
            jobs += [(start + i, job) for i, job in enumerate(loads)]
            start += len(loads) + 2
            room = 2 * events - 4 - start
            jobs += [(start + m * room // (len(maxima) - 1), ("max", m)) for m in range(len(maxima))]
            jobs.append((2 * events - 3, "shift"))
        for k, at in ([] if first else [(1, 2 * LAG)]) + [(0, 2 * (kts + LAG))]:
            if small:
                jobs.append((at + 1, ("sums", k)))
            jobs += [(at + (2 if small else 1) + i, (f"divide{i}", k)) for i in range(CHUNKS)]
            jobs.append((at + CHUNKS + 3, ("out", k)))
        jobs.sort(key=lambda j: j[0])
        order, state = [], [0, 0, 0, [("dve", -1), ("dve", 0)]]

        def add(what, k, back):
            order.append((what, k, back, (*state[:3], state[3][0])))
            if not what.startswith("divide"):
                count(state, what in BY_ACT)

        for g in range(2 * (events + (LAG if last else 0))):
            e = g // 2
            if e < events:
                order.append((f"scores{g % 2}", e, 0, None))
            if e >= LAG:
                order.append((f"values{g % 2}", e - LAG, 0, None))
            elif not first:
                order.append((f"values{g % 2}", events + e - LAG, 1, None))
            for at, job in jobs:
                if at == g:
                    what, k = job if isinstance(job, tuple) else (job, 0)
                    if what == "split":
                        order.append((what, 0, 0, None))
                        continue
                    add(what, k, int(what[0] in "sdo" and what != "shift" and k == 1))
        if last:
            for what in (["sums"] if small else []) + [f"divide{i}" for i in range(CHUNKS)] + ["out"]:
                add(what, 1, 0)
        return order

    def prepare():
        order, state = [("split", 0, 0, None)], [0, 0, 0, [None, None]]
        for job in prep:
            what, k = job if isinstance(job, tuple) else (job, 0)
            order.append((what, k, 0, (*state[:3], state[3][0])))
            count(state, what in BY_ACT)
        return order

    def run(eng, body):
        short = len(after)

        def base(n):
            return (n * (PREP + 2 * short) + PREP - short, n * (1 + 2 * short) + 1 - short,
                    n * (PREP - 1) + PREP - 1, (PREP - short) % 2)
        assert PREP % 2 == 0
        body(-1, 1, (0, 0, 0, 0), prepare())
        body(0, 0, (PREP, 1, PREP - 1, 0), schedule(True, False))
        with eng.Fori(0, (units - 2) // 2) as i:
            body(2 * i + 1, 1, base(2 * i + 1), schedule(False, False))
            body(2 * i + 2, 0, base(2 * i + 2), schedule(False, False))
        body(units - 1, 1, base(units - 1), schedule(False, True))

    def known(n, below):
        return isinstance(n, int) and n < below

    with ExitStack() as ctx:
        pl = Place(nc, ctx, stage)
        QC = len(projections)
        VC = 32 if small else P
        x_high = pl.sb("x_high", [P, T], F16)
        x_low = pl.sb("x_low", [P, T], F16)
        xb_high = pl.sb("xb_high", [P, 2, N], F16)
        xb_low = pl.sb("xb_low", [P, 2, N], F16)
        w = pl.sb("w", [P, 2, QC * P + VC])
        w_high = pl.sb("w_high", [P, QC * P + VC], F16)
        w_low = pl.sb("w_low", [P, QC * P + VC], F16)
        wo = pl.sb("wo", [P, 2, P])
        ident = pl.sb("ident", [P, P])
        consts = pl.sb("consts", [P, 16])
        rowmask = consts[:, 0:kts]
        rope = pl.sb("rope", [P, 2, N]) if small else None
        pick = pl.sb("pick", [P, P]) if small else None
        whole = [pl.sb(f"whole_{c}", [P, N]) for c in "qk"] if small else None
        part = [pl.sb(f"part_{c}", [P, N], F16) for c in "qk"] if small else None
        bare = pl.sb("bare", [P, N], F16) if small else None
        spread = pl.sb("spread", [P, kts, P], F16) if small else None
        QH = 1 if small else 2
        qa = pl.sb("qa", [P, 2, QH, N], F16)
        ka = pl.sb("ka", [P, 2, QH, N], F16)
        qb = None if small else pl.sb("qb", [P, 2, 2, N], F16)
        kb = None if small else pl.sb("kb", [P, 2, 2, N], F16)
        if small:
            v = pl.sb("v", [P, 2, kts, heads, 32])
            prob = pl.sb("prob", [P, RING, heads, BANK])
        else:
            v_whole = pl.sb("v_whole", [P, kts, P])
            v_high = pl.sb("v_high", [P, 2, kts, heads, P], F16)
            v_low = pl.sb("v_low", [P, 2, kts, heads, P], F16)
            prob_whole = pl.sb("prob_whole", [P, WHOLE, BANK])
            prob_high = pl.sb("prob_high", [P, RING, heads, BANK], F16)
            prob_low = pl.sb("prob_low", [P, RING, heads, BANK], F16)
        row_max = pl.sb("row_max", [P, QH, P])
        raw = pl.sb("raw", [P, QH, BANK])
        denom = pl.sb("denom", [P, BANK])
        mixed = pl.sb("mixed", [P, 2, BANK])
        proj = pl.sb("proj", [P, 2, BANK])
        score = pl.ps("score", [P, SLOTS, BANK])
        side_banks = pl.ps("side", [P, 2, 2, BANK])
        o_ps = pl.ps("o_ps", [P, QH, BANK])

        def side_of(base, done):
            side = side_banks[:, (base[3] + done[0]) % 2, :, :]
            return side, side.rearrange("p a b -> p (a b)")

        const_in = pl.sem("const_in")
        unit_in = [pl.sem(f"unit_in{q}") for q in range(2)]
        wo_in = [pl.sem(f"wo_in{q}") for q in range(2)]
        x_high_done = pl.sem("x_high_done")
        x_split = pl.sem("x_split")
        w_high_done = pl.sem("w_high_done")
        w_split = pl.sem("w_split")
        filled = pl.sem("filled")
        side_full = pl.sem("side_full")
        act_freed = pl.sem("act_freed")
        dve_freed = pl.sem("dve_freed")
        high_done = pl.sem("high_done")
        weighed = pl.sem("weighed")
        stacked = pl.sem("stacked")
        score_full = pl.sem("score_full")
        exp_done = pl.sem("exp_done")
        low_done = pl.sem("low_done")
        v_split = pl.sem("v_split")
        pv_done = pl.sem("pv_done")
        first_done = pl.sem("first_done")
        raw_ready = pl.sem("raw_ready")
        denom_ready = pl.sem("denom_ready")
        inverted = pl.sem("inverted")
        spread_done = pl.sem("spread_done")
        out_ready = pl.sem("out_ready")
        added = pl.sem("added")
        CONSTS = 16 * (4 if small else 2)

        with nc.Block() as block:
            @block.sync
            def _(eng):
                eng.dma_start(ident[:, :], ident_d).then_inc(const_in, 16)
                eng.dma_start(consts[:, :], consts_d).then_inc(const_in, 16)
                if small:
                    eng.dma_start(rope[:, :, :], rope_d).then_inc(const_in, 16)
                    eng.dma_start(pick[:, :], pick_d).then_inc(const_in, 16)

                def load(q, b, g):
                    eng.dma_start(xb_high[:, q, :], x_high[:, bass.ds(b * N, N)]).then_inc(unit_in[q], 16)
                    eng.dma_start(xb_low[:, q, :], x_low[:, bass.ds(b * N, N)]).then_inc(unit_in[q], 16)
                    eng.dma_start(w[:, q, 0:QC * P].rearrange("p (c k) -> p c k", c=QC), w_qk[g, :, :, :]).then_inc(unit_in[q], 16)
                    eng.dma_start(w[:, q, QC * P:QC * P + VC], w_v[g, :, :]).then_inc(unit_in[q], 16)

                def load_out(q, g):
                    eng.dma_start(wo[:, q, :], w_out[g, :, :]).then_inc(wo_in[q], 16)

                eng.wait_ge(x_split, 1)
                for q in range(2):
                    load(q, 0, q)
                    load_out(q, q)
                eng.wait_ge(x_split, B)
                with eng.Fori(1, units // 2) as i:
                    for q in range(2):
                        n = 2 * i + q
                        g = 2 * (i % (groups // 2)) + q
                        eng.wait_ge(high_done, QC * (n - 1))
                        load(q, i // (groups // 2), g)
                        eng.wait_ge(added, 2 * (n - 1))
                        load_out(q, g)

            @block.tensor
            def _(eng):
                eng.wait_ge(const_in, CONSTS)
                eng.wait_ge(filled, 1)

                def body(n, q, base, order):
                    m, r = n + 1, 1 - q
                    for what, k, back, done in order:
                        if what.startswith("scores"):
                            second = what == "scores1"
                            if k == 0 and not second:
                                eng.wait_ge(dve_freed, base[2])
                            qs, keys = slice(k // kts * BANK, (k // kts + 1) * BANK), slice(k % kts * P, (k % kts + 1) * P)
                            for h in range(second * pairs, (second + 1) * pairs):
                                step = k * heads + h
                                before = step - SLOTS if step >= SLOTS else -1 - (STEPS - 1 - step) % SLOTS
                                if not known(n, 1) or step >= SLOTS:
                                    eng.wait_ge(exp_done, n * STEPS + before + 1)
                                dst = score[:, step % SLOTS, :]
                                if small:
                                    at = slice(h * 32, (h + 1) * 32)
                                    mm = eng.matmul(dst, ka[at, q, 0, keys], qa[at, q, 0, qs], start=True, stop=True)
                                else:
                                    eng.matmul(dst, ka[:, q, h, keys], qa[:, q, h, qs], start=True, stop=False)
                                    mm = eng.matmul(dst, kb[:, q, h, keys], qb[:, q, h, qs], start=False, stop=True)
                                mm.then_inc(score_full, 1)
                        elif what in ("values0", "values1"):
                            u, uq = (n - 1, 1 - q) if back else (n, q)
                            half, second = 2 * u + k // kts, what == "values1"
                            if small and not second:
                                continue
                            if small or not second:
                                if not small and k == 0:
                                    eng.wait_ge(v_split, u + 1)
                                eng.wait_ge(exp_done if small else low_done, u * STEPS + (k + 1) * heads)
                            if k % kts == 0 and not known(half, 1):
                                eng.wait_ge(raw_ready, half if small else 2 * half - 1 + second)
                            first_key, last_key = k % kts == 0, k % kts == kts - 1
                            if small:
                                for h in range(heads):
                                    mm = eng.matmul(o_ps[32 * h:32 * h + 32, 0, :], v[:, uq, k % kts, h, :], prob[:, k % RING, h, :],
                                                    start=first_key, stop=last_key)
                            else:
                                h, at = int(second), k % RING
                                eng.matmul(o_ps[:, h, :], v_high[:, uq, k % kts, h, :], prob_high[:, at, h, :], start=first_key, stop=False)
                                eng.matmul(o_ps[:, h, :], v_high[:, uq, k % kts, h, :], prob_low[:, at, h, :], start=False, stop=False)
                                mm = eng.matmul(o_ps[:, h, :], v_low[:, uq, k % kts, h, :], prob_high[:, at, h, :], start=False, stop=last_key)
                            if second:
                                mm.then_inc(pv_done, 1)
                            elif last_key:
                                mm.then_inc(first_done, 1)
                        elif not what.startswith("divide") and what != "split":
                            side, side_flat = side_of(base, done)
                            if done[3]:
                                by, nth = done[3]
                                eng.wait_ge(act_freed if by == "act" else dve_freed, base[1 if by == "act" else 2] + nth)
                            if what == loads[0]:
                                eng.wait_ge(unit_in[r], 32 * (m + 2 - r))
                                eng.wait_ge(w_split, m + 1)
                            if what == "v":
                                cols = slice(QC * P, QC * P + VC)
                                for kt in range(kts):
                                    dst, at = side_flat[:, kt * VC:(kt + 1) * VC], slice(kt * P, (kt + 1) * P)
                                    eng.matmul(dst, xb_high[:, r, at], w_high[:, cols], start=True, stop=False)
                                    eng.matmul(dst, xb_high[:, r, at], w_low[:, cols], start=False, stop=False)
                                    mm = eng.matmul(dst, xb_low[:, r, at], w_high[:, cols], start=False, stop=True)
                            elif what in projections:
                                cols = slice(projections.index(what) * P, (projections.index(what) + 1) * P)
                                for c in range(2):
                                    at = slice(c * BANK, (c + 1) * BANK)
                                    eng.matmul(side[:, c, :], w_high[:, cols], xb_high[:, r, at], start=True, stop=False)
                                    eng.matmul(side[:, c, :], w_high[:, cols], xb_low[:, r, at], start=False, stop=False)
                                    mm = eng.matmul(side[:, c, :], w_low[:, cols], xb_high[:, r, at], start=False, stop=True)
                            elif what == "max":
                                h, qt = maxima[k]
                                if small and k == 0:
                                    eng.wait_ge(stacked, 2 * m + 2)
                                elif k == 0:
                                    eng.wait_ge(dve_freed, base[2] + done[2])
                                for c in range(2):
                                    at, qq = (slice(h * 32, h * 32 + 32), bare[:, qt * P:(qt + 1) * P]) if small \
                                        else (slice(0, P), qa[:, r, h, qt * P:(qt + 1) * P])
                                    mm = eng.matmul(side[:, c, :], qq[at, :], ka[at, r, 0 if small else h, c * BANK:(c + 1) * BANK],
                                                    start=True, stop=True)
                            elif what == "shift":
                                eng.wait_ge(dve_freed, base[2] + done[2])
                                for h in range(QH):
                                    mm = eng.transpose(side[:, h, 0:P], row_max[:, h, :], ident[:, :])
                            elif what == "sums":
                                u = n - 1 if back else n
                                eng.wait_ge(raw_ready, 2 * u + k + 1)
                                mm = eng.matmul(side[:, 0, :], pick[:, :], raw[:, 0, :], start=True, stop=True)
                            elif what == "out":
                                u, uq = (n - 1, 1 - q) if back else (n, q)
                                eng.wait_ge(wo_in[uq], 8 * (u + 2 - uq))
                                eng.wait_ge(out_ready, CHUNKS * (2 * u + k + 1))
                                mm = eng.matmul(side[:, 0, :], wo[:, uq, :], mixed[:, k, :], start=True, stop=True)
                            mm.then_inc(side_full, 1)

                run(eng, body)

            @block.scalar
            def _(eng):
                for b in range(B):
                    at = slice(b * N, (b + 1) * N)
                    eng.activation(x_high[:, at], xn_t[:, at], ACT.Copy).then_inc(x_high_done, 1)
                eng.wait_ge(filled, 1)
                eng.wait_ge(const_in, CONSTS)

                def body(n, q, base, order):
                    m, r = n + 1, 1 - q
                    for what, k, back, done in order:
                        if done:
                            side, side_flat = side_of(base, done)
                        if what == "split":
                            eng.wait_ge(unit_in[r], 32 * (m + 2 - r))
                            if not known(m, 1):
                                eng.wait_ge(dve_freed, base[2])
                            eng.activation(w_high[:, :], w[:, r, :], ACT.Copy).then_inc(w_high_done, 1)
                        if what in projections:
                            c = projections.index(what)
                            if small:
                                eng.wait_ge(dve_freed, base[2] + done[2] + 1)
                                if not known(m, 1):
                                    eng.wait_ge(stacked, 2 * m - 1 + c)
                                eng.activation(part[c][:, :], whole[c][:, :], ACT.Copy).then_inc(high_done, 1)
                                eng.wait_ge(high_done, QC * m + c + 1)
                                eng.activation(whole[c][:, :], whole[c][:, :], ACT.Identity, scale=consts[:, 9 + 3 * c:10 + 3 * c],
                                               bias=consts[:, 10 + 3 * c:11 + 3 * c]).then_inc(weighed, 1)
                            else:
                                eng.wait_ge(side_full, base[0] + done[0] + 1)
                                if not known(n, 1):
                                    eng.wait_ge(score_full, STEPS * n)
                                dst = (qa if c % 2 == 0 else ka)[:, r, c // 2, :]
                                eng.activation(dst, side_flat, ACT.Copy).then_inc(high_done, 1)
                        elif what.startswith("scores"):
                            second = what == "scores1"
                            for h in range(second * pairs, (second + 1) * pairs):
                                step = k * heads + h
                                eng.wait_ge(score_full, n * STEPS + step + 1)
                                if h == 0 and not (known(n, 1) and k < RING):
                                    eng.wait_ge(pv_done, n * events + k - RING + 1)
                                src = score[:, step % SLOTS, :]
                                if small:
                                    eng.activation(prob[:, k % RING, h, :], src, ACT.Exp, scale=scale).then_inc(exp_done, 1)
                                else:
                                    if not (known(n, 1) and step < WHOLE):
                                        eng.wait_ge(low_done, n * STEPS + step - WHOLE + 1)
                                    eng.activation(prob_whole[:, step % WHOLE, :], src, ACT.Exp, scale=scale)
                                    eng.activation(prob_high[:, k % RING, h, :], src, ACT.Exp, scale=scale).then_inc(exp_done, 1)
                        elif what == "values0" and k % kts == kts - 1 and not small:
                            half = 2 * (n - 1 if back else n) + k // kts
                            eng.wait_ge(first_done, half + 1)
                            if not known(half, 1):
                                eng.wait_ge(out_ready, CHUNKS * half)
                            eng.activation(raw[:, 0, :], o_ps[:, 0, :], ACT.Copy).then_inc(raw_ready, 1)
                        elif what == "values1" and k % kts == kts - 1:
                            half = 2 * (n - 1 if back else n) + k // kts
                            eng.wait_ge(pv_done, kts * half + kts)
                            if not known(half, 1):
                                eng.wait_ge(out_ready, CHUNKS * half)
                            eng.activation(raw[:, QH - 1, :], o_ps[:, QH - 1, :], ACT.Copy).then_inc(raw_ready, 1)
                            if not small:
                                eng.wait_ge(raw_ready, 2 * half + 2)
                                eng.activation(denom[0:64, :], raw[64:128, 0, :], ACT.Copy, bias=eps)
                                eng.activation(denom[64:128, :], raw[0:64, 1, :], ACT.Copy, bias=eps).then_inc(denom_ready, 1)
                        elif what in BY_ACT:
                            eng.wait_ge(side_full, base[0] + done[0] + 1)
                            if what == "v":
                                if not known(n, 1):
                                    eng.wait_ge(pv_done, events * n)
                                if small:
                                    src = side_flat[:, 0:kts * 32].rearrange("p (a b c) -> p a b c", a=kts, b=4)
                                    op = eng.activation(v[:, r, :, :, 0:8], src, ACT.Copy)
                                else:
                                    src = side_flat.rearrange("p (a b) -> p a b", a=kts)
                                    if not known(m, 1):
                                        eng.wait_ge(v_split, m)
                                    eng.activation(v_whole[:, :, :], src, ACT.Copy)
                                    eng.activation(v_high[:, r, :, 0, 0:64], src[:, :, 0:64], ACT.Copy)
                                    op = eng.activation(v_high[:, r, :, 1, 64:128], src[:, :, 64:128], ACT.Copy)
                            elif what == "sums":
                                half = 2 * (n - 1 if back else n) + k
                                if not known(half, 1):
                                    eng.wait_ge(out_ready, CHUNKS * half)
                                op = eng.activation(denom[:, :], side[:, 0, :], ACT.Copy)
                            elif what == "out":
                                half = 2 * (n - 1 if back else n) + k
                                if not known(half, 2):
                                    eng.wait_ge(added, half - 1)
                                op = eng.activation(proj[:, k, :], side[:, 0, :], ACT.Copy)
                            op.then_inc(act_freed, 1)

                run(eng, body)

            @block.vector
            def _(eng):
                for b in range(B):
                    at = slice(b * N, (b + 1) * N)
                    eng.wait_ge(x_high_done, b + 1)
                    eng.tensor_tensor(x_low[:, at], xn_t[:, at], x_high[:, at], ALU.subtract).then_inc(x_split, 1)
                eng.memset(row_max[:, :, :], 0.0)
                if not small:
                    eng.memset(kb[64:128, :, :, :], 1.0)
                    eng.memset(v_low[:, :, :, :, :], 0.0)
                eng.memset((v if small else v_high)[:, :, :, :, :], 1.0).then_inc(filled, 1)
                eng.wait_ge(filled, 1)
                eng.wait_ge(const_in, CONSTS)

                def body(n, q, base, order):
                    m, r = n + 1, 1 - q
                    for what, k, back, done in order:
                        if what[:6] in ("scores", "values", "split") or what in BY_ACT:
                            continue
                        side, side_flat = side_of(base, done)
                        if what.startswith("divide"):
                            half, i = 2 * (n - 1 if back else n) + k, int(what[-1])
                            at = slice(i * BANK // CHUNKS, (i + 1) * BANK // CHUNKS)
                            if i == 0:
                                if small:
                                    eng.wait_ge(act_freed, base[1] + done[1])
                                else:
                                    eng.wait_ge(denom_ready, half + 1)
                            eng.reciprocal(denom[:, at], denom[:, at]).then_inc(inverted, 1)
                            if i == 0 and not known(half, 2):
                                eng.wait_ge(added, half - 1)
                            eng.wait_ge(inverted, CHUNKS * half + i + 1)
                            for h in range(QH):
                                own = slice(0, P) if small else slice(64 * h, 64 * h + 64)
                                op = eng.tensor_tensor(mixed[own, k, at], raw[own, h, at], denom[own, at], ALU.mult)
                            op.then_inc(out_ready, 1)
                            continue
                        eng.wait_ge(side_full, base[0] + done[0] + 1)
                        if what in projections and small:
                            c = projections.index(what)
                            if not known(m, 1):
                                eng.wait_ge(stacked, 2 * m - 1 + c)
                            op = eng.tensor_tensor(whole[c][:, :], side_flat, rope[:, c, :], ALU.mult)
                        elif what in projections:
                            c = projections.index(what)
                            h = c // 2
                            eng.wait_ge(high_done, QC * m + c + 1)
                            if c % 2 == 0:
                                eng.tensor_copy(qb[0:64, r, h, :], qa[0:64, r, h, :])
                                op = eng.tensor_tensor(qa[64:128, r, h, :], side_flat[64:128, :], qa[64:128, r, h, :], ALU.subtract)
                            else:
                                op = eng.tensor_tensor(kb[0:64, r, h, :], side_flat[0:64, :], ka[0:64, r, h, :], ALU.subtract)
                        elif what == "max":
                            h, qt = maxima[k]
                            col = 32 * h + 24 + qt if small else 64 + qt
                            op = eng.tensor_reduce(row_max[:, 0 if small else h, col:col + 1], side_flat, AX.X, ALU.max)
                        elif what == "shift":
                            if small:
                                mask = rowmask.unsqueeze(2).broadcast_to([P, kts, P])
                                eng.scalar_tensor_tensor(out=spread[:, :, :], in0=side[:, 0:1, 0:P].broadcast_to([P, kts, P]), scalar=-1.0,
                                                         in1=mask, op0=ALU.mult, op1=ALU.mult).then_inc(spread_done, 1)
                                eng.wait_ge(spread_done, m + 1)
                                if not known(n, 1):
                                    eng.wait_ge(score_full, STEPS * n)
                                op = eng.tensor_tensor(qa[:, r, 0, :], bare[:, :], spread[:, :, :].rearrange("p a b -> p (a b)"), ALU.add)
                            else:
                                mask = rowmask[64:128, :].unsqueeze(2).broadcast_to([64, kts, P])
                                for h in range(2):
                                    op = eng.scalar_tensor_tensor(
                                        out=qb[64:128, r, h, :].rearrange("p (a b) -> p a b", a=kts),
                                        in0=side[64:128, h:h + 1, 0:P].broadcast_to([64, kts, P]), scalar=-1.0,
                                        in1=mask, op0=ALU.mult, op1=ALU.mult)
                        op.then_inc(dve_freed, 1)
                        if what in projections and small:
                            c = projections.index(what)
                            eng.wait_ge(weighed, QC * m + c + 1)
                            if c == 1 and not known(n, 1):
                                eng.wait_ge(score_full, STEPS * n)
                            dst = ka[:, r, 0, :] if c else bare[:, :]
                            eng.scalar_tensor_tensor(out=dst, in0=part[c][:, :], scalar=consts[:, 8 + 3 * c:9 + 3 * c],
                                                     in1=whole[c][:, :], op0=ALU.mult, op1=ALU.add).then_inc(stacked, 1)

                run(eng, body)

            @block.gpsimd
            def _(eng):
                eng.wait_ge(filled, 1)

                def body(n, q, base, order):
                    m, r = n + 1, 1 - q
                    for what, k, back, done in order:
                        if what.startswith("scores") and not small:
                            h = int(what == "scores1")
                            step = k * heads + h
                            eng.wait_ge(exp_done, n * STEPS + step + 1)
                            eng.tensor_tensor(prob_low[:, k % RING, h, :], prob_whole[:, step % WHOLE, :],
                                              prob_high[:, k % RING, h, :], ALU.subtract).then_inc(low_done, 1)
                        elif what == "split":
                            eng.wait_ge(w_high_done, m + 1)
                            eng.tensor_tensor(w_low[:, :], w[:, r, :], w_high[:, :], ALU.subtract).then_inc(w_split, 1)
                        elif what == "v" and not small:
                            eng.wait_ge(act_freed, base[1] + done[1] + 1)
                            for h in range(2):
                                own = slice(64 * h, 64 * h + 64)
                                op = eng.tensor_tensor(v_low[:, r, :, h, own], v_whole[:, :, own], v_high[:, r, :, h, own], ALU.subtract)
                            op.then_inc(v_split, 1)
                        elif what == "out":
                            u = n - 1 if back else n
                            half = 2 * u + k
                            at = bass.ds((u // groups) * N + k * BANK, BANK)
                            eng.wait_ge(act_freed, base[1] + done[1] + 1)
                            if not known(half, 1):
                                eng.wait_ge(added, half)
                            eng.tensor_tensor(res_t[:, at], res_t[:, at], proj[:, k, :], ALU.add).then_inc(added, 1)

                run(eng, body)

        pl.close()


def whole_attention(nc, stage, res_t, xn_t, xp_t, w_d, bias_d, ident_d):
    qts = N // P
    scale = float(P) ** -0.5
    ORDER = [(what, t) for s in range(qts + 3) for what, t in (("scores", s), ("turn", s - 1), ("values", s - 2), ("proj", s - 3))
             if 0 <= t < qts and (what != "proj" or t % 4 == 3)]

    with ExitStack() as ctx:
        pl = Place(nc, ctx, stage)
        w = pl.sb("w", [P, 4, P])
        bias = pl.sb("bias", [P, 4])
        ident = pl.sb("ident", [P, P])
        xb = pl.sb("xb", [P, N])
        q = pl.sb("q", [P, N])
        k = pl.sb("k", [P, N])
        v = pl.sb("v", [P, qts, P])
        prob = pl.sb("prob", [P, 2, N])
        top = pl.sb("top", [P, 2])
        total = pl.sb("total", [P, 2])
        prob_t = pl.sb("prob_t", [P, 2, N])
        mixed = pl.sb("mixed", [P, 2, BANK])
        score = pl.ps("score", [P, 2, N])
        turned = pl.ps("turned", [P, N])
        mix = pl.ps("mix", [P, BANK])
        proj = pl.ps("proj", [P, BANK])
        const_in = pl.sem("const_in")
        x_in = pl.sem("x_in")
        projected = pl.sem("projected")
        q_ready = pl.sem("q_ready")
        kv_ready = pl.sem("kv_ready")
        score_full = pl.sem("score_full")
        maxed = pl.sem("maxed")
        negated = pl.sem("negated")
        exp_done = pl.sem("exp_done")
        inverted = pl.sem("inverted")
        prob_ready = pl.sem("prob_ready")
        turned_full = pl.sem("turned_full")
        turned_read = pl.sem("turned_read")
        mixed_tile = pl.sem("mixed_tile")
        mixed_half = pl.sem("mixed_half")
        proj_full = pl.sem("proj_full")
        xp_done = pl.sem("xp_done")
        res_done = pl.sem("res_done")

        def run(eng, body):
            body(0, True)
            with eng.Fori(1, B) as b:
                body(b, False)

        with nc.Block() as block:
            @block.sync
            def _(eng):
                eng.dma_start(w[:, :, :], w_d).then_inc(const_in, 16)
                eng.dma_start(bias[:, :], bias_d).then_inc(const_in, 16)
                eng.dma_start(ident[:, :], ident_d).then_inc(const_in, 16)
                eng.dma_start(xb[:, :], xn_t[:, 0:N]).then_inc(x_in, 16)
                with eng.Fori(1, B) as b:
                    eng.wait_ge(projected, 3 * b)
                    eng.dma_start(xb[:, :], xn_t[:, bass.ds(b * N, N)]).then_inc(x_in, 16)

            @block.tensor
            def _(eng):
                eng.wait_ge(const_in, 48)

                def body(b, first):
                    eng.wait_ge(x_in, 16 * b + 16)
                    if not first:
                        eng.wait_ge(exp_done, qts * b)
                        eng.wait_ge(turned_read, qts * b)
                    for c, dst in ((0, score[:, 0, :]), (1, score[:, 1, :])):
                        for h in range(2):
                            mm = eng.matmul(dst[:, h * BANK:(h + 1) * BANK], w[:, c, :], xb[:, h * BANK:(h + 1) * BANK],
                                            start=True, stop=True)
                        mm.then_inc(projected, 1)
                    for t in range(qts):
                        mm = eng.matmul(turned[:, t * P:(t + 1) * P], xb[:, t * P:(t + 1) * P], w[:, 2, :],
                                        start=True, stop=True)
                    mm.then_inc(projected, 1)
                    eng.wait_ge(q_ready, b + 1)
                    eng.wait_ge(kv_ready, 2 * b + 2)
                    for what, t in ORDER:
                        n = qts * b + t
                        if what == "scores":
                            if not (first and t < 2):
                                eng.wait_ge(exp_done, n - 1)
                            for h in range(2):
                                mm = eng.matmul(score[:, t % 2, h * BANK:(h + 1) * BANK], q[:, t * P:(t + 1) * P],
                                                k[:, h * BANK:(h + 1) * BANK], start=True, stop=True)
                            mm.then_inc(score_full, 1)
                            continue
                        if what == "turn":
                            eng.wait_ge(prob_ready, n + 1)
                            if not (first and t == 0):
                                eng.wait_ge(turned_read, n)
                            for kt in range(qts):
                                mm = eng.transpose(turned[:, kt * P:(kt + 1) * P], prob[:, t % 2, kt * P:(kt + 1) * P], ident[:, :])
                            mm.then_inc(turned_full, 1)
                        elif what == "values":
                            eng.wait_ge(turned_read, n + 1)
                            if t % 4 == 0 and not (first and t == 0):
                                eng.wait_ge(mixed_half, 2 * b + t // 4)
                            for kt in range(qts):
                                mm = eng.matmul(mix[:, t % 4 * P:(t % 4 + 1) * P], v[:, kt, :], prob_t[:, t % 2, kt * P:(kt + 1) * P],
                                                start=(kt == 0), stop=(kt == qts - 1))
                            mm.then_inc(mixed_tile, 1)
                        elif what == "proj":
                            half = 2 * b + t // 4
                            eng.wait_ge(mixed_half, half + 1)
                            if not (first and t == 3):
                                eng.wait_ge(xp_done, half)
                            eng.matmul(proj[:, :], w[:, 3, :], mixed[:, t // 4, :], start=True, stop=True).then_inc(proj_full, 1)

                run(eng, body)

            @block.scalar
            def _(eng):
                eng.wait_ge(const_in, 48)

                def body(b, first):
                    eng.wait_ge(projected, 3 * b + 2)
                    eng.activation(k[:, :], score[:, 1, :], ACT.Identity, bias=bias[:, 1:2]).then_inc(kv_ready, 1)
                    eng.wait_ge(projected, 3 * b + 3)
                    eng.activation(v[:, :, :].rearrange("p a b -> p (a b)"), turned[:, :], ACT.Copy).then_inc(kv_ready, 1)
                    for what, t in ORDER:
                        n = qts * b + t
                        if what == "scores":
                            eng.wait_ge(negated, n + 1)
                            if not (first and t < 2):
                                eng.wait_ge(turned_full, n - 1)
                            eng.activation(prob[:, t % 2, :], score[:, t % 2, :], ACT.Exp, bias=top[:, t % 2:t % 2 + 1],
                                           accum_out=total[:, t % 2:t % 2 + 1]).then_inc(exp_done, 1)
                        elif what == "turn":
                            eng.wait_ge(turned_full, n + 1)
                            if not (first and t < 2):
                                eng.wait_ge(mixed_tile, n - 1)
                            eng.activation(prob_t[:, t % 2, :], turned[:, :], ACT.Copy).then_inc(turned_read, 1)

                run(eng, body)

            @block.vector
            def _(eng):
                eng.wait_ge(const_in, 48)

                def body(b, first):
                    eng.wait_ge(projected, 3 * b + 1)
                    eng.tensor_scalar(q[:, :], score[:, 0, :], bias[:, 0:1], scale, ALU.add, ALU.mult).then_inc(q_ready, 1)
                    for what, t in ORDER:
                        n = qts * b + t
                        if what == "scores":
                            eng.wait_ge(score_full, n + 1)
                            if not (first and t < 2):
                                eng.wait_ge(exp_done, n - 1)
                            eng.tensor_reduce(top[:, t % 2:t % 2 + 1], score[:, t % 2, :], AX.X, ALU.max).then_inc(maxed, 1)
                            eng.wait_ge(maxed, n + 1)
                            eng.tensor_scalar(top[:, t % 2:t % 2 + 1], top[:, t % 2:t % 2 + 1], -1.0, None, ALU.mult).then_inc(negated, 1)
                            continue
                        half = 2 * b + t // 4
                        if what == "turn":
                            eng.wait_ge(exp_done, n + 1)
                            eng.reciprocal(total[:, t % 2:t % 2 + 1], total[:, t % 2:t % 2 + 1]).then_inc(inverted, 1)
                            eng.wait_ge(inverted, n + 1)
                            eng.tensor_scalar(prob[:, t % 2, :], prob[:, t % 2, :], total[:, t % 2:t % 2 + 1], None, ALU.mult).then_inc(prob_ready, 1)
                        elif what == "values" and t % 4 == 3:
                            eng.wait_ge(mixed_tile, n + 1)
                            if not (first and t < 8):
                                eng.wait_ge(proj_full, half - 1)
                            eng.tensor_scalar(mixed[:, t // 4, :], mix[:, :], bias[:, 2:3], None, ALU.add).then_inc(mixed_half, 1)
                        elif what == "proj":
                            at = bass.ds(b * N + t // 4 * BANK, BANK)
                            eng.wait_ge(proj_full, half + 1)
                            eng.scalar_tensor_tensor(out=xp_t[:, at], in0=proj[:, :], scalar=bias[:, 3:4], in1=xn_t[:, at],
                                                     op0=ALU.add, op1=ALU.add).then_inc(xp_done, 1)
                            eng.wait_ge(xp_done, half + 1)
                            eng.tensor_tensor(res_t[:, at], res_t[:, at], xp_t[:, at], ALU.add).then_inc(res_done, 1)

                run(eng, body)

        pl.close()


def linear_attention(nc, stage, res_t, xn_t, w_d, w_out_d, mask_d, ident_d, eps):
    pairs = 8
    units = B * pairs
    tiles = N // P
    W = P + 2

    PREPARE = [("kv", i) for i in range(4)] + [("q", 0), ("state", 0)]

    def schedule(last):
        order = [("mix", 0), ("kv", 0), ("q", 0), ("turn", 0), ("kv", 1), ("mix", 1), ("out", 0), ("kv", 2), ("kv", 3),
                 ("turn", 1), ("out", 1), ("state", 0)]
        return [(what, i) for what, i in order if not (last and what in ("kv", "q", "state"))]

    def run(eng, body):
        body(-1, 1, PREPARE)
        body(0, 0, schedule(False))
        with eng.Fori(0, (units - 2) // 2) as i:
            body(2 * i + 1, 1, schedule(False))
            body(2 * i + 2, 0, schedule(False))
        body(units - 1, 1, schedule(True))

    with ExitStack() as ctx:
        pl = Place(nc, ctx, stage)
        xb = pl.sb("xb", [P, 2, N])
        w = pl.sb("w", [P, 2, 3 * P])
        wo = pl.sb("wo", [P, 2, P])
        mask = pl.sb("mask", [P, P])
        expk = pl.sb("expk", [P, 2, 2, P])
        relk = pl.sb("relk", [P, 2, 2, P])
        expq = pl.sb("expq", [P, N])
        relq = pl.sb("relq", [P, N])
        q_t = pl.sb("q_t", [P, 2, N])
        k_s = pl.sb("k_s", [P, tiles, P])
        v_s = pl.sb("v_s", [P, tiles, W])
        kv_blk = pl.sb("kv_blk", [P, 2, P])
        sum_blk = pl.sb("sum_blk", [P, 2, 2])
        ident = pl.sb("ident", [P, P])
        denom = pl.sb("denom", [P, 4, 2])
        tokens = pl.sb("tokens", [P, 4, 2, 64])
        mixed = pl.sb("mixed", [P, 2, BANK])
        q_ps = pl.ps("q_ps", [P, N])
        kv_ps = pl.ps("kv_ps", [P, 2, 2, 2, P])
        state_den = pl.ps("state_den", [P, BANK])
        state = state_den[:, 0:W]
        den = state_den[:, 256:264].rearrange("p (a b) -> p a b", a=4)
        num = pl.ps("num", [P, 4, P])
        turned = pl.ps("turned", [P, BANK])
        out = pl.ps("out", [P, BANK])
        const_in = pl.sem("const_in")
        unit_in = [pl.sem(f"unit_in{r}") for r in range(2)]
        filled = pl.sem("filled")
        kv_full = pl.sem("kv_full")
        kv_read = pl.sem("kv_read")
        k_ready = pl.sem("k_ready")
        q_full = pl.sem("q_full")
        q_read = pl.sem("q_read")
        q_ready = pl.sem("q_ready")
        state_full = pl.sem("state_full")
        state_ready = pl.sem("state_ready")
        mix_full = pl.sem("mix_full")
        norm = pl.sem("norm")
        divided = pl.sem("divided")
        turned_full = pl.sem("turned_full")
        mixed_ready = pl.sem("mixed_ready")
        out_full = pl.sem("out_full")
        added = pl.sem("added")

        with nc.Block() as block:
            @block.sync
            def _(eng):
                eng.dma_start(mask[:, :], mask_d).then_inc(const_in, 16)
                eng.dma_start(ident[:, :], ident_d).then_inc(const_in, 16)

                def load(r, b, g):
                    eng.dma_start(xb[:, r, :], xn_t[:, bass.ds(b * N, N)]).then_inc(unit_in[r], 16)
                    eng.dma_start(w[:, r, :], w_d[g, :, :]).then_inc(unit_in[r], 16)
                    eng.dma_start(wo[:, r, :], w_out_d[g, :, :]).then_inc(unit_in[r], 16)

                for r in range(2):
                    load(r, 0, r)
                with eng.Fori(1, units // 2) as i:
                    for r in range(2):
                        eng.wait_ge(out_full, 2 * (2 * i + r - 1))
                        load(r, i // (pairs // 2), 2 * (i % (pairs // 2)) + r)

            @block.tensor
            def _(eng):
                eng.wait_ge(const_in, 32)
                eng.wait_ge(filled, 1)

                def body(n, q, order):
                    m, r = n + 1, 1 - q
                    for what, i in order:
                        if what == "kv":
                            if i == 0:
                                eng.wait_ge(unit_in[r], 24 * (m + 2 - r))
                            if not (isinstance(m, int) and m == 0 and i < 2):
                                eng.wait_ge(kv_read, 4 * m + i - 1)
                            for t in range(2):
                                tile = 2 * i + t
                                mm = eng.matmul(kv_ps[:, i % 2, t, :, :].rearrange("p a b -> p (a b)"),
                                                xb[:, r, tile * P:(tile + 1) * P], w[:, r, P:3 * P], start=True, stop=True)
                            mm.then_inc(kv_full, 1)
                        elif what == "q":
                            if not (isinstance(m, int) and m == 0):
                                eng.wait_ge(q_read, m)
                            for h in range(2):
                                mm = eng.matmul(q_ps[:, h * BANK:(h + 1) * BANK], w[:, r, 0:P],
                                                xb[:, r, h * BANK:(h + 1) * BANK], start=True, stop=True)
                            mm.then_inc(q_full, 1)
                        elif what == "state":
                            eng.wait_ge(k_ready, 4 * m + 4)
                            if not (isinstance(m, int) and m == 0):
                                eng.wait_ge(state_ready, 2 * m)
                            for t in range(tiles):
                                mm = eng.matmul(state, k_s[:, t, :], v_s[:, t, :], start=(t == 0), stop=(t == tiles - 1))
                            mm.then_inc(state_full, 1)
                        elif what == "mix":
                            half = 2 * n + i
                            eng.wait_ge(state_ready, 2 * n + 2)
                            eng.wait_ge(q_ready, n + 1)
                            if not (isinstance(half, int) and half == 0):
                                eng.wait_ge(divided, half)
                            for t in range(4):
                                at = slice((4 * i + t) * P, (4 * i + t + 1) * P)
                                eng.matmul(den[:, t, :], q_t[:, q, at], sum_blk[:, q, :], start=True, stop=True)
                                mm = eng.matmul(num[:, t, :], q_t[:, q, at], kv_blk[:, q, :], start=True, stop=True)
                            mm.then_inc(mix_full, 1)
                        elif what == "turn":
                            half = 2 * n + i
                            eng.wait_ge(divided, half + 1)
                            if not (isinstance(half, int) and half == 0):
                                eng.wait_ge(mixed_ready, half)
                            for t in range(4):
                                mm = eng.transpose(turned[:, t * P:(t + 1) * P], tokens[:, t, :, :].rearrange("p a b -> p (a b)"), ident[:, :])
                            mm.then_inc(turned_full, 1)
                        elif what == "out":
                            half = 2 * n + i
                            eng.wait_ge(mixed_ready, half + 1)
                            if not (isinstance(half, int) and half == 0):
                                eng.wait_ge(added, half)
                            eng.matmul(out[:, :], wo[:, q, :], mixed[:, i, :], start=True, stop=True).then_inc(out_full, 1)

                run(eng, body)

            @block.scalar
            def _(eng):
                def body(n, q, order):
                    m, r = n + 1, 1 - q
                    for what, i in order:
                        if what == "kv":
                            eng.wait_ge(kv_full, 4 * m + i + 1)
                            if not (isinstance(m, int) and m == 0 and i < 2):
                                eng.wait_ge(k_ready, 4 * m + i - 1)
                            if i == 0 and not (isinstance(m, int) and m == 0):
                                eng.wait_ge(state_full, m)
                            eng.activation(expk[:, i % 2, :, :], kv_ps[:, i % 2, :, 0, :], ACT.Exp)
                            eng.activation(relk[:, i % 2, :, :], kv_ps[:, i % 2, :, 0, :], ACT.Relu)
                            eng.activation(v_s[:, 2 * i:2 * i + 2, 0:P], kv_ps[:, i % 2, :, 1, :], ACT.Copy).then_inc(kv_read, 1)
                        elif what == "q":
                            eng.wait_ge(q_full, m + 1)
                            if not (isinstance(m, int) and m == 0):
                                eng.wait_ge(q_ready, m)
                            eng.activation(expq[:, :], q_ps[:, :], ACT.Exp)
                            eng.activation(relq[:, :], q_ps[:, :], ACT.Relu).then_inc(q_read, 1)
                        elif what == "turn":
                            half = 2 * n + i
                            eng.wait_ge(turned_full, half + 1)
                            if not (isinstance(half, int) and half < 2):
                                eng.wait_ge(out_full, half - 1)
                            eng.activation(mixed[:, i, :], turned[:, :], ACT.Copy).then_inc(mixed_ready, 1)

                run(eng, body)

            @block.vector
            def _(eng):
                eng.memset(v_s[:, :, P:W], 1.0).then_inc(filled, 1)
                eng.wait_ge(const_in, 32)

                def body(n, q, order):
                    m, r = n + 1, 1 - q
                    for what, i in order:
                        if what == "kv":
                            eng.wait_ge(kv_read, 4 * m + i + 1)
                            if i == 0 and not (isinstance(m, int) and m == 0):
                                eng.wait_ge(state_full, m)
                            eng.scalar_tensor_tensor(out=k_s[:, 2 * i:2 * i + 2, :], in0=expk[:, i % 2, :, :], scalar=1.0,
                                                     in1=relk[:, i % 2, :, :], op0=ALU.min, op1=ALU.add).then_inc(k_ready, 1)
                        elif what == "q":
                            eng.wait_ge(q_read, m + 1)
                            if not (isinstance(n, int) and n <= 0):
                                eng.wait_ge(mix_full, 2 * n)
                            eng.scalar_tensor_tensor(out=q_t[:, r, :], in0=expq[:, :], scalar=1.0, in1=relq[:, :],
                                                     op0=ALU.min, op1=ALU.add).then_inc(q_ready, 1)
                        elif what == "state":
                            eng.wait_ge(state_full, m + 1)
                            if not (isinstance(n, int) and n <= 0):
                                eng.wait_ge(mix_full, 2 * n)
                            eng.tensor_tensor(kv_blk[:, r, :], state[:, 0:P], mask[:, :], ALU.mult).then_inc(state_ready, 1)
                            eng.tensor_scalar(sum_blk[:, r, :], mask[:, 0:P:64], state[:, P:P + 1], None, ALU.mult).then_inc(state_ready, 1)
                        elif what == "mix":
                            half = 2 * n + i
                            eng.wait_ge(mix_full, half + 1)
                            if not (isinstance(half, int) and half == 0):
                                eng.wait_ge(divided, half)
                            eng.tensor_scalar(denom[:, :, :], den, eps, None, ALU.add).then_inc(norm, 1)
                            eng.wait_ge(norm, 2 * half + 1)
                            eng.reciprocal(denom[:, :, :], denom[:, :, :]).then_inc(norm, 1)
                            eng.wait_ge(norm, 2 * half + 2)
                            if not (isinstance(half, int) and half == 0):
                                eng.wait_ge(turned_full, half)
                            eng.tensor_tensor(tokens[:, :, :, :], num[:, :, :].rearrange("p a (b c) -> p a b c", b=2),
                                              denom[:, :, :].unsqueeze(3).broadcast_to([P, 4, 2, 64]), ALU.mult).then_inc(divided, 1)
                        elif what == "out":
                            half = 2 * n + i
                            at = bass.ds((n // pairs) * N + i * BANK, BANK)
                            eng.wait_ge(out_full, half + 1)
                            if not (isinstance(half, int) and half == 0):
                                eng.wait_ge(added, half)
                            eng.tensor_tensor(res_t[:, at], res_t[:, at], out[:, :], ALU.add).then_inc(added, 1)

                run(eng, body)

        pl.close()


def recurrent_mixing(nc, stage, res_t, xn_t, d):
    GROUPS = 4
    HV = 8

    with ExitStack() as ctx:
        pl = Place(nc, ctx, stage)
        shape = {"cols": [P, 20], "w_x1": [P, 160], "w_x2": [P, P], "w_x2b": [32, P], "w_w1": [P, 64],
                 "w_w2": [64, GROUPS, P], "w_r": [P, GROUPS, P], "w_k": [P, GROUPS, P], "w_v": [P, GROUPS, P],
                 "w_g": [P, P], "w_o": [P, P], "pick": [P, 32], "blocks": [P, P]}
        c = {n: pl.sb(n, s) for n, s in shape.items()}
        MU, XB, DB, U, GW, GB = 0, 1, 6, 10, 14, 15
        cols = c["cols"]
        xs = pl.sb("xs", [P, N + 1])
        x = xs[:, 1:N + 1]
        delta = pl.sb("delta", [P, N])
        z = pl.sb("z", [P, N])
        low = pl.sb("low", [P, N])
        low5 = pl.sb("low5", [32, N])
        mixed = pl.sb("mixed", [P, 5, N])
        wt = pl.sb("wt", [64, N])
        gs = pl.sb("gs", [P, N])
        vs = pl.sb("vs", [P, 2, N])
        decay = pl.sb("decay", [P, 2, N])
        kv = pl.sb("kv", [P, N])
        st = pl.sb("st", [P, N + 1])
        rs = pl.sb("rs", [P, 2, N])
        cen = pl.sb("cen", [P, N])
        sq = pl.sb("sq", [P, N])
        std = pl.sb("std", [P, N])
        work = [pl.ps(f"work{i}", [P, N]) for i in range(3)]
        o_ps = pl.ps("o_ps", [P, N])

        JOBS = [("low", "act", "low"), ("low5", "act", "low5")] \
            + [(f"mu{i}", "dve", f"mu{i}") for i in range(5)] \
            + [("tanh_w", "act", "wt"), ("g", "act", "gs")]
        for j in range(GROUPS):
            JOBS += [(f"v{j}", "act", f"vs{j}"), (f"w{j}", "act", f"ew{j}"), (f"k{j}", "dve", f"kv{j}"), (f"r{j}", "dve", f"rs{j}")]
        JOBS += [("mean", "dve", "cen"), ("var", "dve", "eps"), ("out", "dve", "res")]
        slot = {name: work[i % 3] for i, (name, _, _) in enumerate(JOBS)}
        PE = [name for name, _, _ in JOBS]
        for j in range(GROUPS):
            PE.insert(PE.index(f"r{j}") + (1 if j == GROUPS - 1 else 3), f"o{j}")
        ACTS = ["low", "low5", "wt", "gs"] + [s + str(j) for j in range(GROUPS) for s in ("vs", "ew", "decay")] + ["o", "sq", "std"]
        DVES = ["delta", "z"] + [f"mu{i}" for i in range(5)] \
            + [s + str(j) for j in range(GROUPS) for s in ("kv", "scan", "u", "rs")] \
            + ["cen", "eps", "rstd", "norm", "affine", "gated", "res"]
        POOLS = [f"x{i}" for i in range(5)]
        const_in = pl.sem("const_in")
        filled = pl.sem("filled")
        x_in = pl.sem("x_in")
        pe = Steps(pl.sem("pe_done"), PE)
        act = Steps(pl.sem("act_done"), ACTS)
        dve = Steps(pl.sem("dve_done"), DVES)
        pool = Steps(pl.sem("pool_done"), POOLS)
        reader = {"act": act, "dve": dve}

        def run(eng, body):
            body(0)
            with eng.Fori(1, B) as b:
                body(b)

        def before(b):
            return -1 if isinstance(b, int) else b - 1

        with nc.Block() as block:
            @block.sync
            def _(eng):
                for n in shape:
                    eng.dma_start(c[n][tuple(slice(None) for _ in shape[n])], d[n]).then_inc(const_in, 16)
                eng.wait_ge(filled, 2)
                eng.dma_start(x, xn_t[:, 0:N]).then_inc(x_in, 16)
                with eng.Fori(1, B) as b:
                    pool.wait(eng, "x4", b - 1)
                    eng.dma_start(x, xn_t[:, bass.ds(b * N, N)]).then_inc(x_in, 16)

            @block.tensor
            def _(eng):
                eng.wait_ge(const_in, 16 * len(shape))

                def product(b, name, lhs, rhs, dst=None, rows=P):
                    if dst is None:
                        i = [n for n, _, _ in JOBS].index(name)
                        same = [k for k in range(len(JOBS)) if k % 3 == i % 3]
                        at = same.index(i)
                        _, who, step = JOBS[same[at - 1]]
                        reader[who].wait(eng, step, b if at else before(b))
                        dst = slot[name]
                    for h in range(2):
                        mm = eng.matmul(dst[0:rows, h * BANK:(h + 1) * BANK], lhs, rhs[:, h * BANK:(h + 1) * BANK],
                                        start=True, stop=True)
                    mm.then_inc(pe.sem, 1)

                def body(b):
                    for name in PE:
                        j = int(name[-1]) if name[-1].isdigit() and name not in ("low5",) else 0
                        if name == "low":
                            dve.wait(eng, "z", b)
                            product(b, name, c["w_x1"][:, 0:P], z)
                        elif name == "low5":
                            product(b, name, c["w_x1"][:, P:160], z, rows=32)
                        elif name.startswith("mu"):
                            act.wait(eng, "low5" if j == 4 else "low", b)
                            if j < 4:
                                product(b, name, c["w_x2"][32 * j:32 * j + 32, :], low[32 * j:32 * j + 32, :])
                            else:
                                product(b, name, c["w_x2b"][:, :], low5)
                        elif name == "tanh_w":
                            pool.wait(eng, "x1", b)
                            product(b, name, c["w_w1"][:, :], mixed[:, 1, :], rows=64)
                        elif name == "g":
                            pool.wait(eng, "x4", b)
                            product(b, name, c["w_g"][:, :], mixed[:, 4, :])
                        elif name[0] == "v" and name != "var":
                            product(b, name, c["w_v"][:, j, :], mixed[:, 3, :])
                        elif name[0] == "w":
                            act.wait(eng, "wt", b)
                            product(b, name, c["w_w2"][:, j, :], wt)
                        elif name[0] == "k":
                            product(b, name, c["w_k"][:, j, :], mixed[:, 2, :])
                        elif name[0] == "r":
                            product(b, name, c["w_r"][:, j, :], mixed[:, 0, :])
                        elif name[0] == "o" and name != "out":
                            dve.wait(eng, f"rs{j}", b)
                            act.wait(eng, "o", before(b))
                            for h in range(2):
                                mm = eng.matmul(o_ps[32 * j:32 * j + 32, h * BANK:(h + 1) * BANK], c["pick"][:, :],
                                                rs[:, j % 2, h * BANK:(h + 1) * BANK], start=True, stop=True)
                            mm.then_inc(pe.sem, 1)
                        elif name == "mean":
                            act.wait(eng, "o", b)
                            product(b, name, c["blocks"][:, :], z)
                        elif name == "var":
                            act.wait(eng, "sq", b)
                            product(b, name, c["blocks"][:, :], sq)
                        elif name == "out":
                            dve.wait(eng, "gated", b)
                            product(b, name, c["w_o"][:, :], cen)

                run(eng, body)

            @block.scalar
            def _(eng):
                eng.wait_ge(const_in, 16 * len(shape))

                def body(b):
                    prev = before(b)
                    pe.wait(eng, "low", b)
                    pe.wait(eng, "mu3", prev)
                    eng.activation(low[:, :], slot["low"][:, :], ACT.Tanh).then_inc(act.sem, 1)
                    pe.wait(eng, "low5", b)
                    eng.activation(low5[:, :], slot["low5"][0:32, :], ACT.Tanh).then_inc(act.sem, 1)
                    pe.wait(eng, "tanh_w", b)
                    pe.wait(eng, f"w{GROUPS - 1}", prev)
                    eng.activation(wt[:, :], slot["tanh_w"][0:64, :], ACT.Tanh).then_inc(act.sem, 1)
                    pe.wait(eng, "g", b)
                    dve.wait(eng, "gated", prev)
                    eng.activation(gs[:, :], slot["g"][:, :], ACT.Silu).then_inc(act.sem, 1)
                    for j in range(GROUPS):
                        pe.wait(eng, f"v{j}", b)
                        if j >= 2:
                            dve.wait(eng, f"scan{j - 2}", b)
                        eng.activation(vs[:, j % 2, :], slot[f"v{j}"][:, :], ACT.Copy).then_inc(act.sem, 1)
                        pe.wait(eng, f"w{j}", b)
                        eng.activation(decay[:, j % 2, :], slot[f"w{j}"][:, :], ACT.Exp,
                                       bias=cols[:, DB + j:DB + j + 1]).then_inc(act.sem, 1)
                        act.wait(eng, f"ew{j}", b)
                        eng.activation(decay[:, j % 2, :], decay[:, j % 2, :], ACT.Exp, scale=-1.0).then_inc(act.sem, 1)
                    pe.wait(eng, f"o{GROUPS - 1}", b)
                    eng.activation(z[:, :], o_ps[:, :], ACT.Copy).then_inc(act.sem, 1)
                    dve.wait(eng, "cen", b)
                    eng.activation(sq[:, :], cen[:, :], ACT.Square).then_inc(act.sem, 1)
                    dve.wait(eng, "eps", b)
                    eng.activation(std[:, :], std[:, :], ACT.Sqrt).then_inc(act.sem, 1)

                run(eng, body)

            @block.gpsimd
            def _(eng):
                def body(b):
                    for i in range(5):
                        dve.wait(eng, f"mu{i}", b)
                        eng.tensor_tensor(mixed[:, i, :], mixed[:, i, :], x, ALU.add).then_inc(pool.sem, 1)

                run(eng, body)

            @block.vector
            def _(eng):
                eng.memset(xs[:, 0:1], 0.0).then_inc(filled, 1)
                eng.memset(st[:, 0:1], 0.0).then_inc(filled, 1)
                eng.wait_ge(filled, 2)
                eng.wait_ge(const_in, 16 * len(shape))

                def body(b):
                    prev = before(b)
                    eng.wait_ge(x_in, 16 * b + 16)
                    dve.wait(eng, "res", prev)
                    eng.tensor_tensor(delta[:, :], xs[:, 0:N], x, ALU.subtract).then_inc(dve.sem, 1)
                    dve.wait(eng, "delta", b)
                    eng.scalar_tensor_tensor(out=z[:, :], in0=delta[:, :], scalar=cols[:, MU:MU + 1], in1=x,
                                             op0=ALU.mult, op1=ALU.add).then_inc(dve.sem, 1)
                    for i in range(5):
                        pe.wait(eng, f"mu{i}", b)
                        if i == 0:
                            pe.wait(eng, f"r{GROUPS - 1}", prev)
                        eng.scalar_tensor_tensor(out=mixed[:, i, :], in0=slot[f"mu{i}"][:, :], scalar=cols[:, XB + i:XB + i + 1],
                                                 in1=delta[:, :], op0=ALU.add, op1=ALU.mult).then_inc(dve.sem, 1)
                    for j in range(GROUPS):
                        act.wait(eng, f"vs{j}", b)
                        pe.wait(eng, f"k{j}", b)
                        if j:
                            dve.wait(eng, f"u{j - 1}", b)
                        eng.tensor_tensor(kv[:, :], slot[f"k{j}"][:, :], vs[:, j % 2, :], ALU.mult).then_inc(dve.sem, 1)
                        act.wait(eng, f"decay{j}", b)
                        dve.wait(eng, f"kv{j}", b)
                        eng.tensor_tensor_scan(st[:, 1:N + 1], decay[:, j % 2, :], kv[:, :], 0.0, ALU.mult, ALU.add).then_inc(dve.sem, 1)
                        dve.wait(eng, f"scan{j}", b)
                        if j >= 2:
                            pe.wait(eng, f"o{j - 2}", b)
                        eng.scalar_tensor_tensor(out=rs[:, j % 2, :], in0=kv[:, :], scalar=cols[:, U + j:U + j + 1],
                                                 in1=st[:, 0:N], op0=ALU.mult, op1=ALU.add).then_inc(dve.sem, 1)
                        dve.wait(eng, f"u{j}", b)
                        pe.wait(eng, f"r{j}", b)
                        eng.tensor_tensor(rs[:, j % 2, :], rs[:, j % 2, :], slot[f"r{j}"][:, :], ALU.mult).then_inc(dve.sem, 1)
                    pe.wait(eng, "mean", b)
                    eng.tensor_tensor(cen[:, :], z[:, :], slot["mean"][:, :], ALU.subtract).then_inc(dve.sem, 1)
                    pe.wait(eng, "var", b)
                    eng.tensor_scalar(std[:, :], slot["var"][:, :], 1e-5, None, ALU.add).then_inc(dve.sem, 1)
                    act.wait(eng, "std", b)
                    eng.reciprocal(std[:, :], std[:, :]).then_inc(dve.sem, 1)
                    dve.wait(eng, "rstd", b)
                    eng.tensor_tensor(cen[:, :], cen[:, :], std[:, :], ALU.mult).then_inc(dve.sem, 1)
                    dve.wait(eng, "norm", b)
                    eng.tensor_scalar(cen[:, :], cen[:, :], cols[:, GW:GW + 1], cols[:, GB:GB + 1], ALU.mult, ALU.add).then_inc(dve.sem, 1)
                    dve.wait(eng, "affine", b)
                    act.wait(eng, "gs", b)
                    eng.tensor_tensor(cen[:, :], cen[:, :], gs[:, :], ALU.mult).then_inc(dve.sem, 1)
                    pe.wait(eng, "out", b)
                    at = bass.ds(b * N, N)
                    eng.tensor_tensor(res_t[:, at], res_t[:, at], slot["out"][:, :], ALU.add).then_inc(dve.sem, 1)

                run(eng, body)

        pl.close()


def route(nc, stage, x_t, w_d, bias_d, tri_d, ident_d, gates_d, E, top, norm_eps, squash, extra, extra_value, capacity):
    EX = E + extra
    GB = BANK // E

    with ExitStack() as ctx:
        pl = Place(nc, ctx, stage)
        w = pl.sb("w", [P, E])
        bias = pl.sb("bias", [P, E])
        ident = pl.sb("ident", [P, P])
        score = pl.sb("score", [P, NT, E])
        gates = pl.sb("gates", [P, NT, EX])
        small = [pl.sb(f"small{i}", [P, NT]) for i in range(2)]
        tmp = [pl.sb(f"tmp{i}", [P, NT, E]) for i in range(3)] if top else None
        keep = pl.sb("keep", [P, NT, E]) if top else None
        best = pl.sb("best", [P, NT, 8]) if top else None
        chosen = [pl.sb(f"chosen{i}", [P, NT, E]) for i in range(2 if capacity else 1)] if top else None
        gates_t = pl.sb("gates_t", [EX, T])
        logit = pl.ps("logit", [P, NT // GB if NT >= GB else 1, BANK])

        def tile_logits(t):
            return logit[:, t // GB, t % GB * E:(t % GB + 1) * E]

        banks = max(1, NT // GB)
        all_logits = logit[:, :, 0:min(BANK, NT * E)].rearrange("p a (b e) -> p (a b) e", e=E)
        turned = pl.ps("turned", [EX, 2, BANK])
        const_in = pl.sem("const_in")
        logits_full = pl.sem("logits_full")
        vec = pl.sem("vec")
        act_done = pl.sem("act_done")
        turned_full = pl.sem("turned_full")
        turned_free = pl.sem("turned_free")
        stored = pl.sem("stored")
        if capacity:
            marks = pl.sb("marks", [P, NT, 2 * E], BF16)
            tri = pl.sb("tri", [P, P])
            tri16 = pl.sb("tri16", [P, P], BF16)
            ones16 = pl.sb("ones16", [P, P], BF16)
            totals = pl.sb("totals", [P, 2 * E, NT])
            before = pl.sb("before", [P, 2 * E, NT])
            keep_e = pl.sb("keep_e", [P, 2 * E, NT])
            rank = pl.ps("rank", [P, NT, 2 * E])
            count = pl.ps("count", [P, NT, 2 * E])
            counted = pl.sem("counted")
            marked = pl.sem("marked")
        CONSTS = 16 * (2 + (bias_d is not None) + bool(capacity))
        exp_in = pl.sem("exp_in")
        gates_ready = pl.sem("gates_ready")

        with nc.Block() as block:
            @block.sync
            def _(eng):
                eng.dma_start(w[:, :], w_d).then_inc(const_in, 16)
                eng.dma_start(ident[:, :], ident_d).then_inc(const_in, 16)
                if bias_d is not None:
                    eng.dma_start(bias[:, :], bias_d.broadcast_to([P, E])).then_inc(const_in, 16)
                if capacity:
                    eng.dma_start(tri[:, :], tri_d).then_inc(const_in, 16)
                eng.wait_ge(turned_free, CH)
                eng.dma_start(gates_d, gates_t[:, :]).then_inc(stored, 16)
                eng.wait_ge(stored, 16)

            @block.tensor
            def _(eng):
                eng.wait_ge(const_in, CONSTS)
                for t in range(NT):
                    mm = eng.matmul(tile_logits(t), x_t[:, t * P:(t + 1) * P], w[:, :], start=True, stop=True)
                mm.then_inc(logits_full, 1)
                if capacity:
                    eng.wait_ge(marked, 1)
                    eng.matmul(rank[:, :, :].rearrange("p a b -> p (a b)"), tri16[:, :], marks[:, :, :].rearrange("p a b -> p (a b)"), start=True, stop=True)
                    eng.matmul(count[:, :, :].rearrange("p a b -> p (a b)"), ones16[:, :], marks[:, :, :].rearrange("p a b -> p (a b)"), start=True, stop=True).then_inc(counted, 1)
                eng.wait_ge(gates_ready, 1)
                for c in range(CH):
                    if c >= 2:
                        eng.wait_ge(turned_free, c - 1)
                    for t in range(4):
                        mm = eng.transpose(turned[:, c % 2, t * P:(t + 1) * P], gates[:, 4 * c + t, :], ident[:, :])
                    mm.then_inc(turned_full, 1)

            @block.scalar
            def _(eng):
                eng.wait_ge(exp_in, 1)
                eng.activation(score[:, :, :], score[:, :, :], ACT.Exp if squash == "softmax" else ACT.Sigmoid).then_inc(act_done, 1)

            @block.vector
            def _(eng):
                count_vec = [0]

                def then(op):
                    count_vec[0] += 1
                    op.then_inc(vec, 1)
                    eng.wait_ge(vec, count_vec[0])

                def wide(a):
                    return a.unsqueeze(2).broadcast_to([P, NT, E])

                def flat(a):
                    return a[:, :, :].rearrange("p a b -> p (a b)")

                if top:
                    then(eng.memset(keep[:, :, :], 1.0))
                    then(eng.memset(keep[:, :, 0:1], 0.0))
                if extra:
                    then(eng.memset(gates[:, :, E:EX], extra_value))
                eng.wait_ge(const_in, CONSTS)
                if capacity:
                    then(eng.memset(keep_e[:, :, :], 1.0))
                    then(eng.memset(keep_e[:, :, 0:1], 0.0))
                    then(eng.memset(ones16[:, :], 1.0))
                    then(eng.tensor_copy(tri16[:, :], tri[:, :]))
                eng.wait_ge(logits_full, 1)
                if bias_d is not None:
                    then(eng.tensor_tensor(score[:, :, :], all_logits, bias[:, :].unsqueeze(1).broadcast_to([P, NT, E]), ALU.add))
                else:
                    then(eng.tensor_copy(score[:, :, :], all_logits))
                if squash == "softmax":
                    then(eng.tensor_reduce(small[0][:, :], score[:, :, :], AX.X, ALU.max))
                    eng.tensor_tensor(score[:, :, :], score[:, :, :], wide(small[0][:, :]), ALU.subtract).then_inc(exp_in, 1)
                    eng.wait_ge(act_done, 1)
                    then(eng.tensor_reduce(small[0][:, :], score[:, :, :], AX.X, ALU.add))
                    then(eng.reciprocal(small[0][:, :], small[0][:, :]))
                    then(eng.tensor_tensor(score[:, :, :], score[:, :, :], wide(small[0][:, :]), ALU.mult))
                else:
                    eng.sem_inc(exp_in, 1)
                    eng.wait_ge(act_done, 1)

                def select(k, dst):
                    for t in range(NT):
                        op = eng.max(best[:, t, :], score[:, t, :])
                    then(op)
                    limit = best[:, :, k - 1:k].broadcast_to([P, NT, E])
                    then(eng.tensor_tensor(tmp[0][:, :, :], score[:, :, :], limit, ALU.is_gt))
                    then(eng.tensor_tensor(tmp[1][:, :, :], score[:, :, :], limit, ALU.is_equal))
                    then(eng.tensor_reduce(small[0][:, :], tmp[0][:, :, :], AX.X, ALU.add))
                    then(eng.tensor_tensor_scan(flat(tmp[2]), flat(keep), flat(tmp[1]), 0.0, ALU.mult, ALU.add))
                    then(eng.tensor_tensor(tmp[2][:, :, :], tmp[2][:, :, :], wide(small[0][:, :]), ALU.add))
                    then(eng.tensor_scalar(tmp[2][:, :, :], tmp[2][:, :, :], float(k), None, ALU.is_le))
                    then(eng.tensor_tensor(tmp[2][:, :, :], tmp[2][:, :, :], tmp[1][:, :, :], ALU.mult))
                    then(eng.tensor_tensor(dst[:, :, :], tmp[2][:, :, :], tmp[0][:, :, :], ALU.add))

                out = gates[:, :, 0:E]
                if not top:
                    then(eng.tensor_copy(out, score[:, :, :]))
                else:
                    select(top, chosen[0])
                    then(eng.tensor_tensor(tmp[0][:, :, :], score[:, :, :], chosen[0][:, :, :], ALU.mult))
                    then(eng.tensor_reduce(small[0][:, :], tmp[0][:, :, :], AX.X, ALU.add))
                    then(eng.tensor_scalar(small[0][:, :], small[0][:, :], norm_eps, None, ALU.add))
                    then(eng.reciprocal(small[1][:, :], small[0][:, :]))
                    if not capacity:
                        then(eng.tensor_tensor(out, tmp[0][:, :, :], wide(small[1][:, :]), ALU.mult))
                    else:
                        select(1, chosen[1])
                        then(eng.tensor_tensor(chosen[0][:, :, :], chosen[0][:, :, :], chosen[1][:, :, :], ALU.subtract))
                        then(eng.tensor_copy(marks[:, :, 0:E], chosen[1][:, :, :]))
                        eng.tensor_copy(marks[:, :, E:2 * E], chosen[0][:, :, :]).then_inc(marked, 1)
                        eng.wait_ge(counted, 1)
                        then(eng.tensor_copy(totals[:, :, :], count[:, :, :].rearrange("p t e -> p e t")))
                        then(eng.tensor_tensor_scan(flat(before), flat(keep_e), flat(totals), 0.0, ALU.mult, ALU.add))
                        then(eng.tensor_copy(small[0][:, 0:E], before[:, 0:E, NT - 1:NT].rearrange("p a b -> p (a b)")))
                        then(eng.tensor_tensor(before[:, :, :], before[:, :, :], totals[:, :, :], ALU.subtract))
                        then(eng.tensor_tensor(before[:, E:2 * E, :], before[:, E:2 * E, :],
                                               small[0][:, 0:E].unsqueeze(2).broadcast_to([P, E, NT]), ALU.add))
                        for j in range(2):
                            dst = tmp[2 - j]
                            then(eng.tensor_tensor(dst[:, :, :], rank[:, :, j * E:(j + 1) * E],
                                                   before[:, j * E:(j + 1) * E, :].rearrange("p e t -> p t e"), ALU.add))
                            then(eng.tensor_scalar(dst[:, :, :], dst[:, :, :], float(capacity), None, ALU.is_le))
                            then(eng.tensor_tensor(dst[:, :, :], dst[:, :, :], chosen[1 - j][:, :, :], ALU.mult))
                        then(eng.tensor_tensor(tmp[2][:, :, :], tmp[2][:, :, :], tmp[1][:, :, :], ALU.add))
                        then(eng.tensor_tensor(tmp[2][:, :, :], tmp[2][:, :, :], score[:, :, :], ALU.mult))
                        then(eng.tensor_tensor(out, tmp[2][:, :, :], wide(small[1][:, :]), ALU.mult))
                eng.sem_inc(gates_ready, 1)
                for c in range(CH):
                    eng.wait_ge(turned_full, c + 1)
                    eng.tensor_copy(gates_t[:, c * BANK:(c + 1) * BANK], turned[:, c % 2, :]).then_inc(turned_free, 1)

        pl.close()


def gated_experts(nc, stage, res_t, x_t, w_d, gates_d, units, J, act):
    steps = CH * J
    PART_LAG = 1
    LAG = 3
    HB = 3
    HR = 4
    SPLIT_AT = 8
    HALF = T // 2

    def run(eng, body):
        body(0, 0, True, units == 1)
        loops = (units - 2) // 2
        with eng.Fori(0, loops) as i:
            body(2 * i + 1, 1, False, False)
            body(2 * i + 2, 0, False, False)
        for n in range(2 * loops + 1, units):
            body(n, n % 2, False, n == units - 1)

    def schedule(first, last):
        order = []
        for s in range(steps + (LAG if last else 0)):
            if s == SPLIT_AT and not last:
                order.append(("split", 0, 0))
            if s < steps:
                order.append(("hidden", s, 0))
            for what, lag in (("part", PART_LAG), ("out", LAG)):
                if lag <= s < steps + lag:
                    order.append((what, s - lag, 0))
                elif s < lag and not first:
                    order.append((what, steps + s - lag, 1))
        return order

    with ExitStack() as ctx:
        pl = Place(nc, ctx, stage)
        x_high = pl.sb("x_high", [P, T], F16)
        x_low = pl.sb("x_low", [P, T], F16)
        w = pl.sb("w", [P, 3 * J, P])
        w_high = pl.sb("w_high", [P, 2, 3 * J, P], F16)
        w_low = pl.sb("w_low", [P, 2, 3 * J, P], F16)
        gate = pl.sb("gate", [P, 2, J, HALF])
        acted = pl.sb("acted", [P, HR, BANK])
        scaled = pl.sb("scaled", [P, HR, BANK])
        high = pl.sb("high", [P, HR, BANK], F16)
        low = pl.sb("low", [P, HR, BANK], F16)
        hidden = pl.ps("hidden", [P, HB, BANK])
        upper = pl.ps("upper", [P, HB, BANK])
        out = pl.ps("out", [P, 2, BANK])

        w_in = pl.sem("w_in")
        gate_in = [pl.sem(f"gate_in{h}") for h in range(2)]
        x_high_done = pl.sem("x_high_done")
        x_split = pl.sem("x_split")
        w_high_done = pl.sem("w_high_done")
        w_split = pl.sem("w_split")
        hidden_full = pl.sem("hidden_full")
        act_done = pl.sem("act_done")
        upped = pl.sem("upped")
        scaled_done = pl.sem("scaled_done")
        high_done = pl.sem("high_done")
        low_done = pl.sem("low_done")
        out_used = pl.sem("out_used")
        summed = pl.sem("summed")

        with nc.Block() as block:
            @block.sync
            def _(eng):
                def load_w(n):
                    eng.dma_start(w[:, :, :], w_d[n, :, :, :]).then_inc(w_in, 16)

                def load_gates(n, half):
                    for j in range(J):
                        for e in range(2):
                            row = gates_d[bass.ds(2 * J * n + 2 * j + e, 1), half * HALF:(half + 1) * HALF]
                            eng.dma_start(gate[e * 64:e * 64 + 64, half, j, :], row.broadcast_to([64, HALF])).then_inc(gate_in[half], 16)

                def reload(n):
                    eng.wait_ge(w_split, n)
                    load_w(n)
                    for half in range(2):
                        eng.wait_ge(scaled_done, steps * (n - 1) + (half + 1) * steps // 2)
                        load_gates(n, half)

                load_w(0)
                load_gates(0, 0)
                load_gates(0, 1)
                with eng.Fori(1, units) as n:
                    reload(n)

            @block.tensor
            def _(eng):
                def product(dst, block, q, parts, first, last):
                    eng.matmul(dst, w_high[:, q, block, :], parts[0], start=first, stop=False)
                    eng.matmul(dst, w_high[:, q, block, :], parts[1], start=False, stop=False)
                    return eng.matmul(dst, w_low[:, q, block, :], parts[0], start=False, stop=last)

                def body(n, q, first, last):
                    for what, s, back in schedule(first, last):
                        u, uq = (n - 1, 1 - q) if back else (n, q)
                        c, j, step = s // J, s % J, u * steps + s
                        if what == "hidden":
                            if s == 0:
                                eng.wait_ge(w_split, n + 1)
                            if first and j == 0:
                                eng.wait_ge(x_split, c // 2 + 1)
                            if not (first and s < HB):
                                eng.wait_ge(upped, step - HB + 1)
                            x = [part[:, c * BANK:(c + 1) * BANK] for part in (x_high, x_low)]
                            product(hidden[:, s % HB, :], 3 * j, q, x, True, True)
                            product(upper[:, s % HB, :], 3 * j + 1, q, x, True, True).then_inc(hidden_full, 1)
                        elif what == "out":
                            if j == 0 and not (first and c < 2):
                                eng.wait_ge(summed, u * CH + c - 1)
                            eng.wait_ge(low_done, step + 1)
                            product(out[:, c % 2, :], 3 * j + 2, uq, (high[:, s % HR, :], low[:, s % HR, :]),
                                    j == 0, j == J - 1).then_inc(out_used, 1)

                run(eng, body)

            @block.scalar
            def _(eng):
                def split(n, q):
                    eng.wait_ge(w_in, 16 * (n + 1))
                    eng.activation(w_high[:, q, :, :], w[:, :, :], ACT.Copy).then_inc(w_high_done, 1)

                for span in range(CH // 2):
                    at = slice(span * 2 * BANK, (span + 1) * 2 * BANK)
                    eng.activation(x_high[:, at], x_t[:, at], ACT.Copy).then_inc(x_high_done, 1)
                    if span == 0:
                        split(0, 0)

                def body(n, q, first, last):
                    for what, s, back in schedule(first, last):
                        step = (n - 1 if back else n) * steps + s
                        if what == "split":
                            if not first:
                                eng.wait_ge(out_used, steps * n)
                            split(n + 1, 1 - q)
                        elif what == "hidden":
                            eng.wait_ge(hidden_full, step + 1)
                            if not (first and s < HR):
                                eng.wait_ge(scaled_done, step - HR + 1)
                            eng.activation(acted[:, s % HR, :], hidden[:, s % HB, :], act).then_inc(act_done, 1)
                        elif what == "part":
                            eng.wait_ge(scaled_done, step + 1)
                            if not (first and s < HR):
                                eng.wait_ge(out_used, step - HR + 1)
                            eng.activation(high[:, s % HR, :], scaled[:, s % HR, :], ACT.Copy).then_inc(high_done, 1)

                run(eng, body)

            @block.gpsimd
            def _(eng):
                def split(n, q):
                    eng.wait_ge(w_high_done, n + 1)
                    eng.tensor_tensor(w_low[:, q, :, :], w[:, :, :], w_high[:, q, :, :], ALU.subtract).then_inc(w_split, 1)

                split(0, 0)

                def body(n, q, first, last):
                    for what, s, back in schedule(first, last):
                        c, j, step = s // J, s % J, n * steps + s
                        if what == "split":
                            split(n + 1, 1 - q)
                        elif what == "hidden":
                            half, at = c // (CH // 2), slice(c % (CH // 2) * BANK, (c % (CH // 2) + 1) * BANK)
                            if s % (steps // 2) == 0:
                                eng.wait_ge(gate_in[half], 32 * J * (n + 1))
                            eng.wait_ge(upped, step + 1)
                            if not (first and s < HR):
                                eng.wait_ge(low_done, step - HR + 1)
                            eng.tensor_tensor(scaled[:, s % HR, :], acted[:, s % HR, :], gate[:, half, j, at],
                                              ALU.mult).then_inc(scaled_done, 1)

                run(eng, body)

            @block.vector
            def _(eng):
                for span in range(CH // 2):
                    at = slice(span * 2 * BANK, (span + 1) * 2 * BANK)
                    eng.wait_ge(x_high_done, span + 1)
                    eng.tensor_tensor(x_low[:, at], x_t[:, at], x_high[:, at], ALU.subtract).then_inc(x_split, 1)

                def body(n, q, first, last):
                    for what, s, back in schedule(first, last):
                        u = n - 1 if back else n
                        c, j, step = s // J, s % J, u * steps + s
                        if what == "hidden":
                            eng.wait_ge(act_done, step + 1)
                            eng.tensor_tensor(acted[:, s % HR, :], acted[:, s % HR, :], upper[:, s % HB, :],
                                              ALU.mult).then_inc(upped, 1)
                        elif what == "part":
                            eng.wait_ge(high_done, step + 1)
                            eng.tensor_tensor(low[:, s % HR, :], scaled[:, s % HR, :], high[:, s % HR, :],
                                              ALU.subtract).then_inc(low_done, 1)
                        elif what == "out" and j == J - 1:
                            eng.wait_ge(out_used, step + 1)
                            at = slice(c * BANK, (c + 1) * BANK)
                            if not first:
                                eng.wait_ge(summed, u * CH + c)
                            eng.tensor_tensor(res_t[:, at], res_t[:, at], out[:, c % 2, :], ALU.add).then_inc(summed, 1)

                run(eng, body)

        pl.close()


def experts(nc, stage, res_t, x_t, w_d, bias_d, gates_d, units, act):
    J = 4
    W = 2 * BANK
    SPANS = T // W
    steps = SPANS * J
    LAG = 2
    HR = 4
    SPLIT_AT = 6

    def run(eng, body):
        body(0, 0, True, units == 1)
        loops = (units - 2) // 2
        with eng.Fori(0, loops) as i:
            body(2 * i + 1, 1, False, False)
            body(2 * i + 2, 0, False, False)
        for n in range(2 * loops + 1, units):
            body(n, n % 2, False, n == units - 1)

    def schedule(first, last):
        order = []
        for s in range(steps + (LAG if last else 0)):
            if s == SPLIT_AT and not last:
                order.append(("split", 0, 0))
            if s < steps:
                order.append(("hidden", s, 0))
            if s >= LAG:
                order.append(("out", s - LAG, 0))
            elif not first:
                order.append(("out", steps + s - LAG, 1))
        return order

    with ExitStack() as ctx:
        pl = Place(nc, ctx, stage)
        x_high = pl.sb("x_high", [P, T], F16)
        x_low = pl.sb("x_low", [P, T], F16)
        w = pl.sb("w", [P, 2 * J, P])
        w_high = pl.sb("w_high", [P, 2, 2 * J, P], F16)
        w_low = pl.sb("w_low", [P, 2, 2 * J, P], F16)
        bias = pl.sb("bias", [P, 2, J + 1])
        gate = pl.sb("gate", [P, 2, T])
        whole = pl.sb("whole", [P, 2, W])
        high = pl.sb("high", [P, HR, W], F16)
        low = pl.sb("low", [P, HR, W], F16)
        gated = pl.sb("gated", [P, 2, W])
        hidden = pl.ps("hidden", [P, 2, W])
        out = pl.ps("out", [P, 2, W])

        w_in = pl.sem("w_in")
        side_in = [pl.sem(f"side_in{q}") for q in range(2)]
        x_high_done = pl.sem("x_high_done")
        x_split = pl.sem("x_split")
        w_high_done = pl.sem("w_high_done")
        w_split = pl.sem("w_split")
        hidden_full = pl.sem("hidden_full")
        high_done = pl.sem("high_done")
        low_done = pl.sem("low_done")
        out_used = pl.sem("out_used")
        combined = pl.sem("combined")
        added = pl.sem("added")

        with nc.Block() as block:
            @block.sync
            def _(eng):
                def load_w(n):
                    eng.dma_start(w[:, :, :], w_d[n, :, :, :]).then_inc(w_in, 16)

                def load_side(n, q):
                    eng.dma_start(bias[:, q, :], bias_d[n, :, :]).then_inc(side_in[q], 16)
                    eng.dma_start(gate[:, q, :], gates_d[bass.ds(n, 1), :].broadcast_to([P, T])).then_inc(side_in[q], 16)

                load_w(0)
                load_side(0, 0)
                load_side(1, 1)

                def reload(n, q):
                    eng.wait_ge(w_split, n)
                    load_w(n)
                    eng.wait_ge(combined, SPANS * n)
                    load_side(n + 1, 1 - q)

                with eng.Fori(0, (units - 2) // 2) as i:
                    reload(2 * i + 1, 1)
                    reload(2 * i + 2, 0)
                for n in range(2 * ((units - 2) // 2) + 1, units - 1):
                    reload(n, n % 2)
                eng.wait_ge(w_split, units - 1)
                load_w(units - 1)

            @block.tensor
            def _(eng):
                def product(dst, block, q, parts, at, first, last):
                    for c in range(2):
                        cols = slice(at + c * BANK, at + (c + 1) * BANK)
                        to = dst[:, c * BANK:(c + 1) * BANK]
                        eng.matmul(to, w_high[:, q, block, :], parts[0][:, cols], start=first, stop=False)
                        eng.matmul(to, w_high[:, q, block, :], parts[1][:, cols], start=False, stop=False)
                        mm = eng.matmul(to, w_low[:, q, block, :], parts[0][:, cols], start=False, stop=last)
                    return mm

                def body(n, q, first, last):
                    for what, s, back in schedule(first, last):
                        u, uq = (n - 1, 1 - q) if back else (n, q)
                        span, j, step = s // J, s % J, u * steps + s
                        if what == "hidden":
                            if s == 0:
                                eng.wait_ge(w_split, n + 1)
                            if first and j == 0:
                                eng.wait_ge(x_split, span + 1)
                            if not (first and s < 2):
                                eng.wait_ge(high_done, step - 1)
                            product(hidden[:, s % 2, :], j, q, (x_high, x_low), span * W, True, True).then_inc(hidden_full, 1)
                        elif what == "out":
                            if j == 0 and not (first and span < 2):
                                eng.wait_ge(combined, u * SPANS + span - 1)
                            eng.wait_ge(low_done, step + 1)
                            product(out[:, span % 2, :], J + j, uq, (high[:, s % HR, :], low[:, s % HR, :]), 0,
                                    j == 0, j == J - 1).then_inc(out_used, 1)

                run(eng, body)

            @block.scalar
            def _(eng):
                def split(n, q):
                    eng.wait_ge(w_in, 16 * (n + 1))
                    eng.activation(w_high[:, q, :, :], w[:, :, :], ACT.Copy).then_inc(w_high_done, 1)

                for span in range(SPANS):
                    at = slice(span * W, (span + 1) * W)
                    eng.activation(x_high[:, at], x_t[:, at], ACT.Copy).then_inc(x_high_done, 1)
                    if span == 0:
                        split(0, 0)

                def body(n, q, first, last):
                    for what, s, back in schedule(first, last):
                        j, step = s % J, n * steps + s
                        if what == "split":
                            if not first:
                                eng.wait_ge(out_used, steps * n)
                            split(n + 1, 1 - q)
                        elif what == "hidden":
                            if s == 0:
                                eng.wait_ge(side_in[q], (n + 2 - q) * 16)
                            eng.wait_ge(hidden_full, step + 1)
                            if not (first and s < 2):
                                eng.wait_ge(low_done, step - 1)
                            eng.activation(whole[:, s % 2, :], hidden[:, s % 2, :], act, bias=bias[:, q, j:j + 1])
                            if not (first and s < HR):
                                eng.wait_ge(out_used, step - HR + 1)
                            eng.activation(high[:, s % HR, :], hidden[:, s % 2, :], act,
                                           bias=bias[:, q, j:j + 1]).then_inc(high_done, 1)

                run(eng, body)

            @block.gpsimd
            def _(eng):
                def split(n, q):
                    eng.wait_ge(w_high_done, n + 1)
                    eng.tensor_tensor(w_low[:, q, :, :], w[:, :, :], w_high[:, q, :, :], ALU.subtract).then_inc(w_split, 1)

                split(0, 0)

                def body(n, q, first, last):
                    for what, s, back in schedule(first, last):
                        u = n - 1 if back else n
                        if what == "split":
                            split(n + 1, 1 - q)
                        elif what == "out" and s % J == J - 1:
                            span = s // J
                            at = slice(span * W, (span + 1) * W)
                            eng.wait_ge(combined, u * SPANS + span + 1)
                            if not (first and span == 0):
                                eng.wait_ge(added, u * SPANS + span)
                            eng.tensor_tensor(res_t[:, at], res_t[:, at], gated[:, span % 2, :], ALU.add).then_inc(added, 1)

                run(eng, body)

            @block.vector
            def _(eng):
                for span in range(SPANS):
                    at = slice(span * W, (span + 1) * W)
                    eng.wait_ge(x_high_done, span + 1)
                    eng.tensor_tensor(x_low[:, at], x_t[:, at], x_high[:, at], ALU.subtract).then_inc(x_split, 1)

                def body(n, q, first, last):
                    for what, s, back in schedule(first, last):
                        u, uq = (n - 1, 1 - q) if back else (n, q)
                        step = u * steps + s
                        if what == "hidden":
                            eng.wait_ge(high_done, step + 1)
                            eng.tensor_tensor(low[:, s % HR, :], whole[:, s % 2, :], high[:, s % HR, :], ALU.subtract).then_inc(low_done, 1)
                        elif what == "out" and s % J == J - 1:
                            span = s // J
                            at = slice(span * W, (span + 1) * W)
                            eng.wait_ge(out_used, step + 1)
                            if span == 0:
                                eng.wait_ge(side_in[uq], (u + 2 - uq) * 16)
                            if not (first and span < 2):
                                eng.wait_ge(added, u * SPANS + span - 1)
                            eng.scalar_tensor_tensor(out=gated[:, span % 2, :], in0=out[:, span % 2, :], scalar=bias[:, uq, J:J + 1],
                                                     in1=gate[:, uq, at], op0=ALU.add, op1=ALU.mult).then_inc(combined, 1)

                run(eng, body)

        pl.close()


EXPERTS = 8
SMALL_EXPERTS = 64
SMALL = 64
CAPACITY = 2 * T // EXPERTS


def program(nc, d, out):
    gates = nc.dram_tensor("gates", (SMALL_EXPERTS + 2, T), F32, kind="Internal").ap()
    with ExitStack() as ctx:
        pl = Place(nc, ctx, "all")
        res_t = pl.sb("res_t", [P, T])
        xn_t = pl.sb("xn_t", [P, T])
        x_in = pl.sem("x_in")
        stored = pl.sem("stored")

        with nc.Block() as block:
            @block.sync
            def _(eng):
                eng.dma_start(res_t[:, :], d["x"]).then_inc(x_in, 16)
                eng.wait_ge(x_in, 16)

        layer_norm(nc, "n0", res_t, xn_t, d["avg"], d["ident"], d["bias0"])
        head_attention(nc, "a0", res_t, xn_t, d["w_qk0"], d["w_v0"], d["w_o0"], d["ident"], d["consts0"], None, None,
                       groups=8, heads=2, scale=64 ** -0.5, eps=1e-10)
        with nc.sbuf_tensor("xp_t", [P, T], F32) as xp_t:
            whole_attention(nc, "b0", res_t, xn_t, xp_t, d["w_b0"], d["bias_b0"], d["ident"])
            route(nc, "r0", xp_t, d["w_g0"], d["b_g0"], None, d["ident"], gates[0:EXPERTS, :], EXPERTS,
                  top=0, norm_eps=0.0, squash="softmax", extra=0, extra_value=0.0, capacity=0)
            experts(nc, "e0", res_t, xp_t, d["w_moe0"], d["b_moe0"], gates[0:EXPERTS, :],
                    units=EXPERTS, act=ACT.Relu)

        layer_norm(nc, "n1", res_t, xn_t, d["avg"], d["ident"], None)
        head_attention(nc, "a1", res_t, xn_t, d["w_qk1"], d["w_v1"], d["w_o1"], d["ident"], d["consts1"], d["rope"], d["pick1"],
                       groups=4, heads=4, scale=1.0, eps=0.0)
        route(nc, "r1", xn_t, d["w_g1"], None, None, d["ident"], gates[0:EXPERTS + 1, :], EXPERTS,
              top=2, norm_eps=1e-9, squash="softmax", extra=1, extra_value=0.1, capacity=0)
        experts(nc, "e1", res_t, xn_t, d["w_moe1"], d["b_moe1"], gates[0:EXPERTS + 1, :],
                units=EXPERTS + 1, act=ACT.Silu)

        layer_norm(nc, "n2", res_t, xn_t, d["avg"], d["ident"], d["bias2"])
        linear_attention(nc, "a2", res_t, xn_t, d["w_qkv2"], d["w_o2"], d["mask2"], d["ident"], eps=1e-6)
        route(nc, "r2", xn_t, d["w_g2"], None, d["tri"], d["ident"], gates[0:EXPERTS, :], EXPERTS,
              top=2, norm_eps=0.0, squash="softmax", extra=0, extra_value=0.0, capacity=CAPACITY)
        experts(nc, "e2", res_t, xn_t, d["w_moe2"], d["b_moe2"], gates[0:EXPERTS, :],
                units=EXPERTS, act=ACT.Relu)

        layer_norm(nc, "n3", res_t, xn_t, d["avg"], d["ident"], None)
        recurrent_mixing(nc, "a3", res_t, xn_t, {n[:-1]: a for n, a in d.items() if n.endswith("3") and n != "bias3"})
        route(nc, "r3", xn_t, d["w_route"], None, None, d["ident"], gates, SMALL_EXPERTS,
              top=8, norm_eps=1e-9, squash="sigmoid", extra=2, extra_value=1.0, capacity=0)
        gated_experts(nc, "e3", res_t, xn_t, d["w_small"], gates,
                      units=(SMALL_EXPERTS // 2 + 1) // 3, J=3, act=ACT.Silu)

        with nc.Block() as block:
            @block.sync
            def _(eng):
                eng.dma_start(out, res_t[:, :]).then_inc(stored, 16)
                eng.wait_ge(stored, 16)


def lay_out(a):
    def mixture(w1, b1, w2, b2, tag):
        e = w1.shape[0]
        return {f"w_moe{tag}": np.concatenate([w1.reshape(e, P, 4, P), w2.reshape(e, 4, P, P).transpose(0, 2, 1, 3)], 2),
                f"b_moe{tag}": np.concatenate([b1.reshape(e, 4, P).transpose(0, 2, 1), b2.reshape(e, P, 1)], 2)}

    def with_shared(w, shared):
        return np.concatenate([w, shared[None]])

    p, j = np.arange(P)[:, None], np.arange(P)[None]

    w_qk0 = np.stack([a[f"L0_attn_W{n}"].reshape(8, 2, 64, P).transpose(0, 3, 1, 2) for n in "qk"], 3)
    w_qk0 = np.broadcast_to(w_qk0[:, :, :, :, None], (8, P, 2, 2, 2, 64)).reshape(8, P, 4, P)
    consts0 = np.zeros((P, 16), np.float32)
    consts0[:, 0:8] = p - 64 == j[:, 0:8]

    def lead(w):
        out = np.zeros((4, P, 4, 4, 8), w.dtype)
        out[:, :, :, 0:3] = w.reshape(4, 4, 8, P).transpose(0, 3, 1, 2)[:, :, :, None]
        return out.reshape(4, P, P)

    def even(w):
        return w.reshape(16, 8, P)[:, np.arange(8) // 2 * 2]
    w_qk1 = np.stack([lead(even(a["L1_attn_Wq"])), lead(even(a["L1_attn_Wk"]))], 2)
    w_o1 = np.zeros((4, 4, 32, P), np.float32)
    w_o1[:, :, 0:8] = a["L1_attn_Wo"].T.reshape(4, 4, 8, P)
    freqs = np.exp(np.arange(0, 8, 2, dtype=np.float32) * np.float32(-np.log(10000.0) / 8))
    angles = np.arange(N, dtype=np.float32)[None] * freqs[:, None]
    table = np.zeros((8, N), np.float32)
    table[0::2], table[1::2] = np.cos(angles), -np.sin(angles)
    rope = np.zeros((4, 4, 8, 2, N), np.float32)
    rope[:, 0:3, :, 0], rope[:, 0:3, :, 1] = table / np.float32(np.sqrt(8.0)), table
    part = p[:, 0] % 32 // 8
    consts1 = np.zeros((P, 16), np.float32)
    consts1[:, 0:8] = p % 32 - 24 == j[:, 0:8]
    consts1[:, 8], consts1[:, 9] = (part % 2 == 0) * 1.0 - (part == 1), part == 1
    consts1[:, 11], consts1[:, 12], consts1[:, 13] = (part <= 1) * 1.0 - (part == 2), part == 2, part == 3

    entry = np.arange(4 * P).reshape(4, P)
    key_of, value_of = entry // 8, entry // 32 * 8 + entry % 8
    cols3 = np.zeros((P, 20), np.float32)
    cols3[:, 0], cols3[:, 1:6] = a["L3_attn_mu_x"], a["L3_attn_x_bias"].T
    cols3[:, 6:10], cols3[:, 10:14] = a["L3_attn_b_w2"][key_of].T, a["L3_attn_u"].reshape(64)[key_of].T
    cols3[:, 14], cols3[:, 15] = a["L3_attn_gn_w"], a["L3_attn_gn_b"]
    x2 = a["L3_attn_W_x2"].transpose(1, 2, 0)

    def side_by_side(w, shared):
        w = np.concatenate([w, shared[None], np.zeros_like(shared)[None]])
        return w.reshape(33, 2, P, SMALL).transpose(0, 2, 1, 3).reshape(33, P, P)
    down = a["L3_ffn_shared_down_w"]
    down = np.concatenate([a["L3_ffn_expert_down_k"], down[None], np.zeros_like(down)[None]]).reshape(33, P, P)
    w_small = np.stack([side_by_side(a["L3_ffn_expert_gate_k"], a["L3_ffn_shared_gate_w"]),
                        side_by_side(a["L3_ffn_expert_up_k"], a["L3_ffn_shared_up_w"]), down], 2)

    return {
        "x": a["L0_attn_x"].reshape(T, P).T, "avg": np.full((P, P), 1.0 / P, np.float32),
        "ident": np.eye(P, dtype=np.float32), "tri": (p <= j).astype(np.float32),
        "consts0": consts0, "consts1": consts1, "pick1": (p == j // 32 * 32 + 8).astype(np.float32),
        "bias0": a["L0_attn_bo"].reshape(P, 1), "w_qk0": w_qk0,
        "w_v0": a["L0_attn_Wv"].reshape(8, P, P).transpose(0, 2, 1), "w_o0": a["L0_attn_Wo"].T.reshape(8, P, P),
        "w_b0": np.stack([a[f"L0_ffn_W{n}"] for n in "qkvo"], 1), "bias_b0": np.stack([a[f"L0_ffn_b{n}"] for n in "qkvo"], 1),
        "w_g0": a["L0_ffn_Wg"], "b_g0": a["L0_ffn_bg"].reshape(1, EXPERTS),
        **mixture(a["L0_ffn_W1"], a["L0_ffn_b1"], a["L0_ffn_W2"], a["L0_ffn_b2"], "0"),
        "w_qk1": w_qk1, "w_v1": a["L1_attn_Wv"].reshape(4, 32, P).transpose(0, 2, 1), "w_o1": w_o1.reshape(4, P, P), "rope": rope.reshape(P, 2, N), "w_g1": a["L1_ffn_Wg"],
        **mixture(with_shared(a["L1_ffn_W1"], a["L1_ffn_Ws1"]), with_shared(a["L1_ffn_b1"], a["L1_ffn_bs1"]),
                  with_shared(a["L1_ffn_W2"], a["L1_ffn_Ws2"]), with_shared(a["L1_ffn_b2"], a["L1_ffn_bs2"]), "1"),
        "bias2": a["L2_attn_bout"].reshape(P, 1),
        "w_qkv2": a["L2_attn_Wqkv"].reshape(P, 3, 8, P).transpose(2, 0, 1, 3).reshape(8, P, 3 * P),
        "w_o2": a["L2_attn_Wout"].reshape(8, P, P), "mask2": (p // 64 == j // 64).astype(np.float32),
        "w_g2": a["L2_ffn_gate_w"].T,
        **mixture(a["L2_ffn_fc1_w"].transpose(0, 2, 1), a["L2_ffn_fc1_b"], a["L2_ffn_fc2_w"], a["L2_ffn_fc2_b"], "2"),
        "cols3": cols3, "w_x13": a["L3_attn_W_x1"], "w_x23": x2[:4].reshape(P, P), "w_x2b3": x2[4],
        "w_w13": a["L3_attn_W_w1"], "w_w23": a["L3_attn_W_w2"][:, key_of], "w_r3": a["L3_attn_W_r"][:, key_of],
        "w_k3": a["L3_attn_W_k"][:, key_of], "w_v3": a["L3_attn_W_v"][:, value_of], "w_g3": a["L3_attn_W_g"],
        "w_o3": a["L3_attn_W_o"], "pick3": (p // 32 * 8 + p % 8 == j[:, :32]).astype(np.float32),
        "blocks3": (p // 8 == j // 8).astype(np.float32) / 8,
        "w_route": a["L3_ffn_router_w"],
        "w_small": w_small.reshape(11, 3, P, 3, P).transpose(0, 2, 1, 3, 4).reshape(11, P, 9, P),
    }


def kernel(**inputs):
    import concourse.bacc as bacc
    from concourse.bass_utils import run_bass_kernel_spmd

    laid = lay_out({n: np.asarray(v) for n, v in inputs.items()})
    arrays = {f"in_{n}": np.ascontiguousarray(v) for n, v in laid.items()}
    nc = bacc.Bacc("TRN2", target_bir_lowering=False, num_devices=1)
    operands = {n: nc.dram_tensor(f"in_{n}", arrays[f"in_{n}"].shape, mybir.dt.from_np(arrays[f"in_{n}"].dtype), kind="ExternalInput").ap()
                for n in laid}
    out = nc.dram_tensor("out_t", (P, T), F32, kind="ExternalOutput").ap()
    program(nc, operands, out)
    result = run_bass_kernel_spmd(nc, [arrays], core_ids=[0]).results[0]["out_t"]
    return np.ascontiguousarray(result.T).reshape(B, N, P)
```
